# Optimizing a Trainium2 kernel written in Bass

```python
import numpy as np
import jax
import jax.numpy as jnp

def _softmax(x, axis=-1):
    return jax.nn.softmax(x, axis=axis)

def _gelu(x):
    return jax.nn.gelu(x, approximate=True)

def _silu(x):
    return jax.nn.silu(x)

def _sigmoid(x):
    return jax.nn.sigmoid(x)

def _layernorm(x, axis=-1, eps=1e-05):
    m = jnp.mean(x, axis=axis, keepdims=True)
    v = jnp.var(x, axis=axis, keepdims=True)
    return (x - m) / jnp.sqrt(v + eps)

def _scatter_add(tgt, idx, src, axis=0):
    return tgt.at[idx].add(src)

def _segment_sum(src, seg, n):
    return jax.ops.segment_sum(src, seg, n)
kernel_name = 'mk_flamingo_gated_d4_seqx_r8_c7192e'

def setup_inputs(seed: int=0):
    np.random.seed(seed)
    _w = jnp.asarray

    def _rec_inputs():
        import jax
        import jax.numpy as jnp
        _rk = jax.random.key(seed)
        x = -0.000125 + 0.9999 * jax.random.normal(jax.random.fold_in(_rk, 1), (2, 256, 512), jnp.float32)
        _lenS = 256 - jax.random.randint(jax.random.fold_in(_rk, 7), (2,), 0, max(1, 256 // 4) + 1, jnp.int32)
        _lenS2 = 512 - jax.random.randint(jax.random.fold_in(_rk, 8), (2,), 0, max(1, 512 // 4) + 1, jnp.int32)
        _ctx_4096P = jax.random.normal(jax.random.fold_in(_rk, 11), (2, 16, 512), jnp.float32)
        _ctx_4096c = jax.random.dirichlet(jax.random.fold_in(_rk, 511), 0.3 * jnp.ones((16,), jnp.float32), (2, 512))
        _ctx_4096t = jnp.einsum('bsk,bkd->bsd', _ctx_4096c, _ctx_4096P)
        _ctx_4096t = _ctx_4096t * jax.lax.rsqrt(jnp.mean(jnp.square(_ctx_4096t)) + 1e-12) * 0.953939
        ctx_4096 = -5.72187e-05 + 0.999849 * (_ctx_4096t + 0.3 * jax.random.normal(jax.random.fold_in(_rk, 611), (2, 512, 512), jnp.float32))
        _validS = jnp.arange(256)[None, :] < _lenS[:, None]
        _validS2 = jnp.arange(512)[None, :] < _lenS2[:, None]
        _causal = jnp.tril(jnp.ones((256, 256), dtype=bool))
        mask_BxSxS2_ff0 = jnp.where(jnp.ones((2, 256, 512), dtype=bool), 0.0, -1000000000.0).astype(jnp.float32)
        _g = jax.random.normal(jax.random.fold_in(_rk, 9001), (2, 4), jnp.float32)
        _g = jnp.sign(_g) * jnp.maximum(jnp.abs(_g), 1.0) + (_g == 0) * 1.0
        g_xattn = _g[0]
        g_ffn = _g[1]
        return (x, ctx_4096, mask_BxSxS2_ff0, g_xattn, g_ffn)
    x, ctx_4096, mask_BxSxS2_ff0, g_xattn, g_ffn = _rec_inputs()

    def _L0_xattn_setup():
        import jax, jax.numpy as jnp
        import numpy as np
        QMIN = 0.0
        QMAX = 255.0

        def fake_quant(x, scale, zp):
            s = scale.reshape(())
            z = zp.reshape(())
            q = jnp.clip(jnp.round(x / s + z), QMIN, QMAX)
            return (q - z) * s
        key = jax.random.key(seed)
        k1, k2 = jax.random.split(key)
        B, M, K, N = (4, 256, 512, 512)
        x1 = jax.random.normal(k1, (B, M, K), dtype=jnp.float32)
        x2 = jax.random.normal(k2, (B, K, N), dtype=jnp.float32)
        x1_scale = jnp.full((1,), 8.0 / 255.0, dtype=jnp.float32)
        x1_zp = jnp.full((1,), 128.0, dtype=jnp.float32)
        x2_scale = jnp.full((1,), 8.0 / 255.0, dtype=jnp.float32)
        x2_zp = jnp.full((1,), 128.0, dtype=jnp.float32)
        return {'x1': x1, 'x2': x2, 'x1_scale': x1_scale, 'x1_zp': x1_zp, 'x2_scale': x2_scale, 'x2_zp': x2_zp}
    _L0_xattn_all = _L0_xattn_setup()
    _L0_xattn_in = {k: v for k, v in _L0_xattn_all.items() if k in ('x1_scale', 'x1_zp', 'x2_scale', 'x2_zp')}
    del _L0_xattn_all

    def _L0_ffn_setup():
        import jax, jax.numpy as jnp
        import numpy as np
        import math
        B, S, IN, OUT = (4, 256, 512, 512)
        E, R, K = (8, 64, 128)
        SCALE = 64.0 / 64.0
        MULTIPLIER = 1.0
        key = jax.random.key(seed)
        ks = jax.random.split(key, 6)
        return {'x': jax.random.normal(ks[0], (B, S, IN), jnp.float32), 'W_org': jax.random.normal(ks[1], (OUT, IN), jnp.float32) * 0.02, 'lora_down': jax.random.normal(ks[2], (E, IN, R), jnp.float32) * 0.02, 'lora_up': jax.random.normal(ks[3], (E, R, OUT), jnp.float32) * 0.02, 'lora_keys': jax.random.normal(ks[4], (E, K), jnp.float32), 'Wq': jax.random.normal(ks[5], (K, IN), jnp.float32) * 0.02}
    _L0_ffn_all = _L0_ffn_setup()
    _L0_ffn_in = {k: v for k, v in _L0_ffn_all.items() if k in ('W_org', 'lora_down', 'lora_up', 'lora_keys', 'Wq')}
    del _L0_ffn_all

    def _L1_xattn_setup():
        import jax, jax.numpy as jnp
        import numpy as np
        HEADS = 32
        KV_HEADS = 8
        HEAD_DIM = 128
        EPS = 1e-06

        def rms_norm(x, w):
            var = jnp.mean(jnp.square(x.astype(jnp.float32)), axis=-1, keepdims=True)
            return (x.astype(jnp.float32) * jax.lax.rsqrt(var + EPS)).astype(x.dtype) * w
        key = jax.random.key(seed)
        ks = jax.random.split(key, 6)
        bsz, n_lat, seq, hidden = (8, 64, 512, 512)
        return {'latents': jax.random.normal(ks[0], (bsz, n_lat, hidden), jnp.float32), 'context': jax.random.normal(ks[1], (bsz, seq, hidden), jnp.float32), 'Wq': jax.random.normal(ks[2], (hidden, HEADS * HEAD_DIM), jnp.float32) * 0.02, 'Wk': jax.random.normal(ks[3], (hidden, KV_HEADS * HEAD_DIM), jnp.float32) * 0.02, 'Wv': jax.random.normal(ks[4], (hidden, KV_HEADS * HEAD_DIM), jnp.float32) * 0.02, 'Wo': jax.random.normal(ks[5], (HEADS * HEAD_DIM, hidden), jnp.float32) * 0.02, 'q_norm_w': jnp.ones((HEAD_DIM,), jnp.float32), 'k_norm_w': jnp.ones((HEAD_DIM,), jnp.float32)}
    _L1_xattn_all = _L1_xattn_setup()
    _L1_xattn_in = {k: v for k, v in _L1_xattn_all.items() if k in ('Wq', 'Wk', 'Wv', 'Wo', 'q_norm_w', 'k_norm_w')}
    del _L1_xattn_all

    def _L1_ffn_setup():
        import jax, jax.numpy as jnp
        import numpy as np
        DIM = 512
        INTER = 1792
        SPARSITY = 32
        RANK = 16
        key = jax.random.key(seed)
        ks = jax.random.split(key, 5)
        B, T = (32, 1)
        x = jax.random.normal(ks[0], (B, T, DIM), dtype=jnp.float32)
        c1_w = jax.random.normal(ks[1], (RANK, DIM), dtype=jnp.float32) * (1.0 / np.sqrt(DIM))
        c2_w = jax.random.normal(ks[2], (INTER, RANK), dtype=jnp.float32) * (1.0 / np.sqrt(RANK))
        w1 = jax.random.normal(ks[3], (INTER, DIM), dtype=jnp.float32) * (1.0 / np.sqrt(DIM))
        w2t = jax.random.normal(ks[4], (INTER, DIM), dtype=jnp.float32) * (1.0 / np.sqrt(INTER))
        return {'x': x, 'c1_w': c1_w, 'c2_w': c2_w, 'w1': w1, 'w2t': w2t}
    _L1_ffn_all = _L1_ffn_setup()
    _L1_ffn_in = {k: v for k, v in _L1_ffn_all.items() if k in ('c1_w', 'c2_w', 'w1', 'w2t')}
    del _L1_ffn_all

    def _L2_xattn_setup():
        import jax, jax.numpy as jnp
        import numpy as np
        BS, SEQ, D_MODEL = (4, 128, 512)
        N_Q_HEADS, N_KV_HEADS, D_K, D_V = (32, 8, 128, 128)
        ROPE_BASE = 10000.0

        def _rotate_half(x):
            x1, x2 = jnp.split(x, 2, axis=-1)
            return jnp.concatenate([-x2, x1], axis=-1)

        def _apply_rope(x, pos0):
            d = x.shape[-1]
            seq = x.shape[2]
            inv_freq = 1.0 / ROPE_BASE ** (jnp.arange(0, d, 2, dtype=jnp.float32) / d)
            pos = (pos0 + jnp.arange(seq)).astype(jnp.float32)
            ang = pos[:, None] * inv_freq[None, :]
            cos = jnp.concatenate([jnp.cos(ang), jnp.cos(ang)], axis=-1)
            sin = jnp.concatenate([jnp.sin(ang), jnp.sin(ang)], axis=-1)
            return x * cos[None, None] + _rotate_half(x) * sin[None, None]
        key = jax.random.key(seed)
        ks = jax.random.split(key, 8)
        w_scale = 0.02
        return {'query': jax.random.normal(ks[0], (BS, SEQ, D_MODEL), dtype=jnp.float32), 'key': jax.random.normal(ks[1], (BS, SEQ, D_MODEL), dtype=jnp.float32), 'value': jax.random.normal(ks[2], (BS, SEQ, D_MODEL), dtype=jnp.float32), 'mask': jnp.zeros((BS, SEQ, SEQ), dtype=jnp.float32), 'wq': jax.random.normal(ks[3], (D_MODEL, N_Q_HEADS * D_K), dtype=jnp.float32) * w_scale, 'wk': jax.random.normal(ks[4], (D_MODEL, N_KV_HEADS * D_K), dtype=jnp.float32) * w_scale, 'wv': jax.random.normal(ks[5], (D_MODEL, N_KV_HEADS * D_V), dtype=jnp.float32) * w_scale, 'wo': jax.random.normal(ks[6], (N_Q_HEADS * D_V, D_MODEL), dtype=jnp.float32) * w_scale, 'curr_seq_pos': 0}
    _L2_xattn_all = _L2_xattn_setup()
    _L2_xattn_in = {k: v for k, v in _L2_xattn_all.items() if k in ('wq', 'wk', 'wv', 'wo')}
    del _L2_xattn_all

    def _L2_ffn_setup():
        import jax, jax.numpy as jnp
        import numpy as np
        SCALE = 16.0 / 8.0
        key = jax.random.key(seed)
        ks = jax.random.split(key, 6)
        B, S, IN, OUT, E, R = (4, 256, 512, 512, 4, 8)
        x = jax.random.normal(ks[0], (B, S, IN), dtype=jnp.float32)
        W = jax.random.normal(ks[1], (OUT, IN), dtype=jnp.float32) * 0.02
        b = jax.random.normal(ks[2], (OUT,), dtype=jnp.float32) * 0.02
        A = jax.random.normal(ks[3], (E, R, IN), dtype=jnp.float32) * 0.02
        Bm = jax.random.normal(ks[4], (E, OUT, R), dtype=jnp.float32) * 0.02
        Wr = jax.random.normal(ks[5], (E, IN), dtype=jnp.float32) * 0.02
        return {'x': x, 'W': W, 'b': b, 'A': A, 'Bm': Bm, 'Wr': Wr}
    _L2_ffn_all = _L2_ffn_setup()
    _L2_ffn_in = {k: v for k, v in _L2_ffn_all.items() if k in ('W', 'b', 'A', 'Bm', 'Wr')}
    del _L2_ffn_all

    def _L3_xattn_setup():
        import jax, jax.numpy as jnp
        import numpy as np
        B, Q, D = (8, 64, 512)
        CTX = 512
        H, KV, HD = (16, 4, 96)
        G = H // KV
        key = jax.random.key(seed)
        ks = jax.random.split(key, 6)
        s = 0.02
        return {'latents': jax.random.normal(ks[0], (B, Q, D), jnp.float32), 'context': jax.random.normal(ks[1], (B, CTX, D), jnp.float32), 'Wq': jax.random.normal(ks[2], (H * HD, D), jnp.float32) * s, 'Wk': jax.random.normal(ks[3], (KV * HD, D), jnp.float32) * s, 'Wv': jax.random.normal(ks[4], (KV * HD, D), jnp.float32) * s, 'Wo': jax.random.normal(ks[5], (D, H * HD), jnp.float32) * s}
    _L3_xattn_all = _L3_xattn_setup()
    _L3_xattn_in = {k: v for k, v in _L3_xattn_all.items() if k in ('Wq', 'Wk', 'Wv', 'Wo')}
    del _L3_xattn_all

    def _L3_ffn_setup():
        import jax, jax.numpy as jnp
        import numpy as np
        B, S, D = (4, 256, 512)
        NUM_EXPERTS, TOP_K = (3, 2)

        def _expert_outputs(h, w1, b1, w2, b2):
            pre = jnp.einsum('bsd,edf->ebsf', h, w1) + b1[:, None, None, :]
            act = jnp.stack([jnp.tanh(pre[0]), jax.nn.gelu(pre[1], approximate=False), jax.nn.silu(pre[2])])
            return jnp.einsum('ebsf,efd->ebsd', act, w2) + b2[:, None, None, :]
        key = jax.random.key(seed)
        ks = jax.random.split(key, 8)
        scale_in = 1.0 / np.sqrt(D)
        scale_gate = 1.0 / np.sqrt(D + 1)
        return {'h': jax.random.normal(ks[0], (B, S, D), dtype=jnp.float32), 'gate_w': jax.random.uniform(ks[1], (D + 1, NUM_EXPERTS), minval=-scale_gate, maxval=scale_gate, dtype=jnp.float32), 'gate_b': jnp.zeros((NUM_EXPERTS,), dtype=jnp.float32), 'w1': jax.random.uniform(ks[2], (NUM_EXPERTS, D, D), minval=-scale_in, maxval=scale_in, dtype=jnp.float32), 'b1': jnp.zeros((NUM_EXPERTS, D), dtype=jnp.float32), 'w2': jax.random.uniform(ks[3], (NUM_EXPERTS, D, D), minval=-scale_in, maxval=scale_in, dtype=jnp.float32), 'b2': jnp.zeros((NUM_EXPERTS, D), dtype=jnp.float32)}
    _L3_ffn_all = _L3_ffn_setup()
    _L3_ffn_in = {k: v for k, v in _L3_ffn_all.items() if k in ('gate_w', 'gate_b', 'w1', 'b1', 'w2', 'b2')}
    del _L3_ffn_all
    return {'x': x, 'ctx_4096': ctx_4096, 'mask_BxSxS2_ff0': mask_BxSxS2_ff0, 'g_xattn': g_xattn, 'g_ffn': g_ffn, 'L0_xattn_x1_scale': _L0_xattn_in['x1_scale'], 'L0_xattn_x1_zp': _L0_xattn_in['x1_zp'], 'L0_xattn_x2_scale': _L0_xattn_in['x2_scale'], 'L0_xattn_x2_zp': _L0_xattn_in['x2_zp'], 'L0_ffn_W_org': _L0_ffn_in['W_org'], 'L0_ffn_lora_down': _L0_ffn_in['lora_down'], 'L0_ffn_lora_up': _L0_ffn_in['lora_up'], 'L0_ffn_lora_keys': _L0_ffn_in['lora_keys'], 'L0_ffn_Wq': _L0_ffn_in['Wq'], 'L1_xattn_Wq': _L1_xattn_in['Wq'], 'L1_xattn_Wk': _L1_xattn_in['Wk'], 'L1_xattn_Wv': _L1_xattn_in['Wv'], 'L1_xattn_Wo': _L1_xattn_in['Wo'], 'L1_xattn_q_norm_w': _L1_xattn_in['q_norm_w'], 'L1_xattn_k_norm_w': _L1_xattn_in['k_norm_w'], 'L1_ffn_c1_w': _L1_ffn_in['c1_w'], 'L1_ffn_c2_w': _L1_ffn_in['c2_w'], 'L1_ffn_w1': _L1_ffn_in['w1'], 'L1_ffn_w2t': _L1_ffn_in['w2t'], 'L2_xattn_wq': _L2_xattn_in['wq'], 'L2_xattn_wk': _L2_xattn_in['wk'], 'L2_xattn_wv': _L2_xattn_in['wv'], 'L2_xattn_wo': _L2_xattn_in['wo'], 'L2_ffn_W': _L2_ffn_in['W'], 'L2_ffn_b': _L2_ffn_in['b'], 'L2_ffn_A': _L2_ffn_in['A'], 'L2_ffn_Bm': _L2_ffn_in['Bm'], 'L2_ffn_Wr': _L2_ffn_in['Wr'], 'L3_xattn_Wq': _L3_xattn_in['Wq'], 'L3_xattn_Wk': _L3_xattn_in['Wk'], 'L3_xattn_Wv': _L3_xattn_in['Wv'], 'L3_xattn_Wo': _L3_xattn_in['Wo'], 'L3_ffn_gate_w': _L3_ffn_in['gate_w'], 'L3_ffn_gate_b': _L3_ffn_in['gate_b'], 'L3_ffn_w1': _L3_ffn_in['w1'], 'L3_ffn_b1': _L3_ffn_in['b1'], 'L3_ffn_w2': _L3_ffn_in['w2'], 'L3_ffn_b2': _L3_ffn_in['b2']}

def reference(x, ctx_4096, mask_BxSxS2_ff0, g_xattn, g_ffn, L0_xattn_x1_scale, L0_xattn_x1_zp, L0_xattn_x2_scale, L0_xattn_x2_zp, L0_ffn_W_org, L0_ffn_lora_down, L0_ffn_lora_up, L0_ffn_lora_keys, L0_ffn_Wq, L1_xattn_Wq, L1_xattn_Wk, L1_xattn_Wv, L1_xattn_Wo, L1_xattn_q_norm_w, L1_xattn_k_norm_w, L1_ffn_c1_w, L1_ffn_c2_w, L1_ffn_w1, L1_ffn_w2t, L2_xattn_wq, L2_xattn_wk, L2_xattn_wv, L2_xattn_wo, L2_ffn_W, L2_ffn_b, L2_ffn_A, L2_ffn_Bm, L2_ffn_Wr, L3_xattn_Wq, L3_xattn_Wk, L3_xattn_Wv, L3_xattn_Wo, L3_ffn_gate_w, L3_ffn_gate_b, L3_ffn_w1, L3_ffn_b1, L3_ffn_w2, L3_ffn_b2):
    import jax
    import jax.numpy as jnp

    def _L0_xattn_ref(x1, x2, x1_scale, x1_zp, x2_scale, x2_zp):
        import jax, jax.numpy as jnp
        import numpy as np
        QMIN = 0.0
        QMAX = 255.0

        def fake_quant(x, scale, zp):
            s = scale.reshape(())
            z = zp.reshape(())
            q = jnp.clip(jnp.round(x / s + z), QMIN, QMAX)
            return (q - z) * s
        q1 = fake_quant(x1, x1_scale, x1_zp)
        q2 = fake_quant(x2, x2_scale, x2_zp)
        return jnp.matmul(q1, q2)

    def _L0_ffn_ref(x, W_org, lora_down, lora_up, lora_keys, Wq):
        import jax, jax.numpy as jnp
        import numpy as np
        import math
        B, S, IN, OUT = (4, 256, 512, 512)
        E, R, K = (8, 64, 128)
        SCALE = 64.0 / 64.0
        MULTIPLIER = 1.0
        base = jnp.einsum('bsi,oi->bso', x, W_org)
        q = jnp.einsum('bi,ki->bk', x.mean(axis=1), Wq)
        scores = jnp.einsum('bk,ek->be', q, lora_keys) / math.sqrt(K)
        coeffs = jax.nn.softmax(scores, axis=-1)
        h = jnp.einsum('bsi,eir->bser', x, lora_down)
        delta = jnp.einsum('be,bser,ero->bso', coeffs, h, lora_up)
        return base + delta * (SCALE * MULTIPLIER)

    def _L1_xattn_ref(latents, context, Wq, Wk, Wv, Wo, q_norm_w, k_norm_w):
        import jax, jax.numpy as jnp
        import numpy as np
        HEADS = 32
        KV_HEADS = 8
        HEAD_DIM = 128
        EPS = 1e-06

        def rms_norm(x, w):
            var = jnp.mean(jnp.square(x.astype(jnp.float32)), axis=-1, keepdims=True)
            return (x.astype(jnp.float32) * jax.lax.rsqrt(var + EPS)).astype(x.dtype) * w
        bsz, q_len, hidden = latents.shape
        kv = jnp.concatenate([context, latents], axis=1)
        kv_len = kv.shape[1]
        groups = HEADS // KV_HEADS
        q = (latents @ Wq).reshape(bsz, q_len, HEADS, HEAD_DIM).transpose(0, 2, 1, 3)
        k = (kv @ Wk).reshape(bsz, kv_len, KV_HEADS, HEAD_DIM).transpose(0, 2, 1, 3)
        v = (kv @ Wv).reshape(bsz, kv_len, KV_HEADS, HEAD_DIM).transpose(0, 2, 1, 3)
        q = rms_norm(q, q_norm_w)
        k = rms_norm(k, k_norm_w)
        qg = q.reshape(bsz, KV_HEADS, groups, q_len, HEAD_DIM)
        scale = 1.0 / np.sqrt(HEAD_DIM)
        scores = jnp.einsum('bhgqd,bhkd->bhgqk', qg, k) * scale
        probs = jax.nn.softmax(scores.astype(jnp.float32), axis=-1).astype(q.dtype)
        out = jnp.einsum('bhgqk,bhkd->bhgqd', probs, v)
        out = out.reshape(bsz, HEADS, q_len, HEAD_DIM).transpose(0, 2, 1, 3)
        out = out.reshape(bsz, q_len, HEADS * HEAD_DIM)
        return out @ Wo

    def _L1_ffn_ref(x, c1_w, c2_w, w1, w2t):
        import jax, jax.numpy as jnp
        import numpy as np
        DIM = 512
        INTER = 1792
        SPARSITY = 32
        RANK = 16
        B, T, M = x.shape
        xf = x.reshape(B * T, M)
        inter = xf @ c1_w.T @ c2_w.T
        n_blocks = INTER // SPARSITY
        blk = inter.reshape(B * T, n_blocks, SPARSITY)
        idx = jnp.argmax(blk, axis=-1) + jnp.arange(0, INTER, SPARSITY)
        w1_g = w1[idx]
        w2_g = w2t[idx]
        h = jax.nn.relu(jnp.einsum('bkm,bm->bk', w1_g, xf))
        out = jnp.einsum('bk,bkm->bm', h, w2_g)
        return out.reshape(B, T, M)

    def _L2_xattn_ref(query, key, value, mask, wq, wk, wv, wo, curr_seq_pos):
        import jax, jax.numpy as jnp
        import numpy as np
        BS, SEQ, D_MODEL = (4, 128, 512)
        N_Q_HEADS, N_KV_HEADS, D_K, D_V = (32, 8, 128, 128)
        ROPE_BASE = 10000.0

        def _rotate_half(x):
            x1, x2 = jnp.split(x, 2, axis=-1)
            return jnp.concatenate([-x2, x1], axis=-1)

        def _apply_rope(x, pos0):
            d = x.shape[-1]
            seq = x.shape[2]
            inv_freq = 1.0 / ROPE_BASE ** (jnp.arange(0, d, 2, dtype=jnp.float32) / d)
            pos = (pos0 + jnp.arange(seq)).astype(jnp.float32)
            ang = pos[:, None] * inv_freq[None, :]
            cos = jnp.concatenate([jnp.cos(ang), jnp.cos(ang)], axis=-1)
            sin = jnp.concatenate([jnp.sin(ang), jnp.sin(ang)], axis=-1)
            return x * cos[None, None] + _rotate_half(x) * sin[None, None]
        bs, sq, _ = query.shape
        n_groups = N_Q_HEADS // N_KV_HEADS
        q = (query @ wq).reshape(bs, sq, N_Q_HEADS, D_K).transpose((0, 2, 1, 3))
        sk = key.shape[1]
        k = (key @ wk).reshape(bs, sk, N_KV_HEADS, 1, D_K)
        k = jnp.repeat(k, n_groups, axis=3).reshape(bs, sk, N_Q_HEADS, D_K).transpose((0, 2, 1, 3))
        v = (value @ wv).reshape(bs, sk, N_KV_HEADS, 1, D_V)
        v = jnp.repeat(v, n_groups, axis=3).reshape(bs, sk, N_Q_HEADS, D_V).transpose((0, 2, 1, 3))
        scale = jnp.sqrt(jnp.float32(D_K))
        q = _apply_rope(q, curr_seq_pos)
        k = _apply_rope(k, curr_seq_pos)
        raw = jnp.einsum('bhqd,bhkd->bhqk', q, k) / scale
        masked = raw + mask[:bs, None, curr_seq_pos:curr_seq_pos + sq, :sk]
        attn = jax.nn.softmax(masked, axis=-1)
        out = jnp.einsum('bhqk,bhkd->bhqd', attn, v)
        out = out.transpose((0, 2, 1, 3)).reshape(bs, sq, N_Q_HEADS * D_V)
        return out @ wo

    def _L2_ffn_ref(x, W, b, A, Bm, Wr):
        import jax, jax.numpy as jnp
        import numpy as np
        SCALE = 16.0 / 8.0
        base_out = jnp.einsum('bsi,oi->bso', x, W) + b
        gates = jax.nn.softmax(jnp.einsum('bsi,ei->bse', x, Wr), axis=-1)
        proj_r = jnp.einsum('bsi,eri->bser', x, A)
        lora_out = jnp.einsum('bser,eor->bseo', proj_r, Bm)
        lora_mix = jnp.einsum('bse,bseo->bso', gates * SCALE, lora_out)
        return base_out + lora_mix

    def _L3_xattn_ref(latents, context, Wq, Wk, Wv, Wo):
        import jax, jax.numpy as jnp
        import numpy as np
        B, Q, D = (8, 64, 512)
        CTX = 512
        H, KV, HD = (16, 4, 96)
        G = H // KV
        b, q_len, _ = latents.shape
        hidden = jnp.concatenate([context, latents], axis=1)
        s_len = hidden.shape[1]
        q = (latents @ Wq.T).reshape(b, q_len, H, HD)
        k = (hidden @ Wk.T).reshape(b, s_len, KV, HD)
        v = (hidden @ Wv.T).reshape(b, s_len, KV, HD)
        q = q.transpose(0, 2, 1, 3).reshape(b, KV, G, q_len, HD)
        k = k.transpose(0, 2, 1, 3)
        v = v.transpose(0, 2, 1, 3)
        scale = 1.0 / jnp.sqrt(jnp.asarray(HD, q.dtype))
        scores = jnp.einsum('bkgqd,bksd->bkgqs', q, k) * scale
        attn = jax.nn.softmax(scores.astype(jnp.float32), axis=-1).astype(q.dtype)
        out = jnp.einsum('bkgqs,bksd->bkgqd', attn, v)
        out = out.reshape(b, H, q_len, HD).transpose(0, 2, 1, 3).reshape(b, q_len, H * HD)
        return out @ Wo.T

    def _L3_ffn_ref(h, gate_w, gate_b, w1, b1, w2, b2):
        import jax, jax.numpy as jnp
        import numpy as np
        B, S, D = (4, 256, 512)
        NUM_EXPERTS, TOP_K = (3, 2)

        def _expert_outputs(h, w1, b1, w2, b2):
            pre = jnp.einsum('bsd,edf->ebsf', h, w1) + b1[:, None, None, :]
            act = jnp.stack([jnp.tanh(pre[0]), jax.nn.gelu(pre[1], approximate=False), jax.nn.silu(pre[2])])
            return jnp.einsum('ebsf,efd->ebsd', act, w2) + b2[:, None, None, :]
        b, s, d = h.shape
        vision_len = int(s * 0.3)
        text_strength = jnp.mean(jnp.abs(h[:, vision_len:, :]), axis=(1, 2), keepdims=True)
        vision_strength = jnp.mean(jnp.abs(h[:, :vision_len, :]), axis=(1, 2), keepdims=True)
        modality_ratio = text_strength / (vision_strength + 1e-08)
        modality_ratio = jnp.broadcast_to(modality_ratio, (b, s, 1))
        router_input = jnp.concatenate([h, modality_ratio], axis=-1)
        gate_logits = router_input @ gate_w + gate_b
        gate_scores = jax.nn.softmax(gate_logits, axis=-1)
        top_val, top_idx = jax.lax.top_k(gate_scores, TOP_K)
        top_val = top_val / (jnp.sum(top_val, axis=-1, keepdims=True) + 1e-08)
        expert_out = _expert_outputs(h, w1, b1, w2, b2)
        moe_out = jnp.zeros_like(h)
        batch_idx = jnp.arange(b)
        for i in range(TOP_K):
            j = top_idx[:, 0, i]
            out_i = expert_out[j, batch_idx]
            moe_out = moe_out + top_val[..., i:i + 1] * out_i
        return moe_out
    x = x + jnp.tanh(g_xattn[0]) * _L0_xattn_ref(_layernorm(x, axis=-1), ctx_4096, L0_xattn_x1_scale, L0_xattn_x1_zp, L0_xattn_x2_scale, L0_xattn_x2_zp)
    x = x + jnp.tanh(g_ffn[0]) * _L0_ffn_ref(_layernorm(x, axis=-1), L0_ffn_W_org, L0_ffn_lora_down, L0_ffn_lora_up, L0_ffn_lora_keys, L0_ffn_Wq)
    x = x + jnp.tanh(g_xattn[1]) * _L1_xattn_ref(_layernorm(x, axis=-1), ctx_4096, L1_xattn_Wq, L1_xattn_Wk, L1_xattn_Wv, L1_xattn_Wo, L1_xattn_q_norm_w, L1_xattn_k_norm_w)
    x = x + jnp.tanh(g_ffn[1]) * _L1_ffn_ref(_layernorm(x, axis=-1), L1_ffn_c1_w, L1_ffn_c2_w, L1_ffn_w1, L1_ffn_w2t)
    x = x + jnp.tanh(g_xattn[2]) * _L2_xattn_ref(_layernorm(x, axis=-1), ctx_4096, ctx_4096, mask_BxSxS2_ff0, L2_xattn_wq, L2_xattn_wk, L2_xattn_wv, L2_xattn_wo, 0)
    x = x + jnp.tanh(g_ffn[2]) * _L2_ffn_ref(_layernorm(x, axis=-1), L2_ffn_W, L2_ffn_b, L2_ffn_A, L2_ffn_Bm, L2_ffn_Wr)
    x = x + jnp.tanh(g_xattn[3]) * _L3_xattn_ref(_layernorm(x, axis=-1), ctx_4096, L3_xattn_Wq, L3_xattn_Wk, L3_xattn_Wv, L3_xattn_Wo)
    x = x + jnp.tanh(g_ffn[3]) * _L3_ffn_ref(_layernorm(x, axis=-1), L3_ffn_gate_w, L3_ffn_gate_b, L3_ffn_w1, L3_ffn_b1, L3_ffn_w2, L3_ffn_b2)
    return x

_drawn_inputs = setup_inputs


def setup_inputs(seed=0):
    import zlib

    import numpy as np

    out = dict(_drawn_inputs(seed))
    spreads = {'L1_xattn_q_norm_w': (1.0, 0.6),
     'L1_xattn_k_norm_w': (1.0, 0.6),
     'L3_ffn_gate_b': (0.0, 0.8),
     'L3_ffn_b1': (0.0, 0.8),
     'L3_ffn_b2': (0.0, 2.0)}
    factors = {'g_ffn': 8.0,
     'L0_ffn_lora_down': 8.0,
     'L0_ffn_lora_up': 8.0,
     'L0_ffn_lora_keys': 8.0,
     'L0_ffn_Wq': 8.0,
     'L1_xattn_Wq': 7.173,
     'L1_xattn_Wk': 7.211,
     'L1_xattn_Wv': 4.063,
     'L1_xattn_Wo': 4.121,
     'L1_ffn_c1_w': 7.702,
     'L1_ffn_c2_w': 7.623,
     'L1_ffn_w1': 8.0,
     'L1_ffn_w2t': 7.518,
     'L2_xattn_wq': 8.0,
     'L2_xattn_wk': 8.0,
     'L2_xattn_wv': 3.805,
     'L2_xattn_wo': 4.053,
     'L2_ffn_b': 8.0,
     'L2_ffn_A': 8.0,
     'L2_ffn_Bm': 8.0,
     'L2_ffn_Wr': 8.0,
     'L3_xattn_Wq': 8.0,
     'L3_xattn_Wk': 8.0,
     'L3_xattn_Wv': 8.0,
     'L3_xattn_Wo': 8.0,
     'L3_ffn_gate_w': 7.823,
     'L3_ffn_w1': 6.852,
     'L3_ffn_w2': 6.617}
    for name, (base, spread) in spreads.items():
        noise = np.random.default_rng([zlib.crc32(name.encode()), seed]).standard_normal(out[name].shape)
        drawn = base * np.exp(spread * noise) if base else spread * noise
        out[name] = jnp.asarray(drawn.astype(out[name].dtype))
    for name, factor in factors.items():
        out[name] = (out[name] * factor).astype(out[name].dtype)
    return out
```

```python
from contextlib import ExitStack

import numpy as np

import concourse.bass as bass
from concourse import mybir

F32 = mybir.dt.float32
BF16 = mybir.dt.bfloat16
ALU = mybir.AluOpType
ACT = mybir.ActivationFunctionType
AX = mybir.AxisListType

P = 128
D = 512
DC = D // P
NB = 2
SQ = 256
TOK = NB * SQ
NT = TOK // P
SC = 512
BANK = 512
GROUP = 4
ROUND = 12582912.0


def three(pe, out, lhs, rhs, first, last):
    (lh, ll), (rh, rl) = lhs, rhs
    pe.matmul(out, lh, rh, start=first, stop=False)
    pe.matmul(out, lh, rl, start=False, stop=False)
    return pe.matmul(out, ll, rh, start=False, stop=last)


class Chain:

    def __init__(self, eng, sem):
        self.eng, self.sem, self.n = eng, sem, 0

    def __call__(self, ins):
        self.n += 1
        ins.then_inc(self.sem, 1)
        self.eng.wait_ge(self.sem, self.n)


class Core:

    def __init__(self, nc, ctx):
        self.nc, self.ctx = nc, ctx
        self.attention_sems = {}
        self.ps = ctx.enter_context(nc.psum_tensor("psum", [P, 8 * BANK], F32))
        self.x = self.sb("x_state", [P, NT, D])
        self.xn = self.sb("x_normed", [P, NT, D])
        self.xT = [self.sb(f"x_normed_T_{part}", [P, DC, TOK], BF16) for part in ("hi", "lo")]
        self.ctxT = [self.sb(f"context_T_{part}", [P, DC, NB * SC], BF16) for part in ("hi", "lo")]
        self.ident = self.sb("identity", [P, P])
        self.ones = self.sb("ones", [P, P])
        self.minus_half = self.sb("minus_half", [P, 16])
        self.gates = self.sb("gates", [P, 8])
        self.stats = self.sb("ln_stats", [P, NT, 6])
        self.meanvar = self.sb("ln_meanvar", [P, NT, 2])
        self.var_eps = self.sb("ln_var_eps", [P, NT])
        self.rstd = self.sb("ln_rstd", [P, NT])

    def sb(self, name, shape, dt=F32, ctx=None):
        return (ctx or self.ctx).enter_context(self.nc.sbuf_tensor(name, shape, dt))

    def sem(self, name):
        return self.ctx.enter_context(self.nc.semaphore(name))

    def bank(self, b, n=BANK, parts=P, at=0):
        return self.ps[0:parts, b * BANK + at:b * BANK + at + n]


class LayerNorm:

    def __init__(self, core, n):
        self.c, self.n, self.turns = core, n, max(n - 1, 0)
        if n == 0:
            core.ln_sems = [core.sem(f"ln_{s}") for s in (
                "stats_done", "rstd_done", "normed", "turned", "hi_done", "lo_done")]
        self.stats_done, self.rstd_done, self.normed, self.turned, self.hi_done, self.lo_done = core.ln_sems

    def wait_stats(self, eng, k):
        eng.wait_ge(self.stats_done, 2 * NT * self.n + k)

    def wait_rstd(self, eng, k):
        eng.wait_ge(self.rstd_done, 2 * self.n + k)

    def wait_normed(self, eng, k):
        eng.wait_ge(self.normed, NT * self.n + k)

    def wait_turned(self, eng, k):
        eng.wait_ge(self.turned, DC * self.turns + k)

    def wait_hi(self, eng, k):
        eng.wait_ge(self.hi_done, DC * self.turns + k)

    def wait_lo(self, eng, k):
        eng.wait_ge(self.lo_done, DC * self.turns + k)

    def vector_norm(self, dve):
        c = self.c
        for t in range(NT):
            dve.bn_stats(c.stats[:, t, :], c.x[:, t, :]).then_inc(self.stats_done, 1)
        for t in range(NT):
            self.wait_stats(dve, t + 1)
            dve.bn_aggr(c.meanvar[:, t, :], c.stats[:, t, :]).then_inc(self.stats_done, 1)
        self.wait_stats(dve, 2 * NT)
        self.wait_rstd(dve, 2)
        for t in range(NT):
            dve.tensor_scalar(c.xn[:, t, :], c.x[:, t, :], c.meanvar[:, t, 0:1], c.rstd[:, t:t + 1],
                              ALU.subtract, ALU.mult).then_inc(self.normed, 1)

    def gpsimd(self, pool):
        c = self.c
        self.wait_stats(pool, 2 * NT)
        pool.tensor_scalar(c.var_eps[:], c.meanvar[:, :, 1], 1e-5, None, ALU.add).then_inc(self.rstd_done, 1)
        self.wait_rstd(pool, 1)
        pool.tensor_tensor(c.rstd[:], c.var_eps[:], c.minus_half[:, 0:NT], ALU.pow).then_inc(self.rstd_done, 1)

    def tensor_turn(self, pe):
        c = self.c
        for d in range(DC):
            for t in range(NT):
                if d == 0:
                    self.wait_normed(pe, t + 1)
                last = pe.transpose(c.bank(d, P, at=t * P), c.xn[:, t, d * P:(d + 1) * P], c.ident[:])
            last.then_inc(self.turned, 1)

    def scalar_hi(self, act):
        c = self.c
        for d in range(DC):
            self.wait_turned(act, d + 1)
            act.activation(c.xT[0][:, d, :], c.bank(d), ACT.Copy).then_inc(self.hi_done, 1)

    def vector_lo(self, dve):
        c = self.c
        for d in range(DC):
            self.wait_hi(dve, d + 1)
            dve.tensor_tensor(c.xT[1][:, d, :], c.bank(d), c.xT[0][:, d, :], ALU.subtract)\
               .then_inc(self.lo_done, 1)

    def wait_parts(self, eng):
        self.wait_hi(eng, DC)
        self.wait_lo(eng, DC)


def setup_and_quant_product(nc, core, a):
    c = core
    KT = SC // P
    ln = LayerNorm(c, 0)
    loaded_x, loaded_small, loaded_ctx, loaded_ctxT = (c.sem(n) for n in (
        "loaded_x", "loaded_small", "loaded_ctx", "loaded_ctxT"))
    ident_steps, gates_done, ctxT_hi, ctxT_lo = (c.sem(n) for n in (
        "ident_steps", "gates_done", "ctxT_hi_done", "ctxT_lo_done"))
    scal_done, q_chain, q1_done, q1_turned, q1T_done = (c.sem(n) for n in (
        "quant_scalars_done", "quant_chain", "q1_done", "q1_turned", "q1T_done"))
    q2_done, colsum_done, colsum_saved, prod_done, x_done = (c.sem(n) for n in (
        "q2_done", "colsum_done", "colsum_saved", "prod_done", "l0x_x_done"))
    with ExitStack() as st:
        ctx_nat = c.sb("context_rows", [P, NB * KT, D], ctx=st)
        ctxT_raw = c.sb("context_T_raw", [P, DC, NB * SC], ctx=st)
        q1 = c.sb("q1", [P, NT, D], BF16, st)
        q2 = c.sb("q2", [P, NB * KT, D], BF16, st)
        q1T = c.sb("q1_T", [P, DC, TOK], BF16, st)
        q1f = c.sb("q1_float", [P, D], F32, st)
        q2f = c.sb("q2_float", [P, NB * KT, D], F32, st)
        ident16 = c.sb("identity_bf16", [P, P], BF16, st)
        ones16 = c.sb("ones_bf16", [P, P], BF16, st)
        qs = c.sb("quant_scalars_in", [P, 4], F32, st)
        inv = c.sb("quant_inverse_scales", [P, 2], F32, st)
        cz = c.sb("quant_centres", [P, 2], F32, st)
        kcc = c.sb("quant_constant_term", [P, 1], F32, st)
        gss = c.sb("quant_out_scale", [P, 1], F32, st)
        rs = c.sb("q1_row_sums", [P, NT], F32, st)
        rs2 = c.sb("q1_row_terms", [P, NT], F32, st)
        csb = c.sb("q2_column_terms", [P, NB, D], F32, st)
        tmp = c.sb("l0x_sum", [P, NT, D], F32, st)
        gin = c.sb("gates_in", [P, 8], F32, st)
        with nc.Block() as block:

            @block.sync
            def _(sp):
                sp.dma_start(c.x[:], a["x"]).then_inc(loaded_x, 16)
                sp.dma_start(gin[:], a["gates"]).then_inc(loaded_small, 16)
                sp.dma_start(qs[:], a["quant"]).then_inc(loaded_small, 16)
                sp.dma_start(ctx_nat[:], a["context"]).then_inc(loaded_ctx, 16)
                sp.dma_start(ctxT_raw[:], a["context_T"]).then_inc(loaded_ctxT, 16)

            @block.gpsimd
            def _(pool):
                pool.memset(c.ident[:], 0.0).then_inc(ident_steps, 1)
                pool.memset(c.ones[:], 1.0).then_inc(ident_steps, 1)
                pool.memset(ones16[:], 1.0).then_inc(ident_steps, 1)
                pool.memset(c.minus_half[:], -0.5).then_inc(ident_steps, 1)
                pool.wait_ge(ident_steps, 1)
                pool.affine_select(out=c.ident[:], in_=c.ident[:], compare_op=ALU.not_equal, fill=1.0,
                                   base=0, pattern=[[-1, P]], channel_multiplier=1).then_inc(ident_steps, 1)
                pool.wait_ge(ident_steps, 5)
                pool.tensor_copy(ident16[:], c.ident[:]).then_inc(ident_steps, 1)
                ln.gpsimd(pool)
                for d in range(DC):
                    pool.wait_ge(ctxT_hi, d + 1)
                    pool.tensor_tensor(c.ctxT[1][:, d, :], ctxT_raw[:, d, :], c.ctxT[0][:, d, :],
                                       ALU.subtract).then_inc(ctxT_lo, 1)

            @block.scalar
            def _(act):
                act.wait_ge(loaded_small, 32)
                act.activation(c.gates[:], gin[:], ACT.Tanh).then_inc(gates_done, 1)
                for d in range(DC):
                    if d == 0:
                        act.wait_ge(loaded_ctxT, 16)
                    act.activation(c.ctxT[0][:, d, :], ctxT_raw[:, d, :], ACT.Copy).then_inc(ctxT_hi, 1)
                for d in range(DC):
                    act.wait_ge(q1_turned, d + 1)
                    act.activation(q1T[:, d, :], c.bank(d), ACT.Copy).then_inc(q1T_done, 1)

            @block.vector
            def _(dve):
                link = Chain(dve, q_chain)
                dve.wait_ge(loaded_x, 16)
                ln.vector_norm(dve)
                dve.wait_ge(loaded_small, 32)
                link(dve.reciprocal(inv[:], qs[:, 0:4:2]))
                link(dve.tensor_scalar(cz[:], qs[:, 1:4:2], -1.0, 128.0, ALU.mult, ALU.add))
                link(dve.tensor_scalar(kcc[:], cz[:, 0:1], cz[:, 1:2], float(SC), ALU.mult, ALU.mult))
                dve.wait_ge(gates_done, 1)
                link(dve.tensor_scalar(gss[:], qs[:, 0:1], qs[:, 2:3], c.gates[:, 0:1], ALU.mult, ALU.mult))
                for t in range(NT):
                    ln.wait_normed(dve, t + 1)
                    link(dve.tensor_scalar(q1f[:], c.xn[:, t, :], inv[:, 0:1], qs[:, 1:2], ALU.mult, ALU.add))
                    link(dve.tensor_scalar(q1f[:], q1f[:], ROUND, -ROUND, ALU.add, ALU.add))
                    link(dve.tensor_scalar(q1f[:], q1f[:], 0.0, 255.0, ALU.max, ALU.min))
                    dve.tensor_scalar(q1[:, t, :], q1f[:], -128.0, 0.0, ALU.add, ALU.add,
                                      accum_out=rs[:, t:t + 1]).then_inc(q1_done, 1)
                    dve.wait_ge(q1_done, t + 1)
                    link(dve.tensor_scalar(rs2[:, t:t + 1], rs[:, t:t + 1], cz[:, 1:2], None, ALU.mult))
                dve.wait_ge(loaded_ctx, 16)
                for k in range(NB * KT):
                    v = q2f[:, k, :]
                    link(dve.tensor_scalar(v, ctx_nat[:, k, :], inv[:, 1:2], qs[:, 3:4], ALU.mult, ALU.add))
                    link(dve.tensor_scalar(v, v, ROUND, -ROUND, ALU.add, ALU.add))
                    link(dve.tensor_scalar(v, v, 0.0, 255.0, ALU.max, ALU.min))
                    dve.tensor_scalar(q2[:, k, :], v, -128.0, None, ALU.add).then_inc(q2_done, 1)
                for b in range(NB):
                    dve.wait_ge(colsum_done, b + 1)
                    dve.tensor_scalar(csb[:, b, :], c.bank(4 + b), cz[:, 0:1], kcc[:, 0:1],
                                      ALU.mult, ALU.add).then_inc(colsum_saved, 1)
                dve.wait_ge(colsum_saved, NB)
                for t in range(NT):
                    dve.wait_ge(prod_done, t + 1)
                    link(dve.scalar_tensor_tensor(tmp[:, t, :], c.bank(t), rs2[:, t:t + 1],
                                                  csb[:, t // 2, :], ALU.add, ALU.add))
                    dve.scalar_tensor_tensor(c.x[:, t, :], tmp[:, t, :], gss[:, 0:1], c.x[:, t, :],
                                             ALU.mult, ALU.add).then_inc(x_done, 1)

            @block.tensor
            def _(pe):
                pe.wait_ge(ident_steps, 6)
                for d in range(DC):
                    for t in range(NT):
                        if d == 0:
                            pe.wait_ge(q1_done, t + 1)
                        last = pe.matmul(c.bank(d, P, at=t * P), q1[:, t, d * P:(d + 1) * P], ident16[:],
                                         start=True, stop=True)
                    last.then_inc(q1_turned, 1)
                for b in range(NB):
                    for k in range(KT):
                        pe.wait_ge(q2_done, b * KT + k + 1)
                        last = pe.matmul(c.bank(4 + b), ones16[:], q2[:, b * KT + k, :],
                                         start=k == 0, stop=k == KT - 1)
                    last.then_inc(colsum_done, 1)
                pe.wait_ge(q1T_done, DC)
                for t in range(NT):
                    for k in range(KT):
                        last = pe.matmul(c.bank(t), q1T[:, k, t * P:(t + 1) * P], q2[:, (t // 2) * KT + k, :],
                                         start=k == 0, stop=k == KT - 1)
                    last.then_inc(prod_done, 1)


class Attention:

    UNITS = 16
    LAST = 13

    def __init__(self, core, tag, gate, heads, hd, latents, norm=False, rope=False, mask=False):
        self.c, self.tag, self.gate, self.G, self.HD = core, tag, gate, heads, hd
        self.norm, self.rope, self.mask = norm, rope, mask
        self.NK = SC + (SQ if latents else 0)
        self.KB = self.NK // P
        self.TILES = -(-self.NK // BANK)
        self.PER = self.KB // self.TILES
        self.W = (2 + GROUP) * hd
        if norm:
            self.jobs = [("K0", 0, 0), ("K1", 1, 0), ("Q0", 2, 0), ("Q1", 3, 0), ("N", 3, 1), ("R0", 4, 1),
                         ("V0", 5, 0), ("R1", 5, 1), ("V1", 6, 0)]
        elif rope:
            self.jobs = [("K0", 0, 0), ("Q0", 2, 0), ("Q1", 4, 0), ("V0", 5, 0)]
        else:
            self.jobs = [("K0", 0, 0), ("K1", 1, 0), ("Q0", 2, 0), ("Q1", 3, 0), ("V0", 5, 0), ("V1", 6, 0)]
        names = [j[0] for j in self.jobs]
        self.by = {"act": [n != "N" for n in names], "dve": [True for n in names],
                   "pool": [n[0] == "R" or (rope and n[0] != "V") for n in names]}
        self.total = {e: sum(v) for e, v in self.by.items()}
        self.ln = LayerNorm(core, gate)
        J, T, G = len(self.jobs), self.TILES, self.G
        self.rots = sum(1 for n in names if n[0] != "V") if rope else 0
        signals = {
            "qkv_loaded": 16 * G, "wo_loaded": 16 * G, "extra_loaded": 16 * (2 * norm + 4 * rope + mask),
            "qkv_hi": 2 * G, "qkv_lo": 2 * G, "wo_hi": 4 * G, "wo_lo": 4 * G,
            "job_made": 2 * G * J, "job_act": 2 * G * self.total["act"], "job_dve": 2 * G * self.total["dve"],
            "job_pool": 2 * G * self.total["pool"], "ms_done": 2 * G * norm, "pow_done": 2 * G * norm,
            "rot_summed": 2 * G * self.rots, "scored": 16 * G, "max_done": 16 * G, "bias_done": 16 * G,
            "exp_done": 16 * G, "recip_done": 16 * G, "prob_done": 16 * G, "turned": 16 * G * T,
            "pT_hi": 16 * G * T, "pT_lo": 16 * G * T, "pv_done": 4 * G, "o_hi": 4 * G, "o_lo": 4 * G,
            "wo_made": 16 * G, "x_done": 4 * G}
        self.before, found = {}, []
        for n, per_layer in signals.items():
            sem, before = core.attention_sems.get(n) or (core.sem(f"attn_{n}"), 0)
            self.before[sem.name] = before
            core.attention_sems[n] = (sem, before + per_layer)
            found.append(sem)
        (self.qkv_loaded, self.wo_loaded, self.extra_loaded, self.qkv_hi, self.qkv_lo, self.wo_hi, self.wo_lo,
         self.job_made, self.job_act, self.job_dve, self.job_pool, self.ms_done, self.pow_done, self.rot_summed,
         self.scored, self.max_done, self.bias_done, self.exp_done, self.recip_done, self.prob_done, self.turned,
         self.pT_hi, self.pT_lo, self.pv_done, self.o_hi, self.o_lo, self.wo_made, self.x_done) = found

    def need(self, eng, sem, g, per, more):
        if isinstance(g, int):
            if per * g + more > 0:
                eng.wait_ge(sem, self.before[sem.name] + per * g + more)
        else:
            assert per + more > 0
            eng.wait_ge(sem, g * per + (more + self.before[sem.name]))


    def has(self, g, per, more):
        return not isinstance(g, int) or 0 <= per * g + more < per * self.G

    def score_cols(self, s):
        at = (s % 2) * 2 * BANK
        return at, at + self.NK

    def count(self, engine, j):
        return sum(self.by[engine][:j])

    def slot_jobs(self, g, s, after):
        half = s // 8
        if isinstance(g, int) and (g >= self.G or (g == self.G - 1 and half == 1)):
            return []
        return [(j, n, half + 1) for j, (n, at, late) in enumerate(self.jobs) if at == s % 8 and late == after]

    def job_cols(self, name):
        return {"K0": (0, SC), "K1": (SC, self.NK), "Q0": (0, 2), "Q1": (2, 4), "R0": (0, SC),
                "R1": (SC, self.NK), "V0": (0, SC // P), "V1": (SC // P, self.KB)}[name]


    def pe_job(self, pe, g, ahead, j, name):
        c, b = self.c, ahead % 2
        HD = self.HD
        prev = self.jobs[j - 1][0]
        self.need(pe, self.job_dve, g, 2 * self.total["dve"],
             ahead * self.total["dve"] + self.count("dve", j))
        if prev[0] in "KQV" and not (self.rope and prev[0] != "V"):
            self.need(pe, self.job_act, g, 2 * self.total["act"],
                 ahead * self.total["act"] + self.count("act", j))
        if name[0] in "KVQ":
            part = 2 * (ahead // 2) + (2 if name[0] == "Q" else 1)
            self.need(pe, self.qkv_hi, g, 2, part)
            self.need(pe, self.qkv_lo, g, 2, part)
        wk, wv, wq = ([w[:, :, i * HD:n * HD] for w in self.qkv] for i, n in ((0, 1), (1, 2), (2, 6)))
        if name[0] == "K":
            lo, hi = self.job_cols(name)
            src = c.ctxT if name == "K0" else c.xT
            base = b * SC if name == "K0" else b * SQ
            for d in range(DC):
                last = three(pe, c.bank(7, hi - lo, HD), [w[:, d, :] for w in wk],
                             [x[:, d, base:base + hi - lo] for x in src], d == 0, d == DC - 1)
        elif name[0] == "Q":
            for i, h in enumerate(range(*self.job_cols(name))):
                for d in range(DC):
                    last = three(pe, c.bank(7, SQ, HD, at=i * SQ), [w[:, d, h * HD:(h + 1) * HD] for w in wq],
                                 [x[:, d, b * SQ:(b + 1) * SQ] for x in c.xT], d == 0, d == DC - 1)
        elif name[0] == "V":
            for i, k in enumerate(range(*self.job_cols(name))):
                src = c.ctxT if name == "V0" else c.xT
                at = b * SC + k * P if name == "V0" else b * SQ + i * P
                for d in range(DC):
                    last = three(pe, c.bank(7, HD, at=i * HD), [x[:, d, at:at + P] for x in src],
                                 [w[:, d, :] for w in wv], d == 0, d == DC - 1)
        elif name == "N":
            self.need(pe, self.job_act, g, 2 * self.total["act"],
                 ahead * self.total["act"] + self.count("act", j))
            for i in range(self.KB + 8):
                sq = self.k_sq[:, i * P:(i + 1) * P] if i < self.KB else \
                    self.q_sq[:, (i - self.KB) * P:(i - self.KB + 1) * P]
                last = pe.matmul(c.bank(7, 1, at=i), sq, c.ones[:, 0:1], start=True, stop=True)
        else:
            lo, hi = self.job_cols(name)
            for i, k in enumerate(range(lo // P, hi // P)):
                last = pe.matmul(c.bank(7, P, at=i * P), c.ones[:], self.r_diag[:, k, :], start=True, stop=True)
        last.then_inc(self.job_made, 1)

    def pe_turn(self, pe, g, s, i):
        c, U = self.c, self.UNITS
        if self.has(g, U, s - 1):
            if i == 0:
                self.need(pe, self.prob_done, g, U, s)
            m = (s - 1) * self.TILES + i
            self.need(pe, self.pT_hi, g, U * self.TILES, m)
            self.need(pe, self.pT_lo, g, U * self.TILES, m)
            for k in range(self.PER):
                kb = i * self.PER + k
                last = pe.transpose(c.bank(4, P, at=k * P), self.E[(s - 1) % 2][:, kb * P:(kb + 1) * P], c.ident[:])
            last.then_inc(self.turned, 1)

    def pe_slot(self, pe, g, s, live):
        c, U = self.c, self.UNITS
        HD = self.HD
        if live:
            b, t, h = s // 8, s % 8 // 4, s % 4
            if s % 8 == 0:
                for sem, e in ((self.job_act, "act"), (self.job_dve, "dve"), (self.job_pool, "pool")):
                    if self.total[e]:
                        self.need(pe, sem, g, 2 * self.total[e], (b + 1) * self.total[e])
            self.need(pe, self.max_done if self.mask else self.exp_done, g, U, s - 1)
            lo, hi = self.score_cols(s)
            q = [w[0:HD, h, t * P:(t + 1) * P] for w in self.qT[b]]
            cuts = [lo] + [m for m in (BANK, 3 * BANK) if lo < m < hi] + [hi]
            for u, v in zip(cuts, cuts[1:]):
                last = three(pe, c.ps[:, u:v], q, [w[0:HD, u - lo:v - lo] for w in self.kT[b]], True, True)
            last.then_inc(self.scored, 1)
        for j, name, ahead in self.slot_jobs(g, s, 0):
            self.pe_job(pe, g, ahead, j, name)
        self.pe_turn(pe, g, s, 0)
        q, h = (s - 9) // 4, (s - 9) % 4
        if self.has(g, 4, q):
            if h == 0:
                self.need(pe, self.o_hi, g, 4, q + 1)
                self.need(pe, self.o_lo, g, 4, q + 1)
                self.need(pe, self.x_done, g, 4, q)
            if q % 4 == 0:
                self.need(pe, self.wo_hi, g, 4, q + h + 1)
                self.need(pe, self.wo_lo, g, 4, q + h + 1)
            last = three(pe, c.bank(6), [o[0:HD, h * P:(h + 1) * P] for o in self.oT[q % 2]],
                         [w[0:HD, h, :] for w in self.wo], h == 0, h == 3)
            last.then_inc(self.wo_made, 1)
        q, piece = (s - 5) // 4, (s - 5) % 4
        if self.has(g, 4, q):
            if piece == 0:
                self.need(pe, self.pT_hi, g, U * self.TILES, 4 * (q + 1) * self.TILES)
                self.need(pe, self.pT_lo, g, U * self.TILES, 4 * (q + 1) * self.TILES)
                self.need(pe, self.o_hi, g, 4, q)
                self.need(pe, self.o_lo, g, 4, q)
            v, pT = self.v[q % 4 // 2], self.pT[q % 2]
            steps = [(k, x, y) for k in range(self.KB) for x, y in ((0, 0), (0, 1), (1, 0))]
            for i in range(piece * len(steps) // 4, (piece + 1) * len(steps) // 4):
                k, x, y = steps[i]
                last = pe.matmul(c.bank(5, BANK, HD), v[x][:, k, :], pT[y][:, k, :],
                                 start=i == 0, stop=i == len(steps) - 1)
            if piece == 3:
                last.then_inc(self.pv_done, 1)
        if self.TILES == 2:
            self.pe_turn(pe, g, s, 1)
        for j, name, ahead in self.slot_jobs(g, s, 1):
            self.pe_job(pe, g, ahead, j, name)


    def act_split_qkv(self, act, g, more, part):
        cols = slice(0, 2 * self.HD) if part == 0 else slice(2 * self.HD, self.W)
        if part == 0:
            self.need(act, self.qkv_loaded, g, 16, 16 * (more + 1))
            self.need(act, self.job_made, g, 2 * len(self.jobs), 2 * more * len(self.jobs))
        act.activation(self.qkv[0][:, :, cols], self.qkv_raw[:, :, cols], ACT.Copy).then_inc(self.qkv_hi, 1)

    def act_job(self, act, g, ahead, j, name):
        c, b, HD = self.c, ahead % 2, self.HD
        if name == "N":
            return
        if name[0] == "R":
            lo, hi = self.job_cols(name)
            self.need(act, self.job_dve, g, 2 * self.total["dve"],
                 ahead * self.total["dve"] + self.count("dve", j + 1))
            last = act.activation(self.kT[b][0][:, lo:hi], self.k_raw[:, lo:hi], ACT.Copy)
        elif self.rope and name[0] != "V":
            rots = self.rots
            r = ahead * rots + sum(1 for n, *_ in self.jobs[:j] if n[0] != "V")
            self.need(act, self.rot_summed, g, 2 * rots, r + 1)
            last = act.activation(self.target(name, b, 0), self.rot[r % 2][:], ACT.Copy)
        else:
            self.need(act, self.job_made, g, 2 * len(self.jobs), ahead * len(self.jobs) + j + 1)
            if name[0] == "K":
                lo, hi = self.job_cols(name)
                if self.norm:
                    last = act.activation(self.k_sq[:, lo:hi], c.bank(7, hi - lo), ACT.Square)
                else:
                    last = act.activation(self.kT[b][0][0:HD, lo:hi], c.bank(7, hi - lo, HD), ACT.Copy)
            elif name[0] == "Q":
                if self.norm:
                    lo, hi = self.job_cols(name)
                    act.activation(self.q_sq[:, lo * SQ:hi * SQ], c.bank(7), ACT.Square)
                    last = act.activation(self.target(name, b, 0), c.bank(7), ACT.Copy, scale=self.qw[:, 0:1])
                else:
                    last = act.activation(self.target(name, b, 0), c.bank(7, BANK, HD), ACT.Copy)
            else:
                lo, hi = self.job_cols(name)
                last = act.activation(self.target(name, b, 0), c.bank(7, (hi - lo) * HD), ACT.Copy)
        last.then_inc(self.job_act, 1)

    def target(self, name, b, part):
        lo, hi = self.job_cols(name)
        if name[0] == "K":
            return self.kT[b][part][0:self.HD, lo:hi]
        if name[0] == "Q":
            return self.qT[b][part][0:self.HD, lo:hi, :].rearrange("p h q -> p (h q)")
        return self.v[b][part][:, lo:hi, :].rearrange("p k d -> p (k d)")

    def act_turned(self, act, g, s, i):
        U = self.UNITS
        if self.has(g, U, s - 1):
            q, h = (s - 1) // 4, (s - 1) % 4
            m = (s - 1) * self.TILES + i
            self.need(act, self.turned, g, U * self.TILES, m + 1)
            if h == 0 and i == 0:
                self.need(act, self.pv_done, g, 4, q - 1)
            act.activation(self.pT[q % 2][0][:, i * self.PER:(i + 1) * self.PER, h * P:(h + 1) * P],
                           self.c.bank(4, self.PER * P).rearrange("p (k q) -> p k q", q=P),
                           ACT.Copy).then_inc(self.pT_hi, 1)

    def act_slot(self, act, g, s, live):
        c, U, HD = self.c, self.UNITS, self.HD
        if live:
            b, t, h = s // 8, s % 8 // 4, s % 4
            self.need(act, self.bias_done, g, U, s + 1)
            lo, hi = self.score_cols(s)
            E = self.E[s % 2]
            if self.norm:
                scale = self.q_scale[b][:, h * 2 + t:h * 2 + t + 1]
            else:
                scale = 1.0 if self.mask else float(HD) ** -0.5
            act.activation(E[:], E[:] if self.mask else c.ps[:, lo:hi], ACT.Exp, bias=self.bias[:, s:s + 1],
                           scale=scale, accum_out=self.sums[:, s:s + 1]).then_inc(self.exp_done, 1)
        for j, name, ahead in self.slot_jobs(g, s, 0):
            self.act_job(act, g, ahead, j, name)
        self.act_turned(act, g, s, 0)
        if live and 6 <= s < 6 + GROUP:
            h = s - 6
            if h == 0:
                self.need(act, self.wo_loaded, g, 16, 16)
            self.need(act, self.wo_made, g, U, h - 3)
            act.activation(self.wo[0][0:HD, h, :], self.wo_raw[0:HD, h, :], ACT.Copy).then_inc(self.wo_hi, 1)
        if s % 4 == 0 and self.has(g, 4, s // 4 - 2):
            q = s // 4 - 2
            self.need(act, self.pv_done, g, 4, q + 1)
            self.need(act, self.wo_made, g, U, 4 * (q - 1))
            act.activation(self.oT[q % 2][0][0:HD, :], c.bank(5, BANK, HD), ACT.Copy).then_inc(self.o_hi, 1)
        if self.TILES == 2:
            self.act_turned(act, g, s, 1)
        for j, name, ahead in self.slot_jobs(g, s, 1):
            self.act_job(act, g, ahead, j, name)
        if s in (6, 7) and self.slot_jobs(g, 8, 0):
            self.act_split_qkv(act, g, 1, s - 6)


    def dve_job(self, dve, g, ahead, j, name, part=None):
        c, b, HD = self.c, ahead % 2, self.HD
        made = (2 * len(self.jobs), ahead * len(self.jobs) + j + 1)
        act_counts = (2 * self.total["act"], ahead * self.total["act"] + self.count("act", j + 1))
        if name == "N":
            halves = 2 * 1
            if part == 0:
                self.need(dve, self.job_made, g, *made)
                dve.tensor_scalar(self.ms[:], c.bank(7, self.KB + 8), 1.0 / HD, 1e-6, ALU.mult, ALU.add)\
                   .then_inc(self.ms_done, 1)
                return
            self.need(dve, self.pow_done, g, halves, ahead + 1)
            dve.tensor_tensor(self.r_diag[:], c.ident[:].unsqueeze(1).to_broadcast([P, self.KB, P]),
                              self.r[:, 0:self.KB].unsqueeze(2).to_broadcast([P, self.KB, P]), ALU.mult)
            dve.tensor_scalar(self.q_scale[b][:], self.r[:, self.KB:], float(HD) ** -0.5, None, ALU.mult)
            last = dve.tensor_scalar(self.q_scale_neg[b][:], self.r[:, self.KB:], -float(HD) ** -0.5, None, ALU.mult)
        elif name[0] == "R":
            lo, hi = self.job_cols(name)
            self.need(dve, self.job_made, g, *made)
            last = dve.tensor_tensor(self.k_raw[:, lo:hi], self.k_raw[:, lo:hi], c.bank(7, hi - lo), ALU.mult)
        elif self.rope and name[0] != "V":
            rots = self.rots
            r = ahead * rots + sum(1 for n, *_ in self.jobs[:j] if n[0] != "V")
            cos, sin = (self.k_cos, self.k_sin) if name[0] == "K" else (self.q_cos, self.q_sin)
            self.need(dve, self.job_made, g, *made)
            self.need(dve, self.job_pool, g, 2 * rots, r - 1)
            H = HD // 2
            dve.tensor_tensor(self.rot[r % 2][:], c.bank(7), cos[:], ALU.mult)
            dve.tensor_tensor(self.rot2[r % 2][0:H, :], c.ps[H:HD, 7 * BANK:8 * BANK], sin[H:HD, :], ALU.mult)
            last = dve.tensor_tensor(self.rot2[r % 2][H:HD, :], c.ps[0:H, 7 * BANK:8 * BANK], sin[0:H, :], ALU.mult)
        elif name[0] == "K" and self.norm:
            lo, hi = self.job_cols(name)
            self.need(dve, self.job_act, g, *act_counts)
            self.need(dve, self.job_pool, g, 2 * self.total["pool"], ahead * self.total["pool"])
            last = dve.tensor_scalar(self.k_raw[:, lo:hi], c.bank(7, hi - lo), self.kw[:, 0:1], None, ALU.mult)
        else:
            lo, hi = self.job_cols(name)
            self.need(dve, self.job_act, g, *act_counts)
            if name[0] == "Q" and self.norm:
                last = dve.scalar_tensor_tensor(self.target(name, b, 1), c.bank(7), self.qw[:, 0:1],
                                                self.target(name, b, 0), ALU.mult, ALU.subtract)
            else:
                n, parts = {"K": (hi - lo, HD), "Q": (BANK, HD), "V": ((hi - lo) * HD, P)}[name[0]]
                last = dve.tensor_tensor(self.target(name, b, 1), c.bank(7, n, parts), self.target(name, b, 0),
                                         ALU.subtract)
        last.then_inc(self.job_dve, 1)

    def dve_turned(self, dve, g, s, i):
        U = self.UNITS
        if self.has(g, U, s - 1):
            q, h = (s - 1) // 4, (s - 1) % 4
            m = (s - 1) * self.TILES + i
            self.need(dve, self.pT_hi, g, U * self.TILES, m + 1)
            blocks = slice(i * self.PER, (i + 1) * self.PER)
            dve.tensor_tensor(self.pT[q % 2][1][:, blocks, h * P:(h + 1) * P],
                              self.c.bank(4, self.PER * P).rearrange("p (k q) -> p k q", q=P),
                              self.pT[q % 2][0][:, blocks, h * P:(h + 1) * P],
                              ALU.subtract).then_inc(self.pT_lo, 1)

    def dve_slot(self, dve, g, s, live):
        c, U, HD = self.c, self.UNITS, self.HD
        if live:
            b, t, h = s // 8, s % 8 // 4, s % 4
            lo, hi = self.score_cols(s)
            self.need(dve, self.scored, g, U, s + 1)
            top = self.top[:, s:s + 1]
            if self.mask:
                dve.memset(self.bias[:, s:s + 1], 0.0)
                dve.tensor_tensor_reduce(out=self.E[s % 2][:], in0=c.ps[:, lo:hi], in1=self.mask_sb[:, 2 * b + t, :],
                                         scale=1.0, scalar=-3.0e38, op0=ALU.add, op1=ALU.max,
                                         accum_out=top).then_inc(self.max_done, 1)
            else:
                dve.reduce_max(top, c.ps[:, lo:hi], AX.X).then_inc(self.max_done, 1)
            self.need(dve, self.max_done, g, U, s + 1)
            by = self.q_scale_neg[b][:, h * 2 + t:h * 2 + t + 1] if self.norm else \
                (-1.0 if self.mask else -float(HD) ** -0.5)
            dve.tensor_scalar(self.bias[:, s:s + 1], top, by, None, ALU.mult).then_inc(self.bias_done, 1)
        if self.norm and s % 8 == 4 and self.slot_jobs(g, s, 1):
            self.dve_job(dve, g, s // 8 + 1, 4, "N", 1)
        for j, name, ahead in self.slot_jobs(g, s, 0):
            self.dve_job(dve, g, ahead, j, name)
        self.dve_turned(dve, g, s, 0)
        if live:
            self.need(dve, self.exp_done, g, U, s + 1)
            dve.reciprocal(self.recip[:, s:s + 1], self.sums[:, s:s + 1]).then_inc(self.recip_done, 1)
            self.need(dve, self.recip_done, g, U, s + 1)
            dve.tensor_scalar(self.E[s % 2][:], self.E[s % 2][:], self.recip[:, s:s + 1], None, ALU.mult)\
               .then_inc(self.prob_done, 1)
        if s % 4 == 0 and self.has(g, 4, s // 4 - 3):
            q = s // 4 - 3
            self.need(dve, self.wo_made, g, U, 4 * (q + 1))
            dve.scalar_tensor_tensor(c.x[:, q % 4, :], c.bank(6), c.gates[:, self.gate:self.gate + 1],
                                     c.x[:, q % 4, :], ALU.mult, ALU.add).then_inc(self.x_done, 1)
        if s % 4 == 0 and self.has(g, 4, s // 4 - 2):
            q = s // 4 - 2
            self.need(dve, self.o_hi, g, 4, q + 1)
            dve.tensor_tensor(self.oT[q % 2][1][0:HD, :], c.bank(5, BANK, HD), self.oT[q % 2][0][0:HD, :],
                              ALU.subtract).then_inc(self.o_lo, 1)
        if self.TILES == 2:
            self.dve_turned(dve, g, s, 1)
        for j, name, ahead in self.slot_jobs(g, s, 1):
            self.dve_job(dve, g, ahead, j, name, 0)


    def pool_split_qkv(self, pool, g, more, part):
        cols = slice(0, 2 * self.HD) if part == 0 else slice(2 * self.HD, self.W)
        self.need(pool, self.qkv_hi, g, 2, 2 * more + part + 1)
        pool.tensor_tensor(self.qkv[1][:, :, cols], self.qkv_raw[:, :, cols], self.qkv[0][:, :, cols],
                           ALU.subtract).then_inc(self.qkv_lo, 1)

    def pool_job(self, pool, g, ahead, j, name):
        b, HD = ahead % 2, self.HD
        if name == "N":
            self.need(pool, self.ms_done, g, 2, ahead + 1)
            pool.tensor_tensor(self.r[:], self.ms[:], self.c.minus_half[:, 0:self.KB + 8], ALU.pow)\
                .then_inc(self.pow_done, 1)
            return
        if not self.by["pool"][j]:
            return
        if name[0] == "R":
            src = self.k_raw[:, slice(*self.job_cols(name))]
            name = "K" + name[1]
        else:
            rots = self.rots
            r = ahead * rots + sum(1 for n, *_ in self.jobs[:j] if n[0] != "V")
            self.need(pool, self.job_dve, g, 2 * self.total["dve"],
                 ahead * self.total["dve"] + self.count("dve", j + 1))
            src = self.rot[r % 2][:]
            pool.tensor_tensor(src, src, self.rot2[r % 2][:], ALU.add).then_inc(self.rot_summed, 1)
        self.need(pool, self.job_act, g, 2 * self.total["act"],
             ahead * self.total["act"] + self.count("act", j + 1))
        pool.tensor_tensor(self.target(name, b, 1), src, self.target(name, b, 0), ALU.subtract)\
            .then_inc(self.job_pool, 1)

    def pool_slot(self, pool, g, s, live):
        for j, name, ahead in self.slot_jobs(g, s, 0):
            self.pool_job(pool, g, ahead, j, name)
        if live and 6 <= s < 6 + GROUP:
            h = s - 6
            self.need(pool, self.wo_hi, g, 4, h + 1)
            pool.tensor_tensor(self.wo[1][0:self.HD, h, :], self.wo_raw[0:self.HD, h, :],
                               self.wo[0][0:self.HD, h, :], ALU.subtract).then_inc(self.wo_lo, 1)
        for j, name, ahead in self.slot_jobs(g, s, 1):
            self.pool_job(pool, g, ahead, j, name)
        if s in (6, 7) and self.slot_jobs(g, 8, 0):
            self.pool_split_qkv(pool, g, 1, s - 6)


    def rounds(self, eng, slot):
        for s in range(self.UNITS):
            slot(eng, 0, s, True)
        with eng.Fori(1, self.G - 1) as g:
            for s in range(self.UNITS):
                slot(eng, g, s, True)
        for s in range(self.UNITS):
            slot(eng, self.G - 1, s, True)
        for s in range(self.LAST):
            slot(eng, self.G, s, False)

    def run(self, w_qkv, w_o, extra):
        c, HD, ln = self.c, self.HD, self.ln
        with ExitStack() as st:
            sb = lambda name, shape, dt=F32: c.sb(f"{self.tag}_{name}", shape, dt, st)
            pair = lambda name, shape: [sb(f"{name}_{p}", shape, BF16) for p in ("hi", "lo")]
            self.qkv_raw, self.qkv = sb("qkv_raw", [P, DC, self.W]), pair("qkv", [P, DC, self.W])
            self.wo_raw, self.wo = sb("wo_raw", [P, GROUP, D]), pair("wo", [P, GROUP, D])
            self.kT = [pair(f"kT{b}", [P, self.NK]) for b in range(NB)]
            self.qT = [pair(f"qT{b}", [P, GROUP, SQ]) for b in range(NB)]
            self.v = [pair(f"v{b}", [P, self.KB, HD]) for b in range(NB)]
            self.E = [sb(f"probs{i}", [P, self.NK]) for i in range(2)]
            self.pT = [pair(f"pT{i}", [P, self.KB, GROUP * P]) for i in range(2)]
            self.oT = [pair(f"oT{i}", [P, GROUP * P]) for i in range(2)]
            self.top, self.bias, self.sums, self.recip = (
                sb(n, [P, self.UNITS]) for n in ("score_max", "exp_bias", "exp_sums", "exp_recip"))
            loads = []
            if self.norm:
                self.k_sq, self.q_sq = sb("k_sq", [P, self.NK]), sb("q_sq", [P, GROUP * SQ])
                self.k_raw, self.r_diag = sb("k_raw", [P, self.NK]), sb("r_diag", [P, self.KB, P])
                self.ms, self.r = sb("mean_sq", [P, self.KB + 8]), sb("inv_rms", [P, self.KB + 8])
                self.q_scale = [sb(f"q_scale{b}", [P, 8]) for b in range(NB)]
                self.q_scale_neg = [sb(f"q_scale_neg{b}", [P, 8]) for b in range(NB)]
                self.qw, self.kw = sb("q_norm_w", [P, 1]), sb("k_norm_w", [P, 1])
                loads = [(self.qw, "qw"), (self.kw, "kw")]
            if self.rope:
                self.rot, self.rot2 = ([sb(f"{n}{i}", [P, BANK]) for i in range(2)] for n in ("rot", "rot_swap"))
                self.k_cos, self.k_sin, self.q_cos, self.q_sin = (
                    sb(n, [P, BANK]) for n in ("k_cos", "k_sin", "q_cos", "q_sin"))
                loads = [(self.k_cos, "k_cos"), (self.k_sin, "k_sin"), (self.q_cos, "q_cos"), (self.q_sin, "q_sin")]
            if self.mask:
                self.mask_sb = sb("mask", [P, NT, self.NK])
                loads.append((self.mask_sb, "mask"))
            WQKV, WO = DC * self.W, GROUP * D
            with c.nc.Block() as block:

                @block.sync
                def _(sp):
                    def load_qkv(at, n):
                        sp.dma_start(self.qkv_raw[:].rearrange("p d n -> p (d n)"), w_qkv[:, at])\
                          .then_inc(self.qkv_loaded, 16)

                    def load_wo(at):
                        sp.dma_start(self.wo_raw[0:HD].rearrange("p h n -> p (h n)"), w_o[:, at])\
                          .then_inc(self.wo_loaded, 16)

                    load_qkv(slice(0, WQKV), 0)
                    for dst, name in loads:
                        sp.dma_start(dst[:], extra[name]).then_inc(self.extra_loaded, 16)
                    self.need(sp, self.qkv_lo, 0, 0, 2)
                    load_qkv(slice(WQKV, 2 * WQKV), 1)
                    load_wo(slice(0, WO))
                    with sp.Fori(1, self.G - 1) as g:
                        self.need(sp, self.qkv_lo, g, 2, 2)
                        load_qkv(bass.ds(g * WQKV + WQKV, WQKV), g)
                        self.need(sp, self.wo_lo, g, 4, 0)
                        load_wo(bass.ds(g * WO, WO))
                    self.need(sp, self.wo_lo, self.G - 1, 4, 0)
                    load_wo(slice((self.G - 1) * WO, self.G * WO))

                @block.gpsimd
                def _(pool):
                    ln.gpsimd(pool)
                    for part in range(2):
                        self.pool_split_qkv(pool, 0, 0, part)
                    for j, (name, *_) in enumerate(self.jobs):
                        self.pool_job(pool, 0, 0, j, name)
                    self.rounds(pool, self.pool_slot)

                @block.scalar
                def _(act):
                    for part in range(2):
                        self.act_split_qkv(act, 0, 0, part)
                    ln.scalar_hi(act)
                    if loads:
                        self.need(act, self.extra_loaded, 0, 0, 16 * len(loads))
                    for j, (name, *_) in enumerate(self.jobs):
                        self.act_job(act, 0, 0, j, name)
                    self.rounds(act, self.act_slot)

                @block.vector
                def _(dve):
                    ln.vector_norm(dve)
                    ln.vector_lo(dve)
                    if loads:
                        self.need(dve, self.extra_loaded, 0, 0, 16 * len(loads))
                    for j, (name, *_) in enumerate(self.jobs):
                        self.dve_job(dve, 0, 0, j, name, 0)
                        if name == "N":
                            self.dve_job(dve, 0, 0, j, name, 1)
                    self.rounds(dve, self.dve_slot)

                @block.tensor
                def _(pe):
                    ln.tensor_turn(pe)
                    ln.wait_parts(pe)
                    for j, (name, *_) in enumerate(self.jobs):
                        self.pe_job(pe, 0, 0, j, name)
                    self.rounds(pe, self.pe_slot)


class Pieces:

    def __init__(self, core, tag, st):
        self.c, self.tag, self.st, self.items = core, tag, st, []
        self.hi_done, self.lo_done = core.sem(f"{tag}_w_hi"), core.sem(f"{tag}_w_lo")

    def add(self, name, shape):
        raw = self.c.sb(f"{self.tag}_{name}_raw", shape, F32, self.st)
        hi, lo = (self.c.sb(f"{self.tag}_{name}_{p}", shape, BF16, self.st) for p in ("hi", "lo"))
        self.items.append((raw, hi, lo, self.c.sem(f"{self.tag}_{name}_loaded")))
        return raw, [hi, lo]

    def load(self, sp, i, src):
        sp.dma_start(self.items[i][0][:], src).then_inc(self.items[i][3], 16)

    def scalar_hi(self, act, i):
        raw, hi, _, loaded = self.items[i]
        act.wait_ge(loaded, 16)
        act.activation(hi[:], raw[:], ACT.Copy).then_inc(self.hi_done, 1)

    def gpsimd_lo(self, pool, i):
        raw, hi, lo, _ = self.items[i]
        pool.wait_ge(self.hi_done, i + 1)
        pool.tensor_tensor(lo[:], raw[:], hi[:], ALU.subtract).then_inc(self.lo_done, 1)

    def wait(self, pe, i):
        pe.wait_ge(self.hi_done, i + 1)
        pe.wait_ge(self.lo_done, i + 1)


def lora_experts(nc, core, a):
    c, E, R, K = core, 8, 64, 128
    ln = LayerNorm(c, 1)
    S = lambda n: c.sem(f"l0f_{n}")
    small, mean_done, chain_sem, q_done, q_rep, score_done, bias_done, exp_done, coef_done = (S(n) for n in (
        "small_loaded", "mean_done", "chain", "q_done", "q_repeated", "scores_done", "bias_done", "exp_done",
        "coef_done"))
    h_done, h_scaled, h_hi, h_lo, out_done, x_done = (S(n) for n in (
        "h_done", "h_scaled", "h_hi", "h_lo", "out_done", "x_done"))
    with ExitStack() as st:
        w = Pieces(c, "l0f", st)
        _, down = w.add("down", [P, DC, E * R])
        _, worg = w.add("worg", [P, DC, D])
        _, up = w.add("up", [P, E * R // P, D])
        sb = lambda name, shape, dt=F32: c.sb(f"l0f_{name}", shape, dt, st)
        wq, keys = sb("wq", [P, DC, K]), sb("keys", [K, E])
        xm, q_all, coef = sb("x_mean", [P, DC, NB]), sb("q_all", [K, NB, P]), sb("coef", [P, NB, E])
        top, bias, sums, rec = (sb(n, [P, NB]) for n in ("top", "bias", "sums", "recip"))
        rowc = sb("row_coef", [P, NB, E * R // P])
        hf = sb("h_float", [P, E * R // P, TOK])
        hT = [sb(f"h_{p}", [P, E * R // P, TOK], BF16) for p in ("hi", "lo")]
        M = E * R // P
        with nc.Block() as block:

            @block.sync
            def _(sp):
                w.load(sp, 0, a["l0_down"])
                sp.dma_start(wq[:], a["l0_wq"]).then_inc(small, 16)
                sp.dma_start(keys[:], a["l0_keys"]).then_inc(small, 16)
                w.load(sp, 1, a["l0_worg"])
                w.load(sp, 2, a["l0_up"])

            @block.gpsimd
            def _(pool):
                ln.gpsimd(pool)
                for i in range(3):
                    w.gpsimd_lo(pool, i)
                for m in range(M):
                    pool.wait_ge(h_hi, m + 1)
                    pool.tensor_tensor(hT[1][:, m, :], hf[:, m, :], hT[0][:, m, :], ALU.subtract).then_inc(h_lo, 1)

            @block.scalar
            def _(act):
                w.scalar_hi(act, 0)
                ln.scalar_hi(act)
                for i in (1, 2):
                    w.scalar_hi(act, i)
                for b in range(NB):
                    act.wait_ge(bias_done, 1)
                    act.activation(coef[:, b, :], c.bank(5, E, at=b * E), ACT.Exp, bias=bias[:, b:b + 1],
                                   scale=float(K) ** -0.5, accum_out=sums[:, b:b + 1]).then_inc(exp_done, 1)
                for m in range(M):
                    act.wait_ge(h_scaled, m + 1)
                    act.activation(hT[0][:, m, :], hf[:, m, :], ACT.Copy).then_inc(h_hi, 1)

            @block.vector
            def _(dve):
                link = Chain(dve, chain_sem)
                ln.vector_norm(dve)
                ln.vector_lo(dve)
                for d in range(DC):
                    dve.reduce_sum(xm[:, d, :], c.bank(d).rearrange("p (b s) -> p b s", b=NB), AX.X)\
                       .then_inc(mean_done, 1)
                dve.wait_ge(q_done, 1)
                for b in range(NB):
                    dve.tensor_scalar(q_all[:, b, :], c.bank(4, 1, at=b).to_broadcast([K, P]), 1.0 / SQ, None,
                                      ALU.mult).then_inc(q_rep, 1)
                dve.wait_ge(score_done, 1)
                link(dve.reduce_max(top[:], c.bank(5, NB * E).rearrange("p (b e) -> p b e", b=NB), AX.X))
                dve.tensor_scalar(bias[:], top[:], -float(K) ** -0.5, None, ALU.mult).then_inc(bias_done, 1)
                dve.wait_ge(exp_done, NB)
                link(dve.reciprocal(rec[:], sums[:]))
                link(dve.tensor_tensor(coef[:], coef[:], rec[:].unsqueeze(2).to_broadcast([P, NB, E]), ALU.mult))
                dve.tensor_copy(rowc[0:R], coef[0:R, :, 0:E:2]).then_inc(coef_done, 1)
                dve.tensor_copy(rowc[R:P], coef[R:P, :, 1:E:2]).then_inc(coef_done, 1)
                dve.wait_ge(coef_done, 2)
                for m in range(M):
                    dve.wait_ge(h_done, m + 1)
                    for b in range(NB):
                        last = dve.tensor_scalar(hf[:, m, b * SQ:(b + 1) * SQ], c.bank(m, SQ, at=b * SQ),
                                                 rowc[:, b, m:m + 1], None, ALU.mult)
                    last.then_inc(h_scaled, 1)
                for t in range(NT):
                    dve.wait_ge(out_done, t + 1)
                    dve.scalar_tensor_tensor(c.x[:, t, :], c.bank(4 + t), c.gates[:, 1:2], c.x[:, t, :],
                                             ALU.mult, ALU.add).then_inc(x_done, 1)

            @block.tensor
            def _(pe):
                ln.tensor_turn(pe)
                ln.wait_parts(pe)
                pe.wait_ge(mean_done, DC)
                pe.wait_ge(small, 32)
                for d in range(DC):
                    last = pe.matmul(c.bank(4, NB), wq[:, d, :], xm[:, d, :], start=d == 0, stop=d == DC - 1)
                last.then_inc(q_done, 1)
                w.wait(pe, 0)
                for m in range(M):
                    for d in range(DC):
                        last = three(pe, c.bank(m), [v[:, d, m * P:(m + 1) * P] for v in down],
                                     [v[:, d, :] for v in c.xT], d == 0, d == DC - 1)
                    last.then_inc(h_done, 1)
                    if m == 0:
                        pe.wait_ge(q_rep, NB)
                        for b in range(NB):
                            last = pe.matmul(c.bank(5, E, at=b * E), q_all[:, b, :], keys[:], start=True, stop=True)
                        last.then_inc(score_done, 1)
                pe.wait_ge(coef_done, 2)
                w.wait(pe, 1)
                for t in range(NT):
                    for d in range(DC):
                        three(pe, c.bank(4 + t), [v[:, d, t * P:(t + 1) * P] for v in c.xT],
                              [v[:, d, :] for v in worg], d == 0, False)
                w.wait(pe, 2)
                pe.wait_ge(h_lo, M)
                for t in range(NT):
                    for m in range(M):
                        last = three(pe, c.bank(4 + t), [v[:, m, t * P:(t + 1) * P] for v in hT],
                                     [v[:, m, :] for v in up], False, m == M - 1)
                    last.then_inc(out_done, 1)


def sparse_rows(nc, core, a):
    c, F, SP_, RANK = core, 1792, 32, 16
    BL, M = F // SP_, F // P
    ln = LayerNorm(c, 3)
    S = lambda n: c.sem(f"l1f_{n}")
    small, zeroed, xf_done, u_done, u_saved, inter_done, chain_sem, eq_done, key_done, mask_done = (S(n) for n in (
        "small_loaded", "zeroed", "x_float_done", "u_done", "u_saved", "inter_done", "chain", "eq_done",
        "key_done", "mask_done"))
    mT_done, mT_saved, h_done, h_masked, h_hi, h_lo, out_used, out_done, x_done = (S(n) for n in (
        "mask_turned", "mask_T_saved", "h_done", "h_masked", "h_hi", "h_lo", "out_used", "out_done", "x_done"))
    with ExitStack() as st:
        w = Pieces(c, "l1f", st)
        sb = lambda name, shape, dt=F32: c.sb(f"l1f_{name}", shape, dt, st)
        w1 = [w.add(f"w1_{d}", [P, F])[1] for d in range(DC)]
        w2 = [w.add(f"w2_{i}", [P, M // 2, D])[1] for i in range(2)]
        c1, c2 = sb("c1", [P, DC, P]), sb("c2", [P, F])
        u = sb("u", [P, TOK])
        mx, eq, key = sb("block_max", [P, BL]), sb("at_max", [P, BL, SP_], BF16), sb("key", [P, BL, SP_], BF16)
        key_max, rev = sb("key_max", [P, BL], BF16), sb("place_value", [P, SP_])
        mask = sb("chosen", [P, NT, F], BF16)
        ident16 = sb("identity_bf16", [P, P], BF16)
        mT = [sb(f"chosen_T{i}", [P, TOK], BF16) for i in range(2)]
        hf = [sb(f"h_float{i}", [P, TOK]) for i in range(2)]
        hT = [[sb(f"h{i}_{p}", [P, TOK], BF16) for p in ("hi", "lo")] for i in range(2)]
        inter = c.ps[:, 0:F].rearrange("p (n s) -> p n s", s=SP_)
        with nc.Block() as block:

            @block.sync
            def _(sp):
                sp.wait_ge(zeroed, 2)
                sp.dma_start(c1[:, :, 0:RANK], a["l1_c1"]).then_inc(small, 16)
                sp.dma_start(c2[0:RANK, :], a["l1_c2"]).then_inc(small, 16)
                sp.dma_start(rev[:], a["place_value"]).then_inc(small, 16)
                for d in range(DC):
                    w.load(sp, d, a["l1_w1"][:, d, :])
                for i in range(2):
                    w.load(sp, DC + i, a["l1_w2"][:, i * M // 2:(i + 1) * M // 2, :])

            @block.gpsimd
            def _(pool):
                pool.memset(c1[:], 0.0).then_inc(zeroed, 1)
                pool.memset(c2[:], 0.0).then_inc(zeroed, 1)
                pool.tensor_copy(ident16[:], c.ident[:]).then_inc(zeroed, 1)
                ln.gpsimd(pool)
                for i in range(DC + 2):
                    w.gpsimd_lo(pool, i)
                for m in range(M):
                    pool.wait_ge(h_hi, m + 1)
                    pool.tensor_tensor(hT[m % 2][1][:], hf[m % 2][:], hT[m % 2][0][:], ALU.subtract).then_inc(h_lo, 1)

            @block.scalar
            def _(act):
                ln.scalar_hi(act)
                for d in range(DC):
                    ln.wait_lo(act, d + 1)
                    act.activation(c.xn[:, d, :], c.bank(d), ACT.Copy).then_inc(xf_done, 1)
                act.wait_ge(u_done, 1)
                act.activation(u[:], c.bank(4), ACT.Copy).then_inc(u_saved, 1)
                for i in range(DC + 2):
                    w.scalar_hi(act, i)
                for m in range(M):
                    act.wait_ge(mT_done, m + 1)
                    if m >= 2:
                        act.wait_ge(h_masked, m - 1)
                    act.activation(mT[m % 2][:], c.bank(2 + m % 2), ACT.Copy).then_inc(mT_saved, 1)
                    act.wait_ge(h_masked, m + 1)
                    if m >= 2:
                        act.wait_ge(out_used, m - 1)
                    act.activation(hT[m % 2][0][:], hf[m % 2][:], ACT.Copy).then_inc(h_hi, 1)

            @block.vector
            def _(dve):
                link = Chain(dve, chain_sem)
                ln.vector_norm(dve)
                ln.vector_lo(dve)
                dve.wait_ge(small, 48)
                for t in range(NT):
                    dve.wait_ge(inter_done, t + 1)
                    link(dve.reduce_max(mx[:], inter, AX.X))
                    dve.tensor_tensor(eq[:], inter, mx[:].unsqueeze(2).to_broadcast([P, BL, SP_]),
                                      ALU.is_equal).then_inc(eq_done, 1)
                    dve.wait_ge(eq_done, t + 1)
                    link(dve.tensor_tensor(key[:], eq[:], rev[:].unsqueeze(1).to_broadcast([P, BL, SP_]), ALU.mult))
                    link(dve.reduce_max(key_max[:], key[:], AX.X))
                    dve.tensor_tensor(mask[:, t, :].rearrange("p (n s) -> p n s", s=SP_), key[:],
                                      key_max[:].unsqueeze(2).to_broadcast([P, BL, SP_]), ALU.is_equal)\
                       .then_inc(mask_done, 1)
                for m in range(M):
                    dve.wait_ge(h_done, m + 1)
                    dve.wait_ge(mT_saved, m + 1)
                    if m >= 2:
                        dve.wait_ge(h_lo, m - 1)
                    dve.scalar_tensor_tensor(hf[m % 2][:], c.bank(m % 2), 0.0, mT[m % 2][:], ALU.max, ALU.mult)\
                       .then_inc(h_masked, 1)
                for t in range(NT):
                    dve.wait_ge(out_done, t + 1)
                    dve.scalar_tensor_tensor(c.x[:, t, :], c.bank(4 + t), c.gates[:, 3:4], c.x[:, t, :],
                                             ALU.mult, ALU.add).then_inc(x_done, 1)

            @block.tensor
            def _(pe):
                ln.tensor_turn(pe)
                pe.wait_ge(small, 48)
                for d in range(DC):
                    pe.wait_ge(xf_done, d + 1)
                    last = pe.matmul(c.bank(4), c1[:, d, :], c.xn[:, d, :], start=d == 0, stop=d == DC - 1)
                last.then_inc(u_done, 1)
                pe.wait_ge(u_saved, 1)
                for t in range(NT):
                    if t:
                        pe.wait_ge(eq_done, t)
                    for n in range(0, F, BANK):
                        last = pe.matmul(c.ps[:, n:min(n + BANK, F)], u[:, t * P:(t + 1) * P],
                                         c2[:, n:min(n + BANK, F)], start=True, stop=True)
                    last.then_inc(inter_done, 1)
                pe.wait_ge(eq_done, NT)
                pe.wait_ge(zeroed, 3)
                w.wait(pe, DC + 1)

                def add_out(m):
                    pe.wait_ge(h_lo, m + 1)
                    for t in range(NT):
                        last = three(pe, c.bank(4 + t), [v[:, t * P:(t + 1) * P] for v in hT[m % 2]],
                                     [v[:, m % (M // 2), :] for v in w2[m // (M // 2)]], m == 0, m == M - 1)
                        if m == M - 1:
                            last.then_inc(out_done, 1)
                    if m < M - 1:
                        last.then_inc(out_used, 1)

                for m in range(M):
                    if m >= 2:
                        pe.wait_ge(mT_saved, m - 1)
                    for t in range(NT):
                        if m == 0:
                            pe.wait_ge(mask_done, t + 1)
                        last = pe.matmul(c.bank(2 + m % 2, P, at=t * P), mask[:, t, m * P:(m + 1) * P], ident16[:],
                                         start=True, stop=True)
                    last.then_inc(mT_done, 1)
                    if m >= 2:
                        pe.wait_ge(h_masked, m - 1)
                    for d in range(DC):
                        last = three(pe, c.bank(m % 2), [v[:, m * P:(m + 1) * P] for v in w1[d]],
                                     [v[:, d, :] for v in c.xT], d == 0, d == DC - 1)
                    last.then_inc(h_done, 1)
                    if m:
                        add_out(m - 1)
                add_out(M - 1)


def gated_lora(nc, core, a):
    c, E, R = core, 4, 8
    G = E * R + E
    ln = LayerNorm(c, 5)
    S = lambda n: c.sem(f"l2f_{n}")
    small, zeroed, ga_done, chain_sem, sub_done, exp_done, gp_done, gp_turned, gp_hi, gp_lo, out_done, x_done = (
        S(n) for n in ("small_loaded", "zeroed", "proj_done", "chain", "sub_done", "exp_done", "mix_done",
                       "mix_turned", "mix_hi", "mix_lo", "out_done", "x_done"))
    with ExitStack() as st:
        w = Pieces(c, "l2f", st)
        _, ar = w.add("a_wr", [P, DC, G])
        _, wt = w.add("w", [P, DC, D])
        bm_raw, bm = w.add("bm", [P, D])
        sb = lambda name, shape, dt=F32: c.sb(f"l2f_{name}", shape, dt, st)
        bias = sb("bias", [P, D])
        top, sums = sb("top", [P, NT]), sb("sums", [P, NT])
        e = sb("gate", [P, NT, E])
        gp = sb("mix", [P, NT, P])
        gpT = [sb(f"mix_T_{p}", [P, TOK], BF16) for p in ("hi", "lo")]
        tmp = sb("out", [P, NT, D])
        ga = c.bank(4, NT * G).rearrange("p (t g) -> p t g", t=NT)
        with nc.Block() as block:

            @block.sync
            def _(sp):
                w.load(sp, 0, a["l2_awr"])
                w.load(sp, 1, a["l2_w"])
                sp.wait_ge(zeroed, 2)
                sp.dma_start(bm_raw[0:E * R, :], a["l2_bm"]).then_inc(w.items[2][3], 16)
                sp.dma_start(bias[:], a["l2_b"]).then_inc(small, 16)

            @block.gpsimd
            def _(pool):
                pool.memset(gp[:], 0.0).then_inc(zeroed, 1)
                pool.memset(bm_raw[:], 0.0).then_inc(zeroed, 1)
                ln.gpsimd(pool)
                for i in range(3):
                    w.gpsimd_lo(pool, i)

            @block.scalar
            def _(act):
                w.scalar_hi(act, 0)
                ln.scalar_hi(act)
                for i in (1, 2):
                    w.scalar_hi(act, i)
                act.wait_ge(sub_done, 1)
                act.activation(e[:], e[:], ACT.Exp).then_inc(exp_done, 1)
                act.wait_ge(gp_turned, 1)
                act.activation(gpT[0][:], c.bank(5), ACT.Copy).then_inc(gp_hi, 1)

            @block.vector
            def _(dve):
                link = Chain(dve, chain_sem)
                each = lambda v, n: v[:].unsqueeze(2).to_broadcast([P, NT, n])
                ln.vector_norm(dve)
                ln.vector_lo(dve)
                dve.wait_ge(ga_done, 1)
                link(dve.reduce_max(top[:], ga[:, :, E * R:], AX.X))
                dve.tensor_tensor(e[:], ga[:, :, E * R:], each(top, E), ALU.subtract).then_inc(sub_done, 1)
                dve.wait_ge(exp_done, 1)
                link(dve.reduce_sum(sums[:], e[:], AX.X))
                link(dve.reciprocal(sums[:], sums[:]))
                link(dve.tensor_scalar(sums[:], sums[:], 2.0, None, ALU.mult))
                link(dve.tensor_tensor(e[:], e[:], each(sums, E), ALU.mult))
                dve.wait_ge(zeroed, 1)
                for t in range(NT):
                    dve.tensor_tensor(gp[:, t, 0:E * R].rearrange("p (e r) -> p e r", e=E),
                                      ga[:, t, 0:E * R].rearrange("p (e r) -> p e r", e=E),
                                      e[:, t, :].unsqueeze(2).to_broadcast([P, E, R]), ALU.mult).then_inc(gp_done, 1)
                dve.wait_ge(gp_hi, 1)
                dve.tensor_tensor(gpT[1][:], c.bank(5), gpT[0][:], ALU.subtract).then_inc(gp_lo, 1)
                dve.wait_ge(small, 16)
                for t in range(NT):
                    dve.wait_ge(out_done, t + 1)
                    link(dve.tensor_tensor(tmp[:, t, :], c.bank(t), bias[:], ALU.add))
                    dve.scalar_tensor_tensor(c.x[:, t, :], tmp[:, t, :], c.gates[:, 5:6], c.x[:, t, :],
                                             ALU.mult, ALU.add).then_inc(x_done, 1)

            @block.tensor
            def _(pe):
                ln.tensor_turn(pe)
                ln.wait_parts(pe)
                w.wait(pe, 0)
                for t in range(NT):
                    for d in range(DC):
                        last = three(pe, c.bank(4, G, at=t * G), [v[:, d, t * P:(t + 1) * P] for v in c.xT],
                                     [v[:, d, :] for v in ar], d == 0, d == DC - 1)
                last.then_inc(ga_done, 1)
                w.wait(pe, 1)
                for t in range(NT):
                    for d in range(DC):
                        three(pe, c.bank(t), [v[:, d, t * P:(t + 1) * P] for v in c.xT],
                              [v[:, d, :] for v in wt], d == 0, False)
                pe.wait_ge(gp_done, NT)
                for t in range(NT):
                    last = pe.transpose(c.bank(5, P, at=t * P), gp[:, t, :], c.ident[:])
                last.then_inc(gp_turned, 1)
                w.wait(pe, 2)
                pe.wait_ge(gp_lo, 1)
                for t in range(NT):
                    last = three(pe, c.bank(t), [v[:, t * P:(t + 1) * P] for v in gpT], [v[:] for v in bm],
                                 False, True)
                    last.then_inc(out_done, 1)


def routed_experts(nc, core, a):
    c, E, M = core, 3, D // P
    VIS = int(SQ * 0.3)
    ln = LayerNorm(c, 7)
    S = lambda n: c.sem(f"l3f_{n}")
    small, sel_done, abs_done, tot_done, gate_made, chain_sem, sub_done, exp_done, pick_done, pick_rep, coef_done = (
        S(n) for n in ("small_loaded", "row0_done", "abs_done", "totals_done", "gate_made", "chain", "sub_done",
                       "exp_done", "picks_done", "picks_repeated", "coef_done"))
    pre_done, act_done, a_hi, a_lo, out_done, x_done = (
        S(n) for n in ("pre_done", "act_done", "act_hi", "act_lo", "out_done", "x_done"))
    with ExitStack() as st:
        w = Pieces(c, "l3f", st)
        w1, w2 = [], []
        for e in range(E):
            w1.append(w.add(f"w1_{e}", [P, DC, D])[1])
            w2.append(w.add(f"w2_{e}", [P, M, D])[1])
        _, gw = w.add("gate_w", [P, DC, E])
        order = [0, 2, 1, 4, 3, 5]
        sb = lambda name, shape, dt=F32: c.sb(f"l3f_{name}", shape, dt, st)
        b1, b2 = sb("b1", [P, E, M]), sb("b2", [P, E, D])
        gw_last, gb, place = sb("gate_w_last", [P, E]), sb("gate_b", [P, E]), sb("place_value", [P, E])
        row0, junk = sb("row0", [P, P]), sb("junk", [P, SQ])
        absum, tot = sb("abs_sums", [P, DC, 4]), sb("abs_totals", [P, 4])
        ratio, gb2 = sb("ratio", [P, NB]), sb("gate_const", [P, NB, E])
        s, key, s2 = sb("scores", [P, NT, E]), sb("key", [P, NT, E]), sb("scores2", [P, NT, E])
        picks = sb("picks", [P, 2, NT, E])
        pick0 = sb("picks_of_token0", [P, 2, NB, E])
        v1, v2, t4, u4 = (sb(n, [P, NT]) for n in ("value1", "value2", "t4", "u4"))
        coef, coef2 = sb("coef", [P, NT, E]), sb("coef2", [P, NT, E])
        af = [sb(f"act_float{i}", [P, TOK]) for i in range(2)]
        aT = [[sb(f"act{i}_{p}", [P, M, TOK], BF16) for p in ("hi", "lo")] for i in range(2)]
        tmp = [sb(f"out{i}", [P, D]) for i in range(2)]
        with nc.Block() as block:

            @block.sync
            def _(sp):
                w.load(sp, 6, a["l3_gate_w"])
                for dst, name in ((b1, "l3_b1"), (b2, "l3_b2"), (gw_last, "l3_gate_w_last"), (gb, "l3_gate_b"),
                                  (place, "place3")):
                    sp.dma_start(dst[:], a[name]).then_inc(small, 16)
                for i in order:
                    w.load(sp, i, a["l3_w1" if i % 2 == 0 else "l3_w2"][:, i // 2])

            @block.gpsimd
            def _(pool):
                pool.memset(row0[:], 0.0).then_inc(sel_done, 1)
                pool.wait_ge(sel_done, 1)
                pool.memset(row0[0:1, :], 1.0).then_inc(sel_done, 1)
                ln.gpsimd(pool)
                for n, i in enumerate([6] + order):
                    raw, hi, lo, _ = w.items[i]
                    pool.wait_ge(w.hi_done, n + 1)
                    pool.tensor_tensor(lo[:], raw[:], hi[:], ALU.subtract).then_inc(w.lo_done, 1)
                for n in range(E * M):
                    e, m = n // M, n % M
                    pool.wait_ge(a_hi, n + 1)
                    pool.tensor_tensor(aT[e % 2][1][:, m, :], af[n % 2][:], aT[e % 2][0][:, m, :], ALU.subtract)\
                        .then_inc(a_lo, 1)

            @block.scalar
            def _(act):
                w.scalar_hi(act, 6)
                ln.scalar_hi(act)
                for d in range(DC):
                    ln.wait_lo(act, d + 1)
                    for b in range(NB):
                        for k, (lo, hi) in enumerate(((0, VIS), (VIS, SQ))):
                            n = 2 * b + k
                            act.wait_ge(abs_done, 4 * d + n) if 4 * d + n else None
                            act.activation(junk[:, 0:hi - lo], c.bank(d, hi - lo, at=b * SQ + lo), ACT.Abs,
                                           accum_out=absum[:, d, n:n + 1]).then_inc(abs_done, 1)
                for i in order[:1]:
                    w.scalar_hi(act, i)
                act.wait_ge(sub_done, 1)
                act.activation(s[:], s[:], ACT.Exp).then_inc(exp_done, 1)
                for i in order[1:]:
                    w.scalar_hi(act, i)
                act.wait_ge(small, 80)
                for n in range(E * M):
                    e, m = n // M, n % M
                    act.wait_ge(pre_done, n + 1)
                    if n >= 2:
                        act.wait_ge(a_lo, n - 1)
                    act.activation(af[n % 2][:], c.bank(m), (ACT.Tanh, ACT.Gelu, ACT.Silu)[e],
                                   bias=b1[:, e, m:m + 1]).then_inc(act_done, 1)
                    act.wait_ge(act_done, n + 1)
                    if e == 2:
                        act.wait_ge(out_done, NT)
                    act.activation(aT[e % 2][0][:, m, :], af[n % 2][:], ACT.Copy).then_inc(a_hi, 1)

            @block.vector
            def _(dve):
                link = Chain(dve, chain_sem)
                each = lambda v: v[:].unsqueeze(2).to_broadcast([P, NT, E])
                places = place[:].unsqueeze(1).to_broadcast([P, NT, E])

                def pick(src, value, i):
                    link(dve.reduce_max(value[:], src[:], AX.X))
                    link(dve.tensor_tensor(key[:], src[:], each(value), ALU.is_equal))
                    link(dve.tensor_tensor(key[:], key[:], places, ALU.mult))
                    link(dve.reduce_max(t4[:], key[:], AX.X))
                    link(dve.tensor_tensor(picks[:, i], key[:], each(t4), ALU.is_equal))

                ln.vector_norm(dve)
                ln.vector_lo(dve)
                dve.wait_ge(tot_done, 1)
                dve.wait_ge(small, 80)
                link(dve.reduce_sum(tot[:], c.bank(4, DC * 4).rearrange("p (d n) -> p n d", d=DC), AX.X))
                link(dve.tensor_scalar(ratio[:], tot[:, 0:4:2], 1.0 / (VIS * D), 1e-8, ALU.mult, ALU.add))
                link(dve.reciprocal(ratio[:], ratio[:]))
                link(dve.tensor_scalar(tot[:, 1:4:2], tot[:, 1:4:2], 1.0 / ((SQ - VIS) * D), None, ALU.mult))
                link(dve.tensor_tensor(ratio[:], ratio[:], tot[:, 1:4:2], ALU.mult))
                for b in range(NB):
                    link(dve.scalar_tensor_tensor(gb2[:, b, :], gw_last[:], ratio[:, b:b + 1], gb[:],
                                                  ALU.mult, ALU.add))
                dve.wait_ge(gate_made, 1)
                for b in range(NB):
                    link(dve.tensor_tensor(s[:, 2 * b:2 * b + 2, :],
                                           c.bank(5, 2 * E, at=2 * E * b).rearrange("p (t e) -> p t e", e=E),
                                           gb2[:, b, :].unsqueeze(1).to_broadcast([P, 2, E]), ALU.add))
                link(dve.reduce_max(t4[:], s[:], AX.X))
                dve.tensor_tensor(s[:], s[:], each(t4), ALU.subtract).then_inc(sub_done, 1)
                dve.wait_ge(exp_done, 1)
                link(dve.reduce_sum(t4[:], s[:], AX.X))
                link(dve.reciprocal(t4[:], t4[:]))
                link(dve.tensor_tensor(s[:], s[:], each(t4), ALU.mult))
                pick(s, v1, 0)
                link(dve.scalar_tensor_tensor(s2[:], picks[:, 0], -4.0, s[:], ALU.mult, ALU.add))
                pick(s2, v2, 1)
                link(dve.tensor_tensor(u4[:], v1[:], v2[:], ALU.add))
                link(dve.tensor_scalar(u4[:], u4[:], 1e-8, None, ALU.add))
                link(dve.reciprocal(u4[:], u4[:]))
                link(dve.tensor_scalar(u4[:], u4[:], c.gates[:, 7:8], None, ALU.mult))
                link(dve.tensor_tensor(v1[:], v1[:], u4[:], ALU.mult))
                dve.tensor_tensor(v2[:], v2[:], u4[:], ALU.mult).then_inc(pick_done, 1)
                dve.wait_ge(pick_rep, 1)
                link(dve.tensor_copy(pick0[:], c.bank(6, 2 * NT * E).rearrange(
                    "p (i b t e) -> p i b t e", i=2, b=NB, t=2)[:, :, :, 0, :]))
                for b in range(NB):
                    rows = slice(2 * b, 2 * b + 2)
                    of0 = lambda i: pick0[:, i, b, :].unsqueeze(1).to_broadcast([P, 2, E])
                    w_of = lambda v: v[:, rows].unsqueeze(2).to_broadcast([P, 2, E])
                    link(dve.tensor_tensor(coef[:, rows, :], of0(0), w_of(v1), ALU.mult))
                    link(dve.tensor_tensor(coef2[:, rows, :], of0(1), w_of(v2), ALU.mult))
                dve.tensor_tensor(coef[:], coef[:], coef2[:], ALU.add).then_inc(coef_done, 1)
                dve.wait_ge(coef_done, 1)
                for n in range(E * NT):
                    e, t = n // NT, n % NT
                    dve.wait_ge(out_done, n + 1)
                    link(dve.tensor_tensor(tmp[n % 2][:], c.bank(4 + t), b2[:, e, :], ALU.add))
                    dve.scalar_tensor_tensor(c.x[:, t, :], tmp[n % 2][:], coef[:, t, e:e + 1], c.x[:, t, :],
                                             ALU.mult, ALU.add).then_inc(x_done, 1)

            @block.tensor
            def _(pe):
                def ready(n):
                    pe.wait_ge(w.hi_done, n)
                    pe.wait_ge(w.lo_done, n)

                def up(e):
                    ready(2 + order.index(2 * e))
                    for m in range(M):
                        n = e * M + m
                        if n >= M:
                            pe.wait_ge(act_done, n - M + 1)
                        for d in range(DC):
                            last = three(pe, c.bank(m), [v[:, d, m * P:(m + 1) * P] for v in w1[e]],
                                         [v[:, d, :] for v in c.xT], d == 0, d == DC - 1)
                        last.then_inc(pre_done, 1)

                def down(e):
                    ready(2 + order.index(2 * e + 1))
                    pe.wait_ge(a_lo, (e + 1) * M)
                    for t in range(NT):
                        if e:
                            pe.wait_ge(x_done, (e - 1) * NT + t + 1)
                        for m in range(M):
                            last = three(pe, c.bank(4 + t), [v[:, m, t * P:(t + 1) * P] for v in aT[e % 2]],
                                         [v[:, m, :] for v in w2[e]], m == 0, m == M - 1)
                        last.then_inc(out_done, 1)

                ln.tensor_turn(pe)
                ln.wait_parts(pe)
                ready(1)
                for t in range(NT):
                    for d in range(DC):
                        last = three(pe, c.bank(5, E, at=t * E), [v[:, d, t * P:(t + 1) * P] for v in c.xT],
                                     [v[:, d, :] for v in gw], d == 0, d == DC - 1)
                last.then_inc(gate_made, 1)
                pe.wait_ge(abs_done, 4 * DC)
                pe.matmul(c.bank(4, DC * 4), c.ones[:], absum[:].rearrange("p d n -> p (d n)"),
                          start=True, stop=True).then_inc(tot_done, 1)
                up(0)
                pe.wait_ge(pick_done, 1)
                pe.wait_ge(sel_done, 2)
                pe.matmul(c.bank(6, 2 * NT * E), row0[:], picks[:].rearrange("p i t e -> p (i t e)"),
                          start=True, stop=True).then_inc(pick_rep, 1)
                up(1)
                pe.wait_ge(coef_done, 1)
                down(0)
                up(2)
                down(1)
                down(2)


def store(nc, core, out):
    stored = core.sem("stored")
    with nc.Block() as block:

        @block.sync
        def _(sp):
            sp.dma_start(out, core.x[:]).then_inc(stored, 16)
            sp.wait_ge(stored, 16)


def build(nc, a, out):
    with ExitStack() as ctx:
        core = Core(nc, ctx)
        setup_and_quant_product(nc, core, a)
        lora_experts(nc, core, a)
        Attention(core, "l1x", 2, 8, 128, True, norm=True).run(
            a["l1_qkv"], a["l1_wo"], {"qw": a["l1_qw"], "kw": a["l1_kw"]})
        sparse_rows(nc, core, a)
        Attention(core, "l2x", 4, 8, 128, False, rope=True, mask=True).run(
            a["l2_qkv"], a["l2_wo"], {n: a[n] for n in ("k_cos", "k_sin", "q_cos", "q_sin", "mask")})
        gated_lora(nc, core, a)
        Attention(core, "l3x", 6, 4, 96, True).run(a["l3_qkv"], a["l3_wo"], {})
        routed_experts(nc, core, a)
        store(nc, core, out)


def columns(w):
    k, n = w.shape
    return w.reshape(k // P, P, n).transpose(1, 0, 2)


def heads_together(wk, wv, wq, hd):
    rounds = wk.shape[1] // hd
    parts = [w.reshape(DC, P, rounds, -1) for w in (wk, wv, wq)]
    return np.concatenate(parts, 3).transpose(1, 2, 0, 3).reshape(P, -1)


def heads_out(wo, hd):
    return wo.reshape(-1, hd, D).transpose(1, 0, 2).reshape(hd, -1)


def rotation_tables(hd):
    inv = (1.0 / 10000.0 ** (np.arange(0, hd, 2, dtype=np.float32) / np.float32(hd))).astype(np.float32)
    ang = (np.arange(SC, dtype=np.float32)[None, :] * inv[:, None]).astype(np.float32)
    cos, sin = np.cos(ang).astype(np.float32), np.sin(ang).astype(np.float32)
    k_cos, k_sin = np.concatenate([cos, cos]), np.concatenate([sin, -sin])
    scale = np.float32(hd) ** np.float32(-0.5)
    q_cos, q_sin = (np.tile(w[:, :SQ] * scale, (1, 2)).astype(np.float32) for w in (k_cos, k_sin))
    return {"k_cos": k_cos, "k_sin": k_sin, "q_cos": q_cos, "q_sin": q_sin}


def lay_out(v):
    rows = lambda w: np.broadcast_to(w, (P, *w.shape))
    d = {
        "x": v["x"].reshape(NT, P, D).transpose(1, 0, 2),
        "context": v["ctx_4096"].reshape(-1, P, D).transpose(1, 0, 2),
        "context_T": columns(v["ctx_4096"].reshape(-1, D).T),
        "gates": rows(np.stack([v["g_xattn"], v["g_ffn"]], 1).reshape(8)),
        "quant": rows(np.concatenate([v["L0_xattn_x1_scale"], v["L0_xattn_x1_zp"],
                                      v["L0_xattn_x2_scale"], v["L0_xattn_x2_zp"]])),
    }
    d["l1_qkv"] = heads_together(v["L1_xattn_Wk"], v["L1_xattn_Wv"], v["L1_xattn_Wq"], 128)
    d["l1_wo"] = heads_out(v["L1_xattn_Wo"], 128)
    d["l1_qw"], d["l1_kw"] = v["L1_xattn_q_norm_w"][:, None], v["L1_xattn_k_norm_w"][:, None]
    d["l2_qkv"] = heads_together(v["L2_xattn_wk"], v["L2_xattn_wv"], v["L2_xattn_wq"], 128)
    d["l2_wo"] = heads_out(v["L2_xattn_wo"], 128)
    d.update(rotation_tables(128))
    d["mask"] = v["mask_BxSxS2_ff0"].reshape(NT, P, SC).transpose(1, 0, 2)
    d["l3_qkv"] = heads_together(v["L3_xattn_Wk"].T, v["L3_xattn_Wv"].T, v["L3_xattn_Wq"].T, 96)
    d["l3_wo"] = heads_out(v["L3_xattn_Wo"].T, 96)
    d["l0_down"] = columns(v["L0_ffn_lora_down"].transpose(1, 0, 2).reshape(D, -1))
    d["l0_up"] = columns(v["L0_ffn_lora_up"].reshape(-1, D))
    d["l0_worg"], d["l0_wq"] = columns(v["L0_ffn_W_org"].T), columns(v["L0_ffn_Wq"].T)
    d["l0_keys"] = v["L0_ffn_lora_keys"].T
    d["l1_c1"], d["l1_c2"] = columns(v["L1_ffn_c1_w"].T), v["L1_ffn_c2_w"].T
    d["l1_w1"], d["l1_w2"] = columns(v["L1_ffn_w1"].T), columns(v["L1_ffn_w2t"])
    d["place_value"] = rows(np.arange(32, 0, -1, dtype=np.float32))
    d["l2_awr"] = np.concatenate([columns(v["L2_ffn_A"].reshape(-1, D).T), columns(v["L2_ffn_Wr"].T)], 2)
    d["l2_w"], d["l2_b"] = columns(v["L2_ffn_W"].T), rows(v["L2_ffn_b"])
    d["l2_bm"] = v["L2_ffn_Bm"].transpose(0, 2, 1).reshape(-1, D)
    per_expert = lambda w: w.reshape(3, DC, P, D).transpose(2, 0, 1, 3)
    d["l3_w1"], d["l3_w2"] = per_expert(v["L3_ffn_w1"]), per_expert(v["L3_ffn_w2"])
    d["l3_b1"] = v["L3_ffn_b1"].reshape(3, DC, P).transpose(2, 0, 1)
    d["l3_b2"] = rows(v["L3_ffn_b2"])
    d["l3_gate_w"], d["l3_gate_w_last"] = columns(v["L3_ffn_gate_w"][:D]), rows(v["L3_ffn_gate_w"][D])
    d["l3_gate_b"] = rows(v["L3_ffn_gate_b"])
    d["place3"] = rows(np.arange(3, 0, -1, dtype=np.float32))
    return {k: np.ascontiguousarray(w) for k, w in d.items()}


def kernel(**inputs):
    import concourse.bacc as bacc
    from concourse.bass_utils import run_bass_kernel_spmd as run

    nc = bacc.Bacc("TRN2", target_bir_lowering=False, num_devices=1)
    arrays = lay_out({k: np.asarray(w) for k, w in inputs.items()})
    a = {k: nc.dram_tensor(k + "_dram", w.shape, mybir.dt.from_np(w.dtype), kind="ExternalInput").ap()
         for k, w in arrays.items()}
    out = nc.dram_tensor("out_dram", (P, NT, D), F32, kind="ExternalOutput").ap()
    build(nc, a, out)
    r = run(nc, [{k + "_dram": w for k, w in arrays.items()}], core_ids=[0])
    return r.results[0]["out_dram"].transpose(1, 0, 2).reshape(NB, SQ, D)
```

```python
from contextlib import ExitStack

import numpy as np

import concourse.bass as bass
from concourse import mybir

F32 = mybir.dt.float32
BF16 = mybir.dt.bfloat16
ALU = mybir.AluOpType
ACT = mybir.ActivationFunctionType
AX = mybir.AxisListType

P = 128
D = 512
DC = D // P
NB = 2
SQ = 256
TOK = NB * SQ
NT = TOK // P
SC = 512
BANK = 512
GROUP = 4
ROUND = 12582912.0


def three(pe, out, lhs, rhs, first, last):
    (lh, ll), (rh, rl) = lhs, rhs
    pe.matmul(out, lh, rh, start=first, stop=False)
    pe.matmul(out, lh, rl, start=False, stop=False)
    return pe.matmul(out, ll, rh, start=False, stop=last)


class Chain:

    def __init__(self, eng, sem):
        self.eng, self.sem, self.n = eng, sem, 0

    def __call__(self, ins):
        self.n += 1
        ins.then_inc(self.sem, 1)
        self.eng.wait_ge(self.sem, self.n)


class Core:

    def __init__(self, nc, ctx):
        self.nc, self.ctx = nc, ctx
        self.norms = self.turns = 0
        self.attention_sems = {}
        self.ps = ctx.enter_context(nc.psum_tensor("psum", [P, 8 * BANK], F32))
        self.x = self.sb("x_state", [P, NT, D])
        self.xn = self.sb("x_normed", [P, NT, D])
        self.xT = [self.sb(f"x_normed_T_{part}", [P, DC, TOK], BF16) for part in ("hi", "lo")]
        self.ctxT = [self.sb(f"context_T_{part}", [P, DC, NB * SC], BF16) for part in ("hi", "lo")]
        self.ident = self.sb("identity", [P, P])
        self.ones = self.sb("ones", [P, P])
        self.ident16 = self.sb("identity_bf16", [P, P], BF16)
        self.ones16 = self.sb("ones_bf16", [P, P], BF16)
        self.minus_half = self.sb("minus_half", [P, 16])
        self.gates = self.sb("gates", [P, 8])
        self.stats = self.sb("ln_stats", [P, NT, 6])
        self.meanvar = self.sb("ln_meanvar", [P, NT, 2])
        self.var_eps = self.sb("ln_var_eps", [P, NT])
        self.rstd = self.sb("ln_rstd", [P, NT])

    def sb(self, name, shape, dt=F32, ctx=None):
        return (ctx or self.ctx).enter_context(self.nc.sbuf_tensor(name, shape, dt))

    def sem(self, name):
        return self.ctx.enter_context(self.nc.semaphore(name))

    def bank(self, b, n=BANK, parts=P, at=0):
        return self.ps[0:parts, b * BANK + at:b * BANK + at + n]


class LayerNorm:

    def __init__(self, core, turn=True):
        self.c, self.n, self.turns = core, core.norms, core.turns
        core.norms, core.turns = core.norms + 1, core.turns + turn
        if self.n == 0:
            core.ln_sems = [core.sem(f"ln_{s}") for s in (
                "stats_done", "rstd_done", "normed", "turned", "hi_done", "lo_done")]
        self.stats_done, self.rstd_done, self.normed, self.turned, self.hi_done, self.lo_done = core.ln_sems

    def wait_stats(self, eng, k):
        eng.wait_ge(self.stats_done, 2 * NT * self.n + k)

    def wait_rstd(self, eng, k):
        eng.wait_ge(self.rstd_done, 2 * self.n + k)

    def wait_normed(self, eng, k):
        eng.wait_ge(self.normed, NT * self.n + k)

    def wait_turned(self, eng, k):
        eng.wait_ge(self.turned, DC * self.turns + k)

    def wait_hi(self, eng, k):
        eng.wait_ge(self.hi_done, DC * self.turns + k)

    def wait_lo(self, eng, k):
        eng.wait_ge(self.lo_done, DC * self.turns + k)

    def vector_norm(self, dve):
        c = self.c
        for t in range(NT):
            dve.bn_stats(c.stats[:, t, :], c.x[:, t, :]).then_inc(self.stats_done, 1)
        for t in range(NT):
            self.wait_stats(dve, t + 1)
            dve.bn_aggr(c.meanvar[:, t, :], c.stats[:, t, :]).then_inc(self.stats_done, 1)
        self.wait_stats(dve, 2 * NT)
        self.wait_rstd(dve, 2)
        for t in range(NT):
            dve.tensor_scalar(c.xn[:, t, :], c.x[:, t, :], c.meanvar[:, t, 0:1], c.rstd[:, t:t + 1],
                              ALU.subtract, ALU.mult).then_inc(self.normed, 1)

    def gpsimd(self, pool):
        c = self.c
        self.wait_stats(pool, 2 * NT)
        pool.tensor_scalar(c.var_eps[:], c.meanvar[:, :, 1], 1e-5, None, ALU.add).then_inc(self.rstd_done, 1)
        self.wait_rstd(pool, 1)
        pool.tensor_tensor(c.rstd[:], c.var_eps[:], c.minus_half[:, 0:NT], ALU.pow).then_inc(self.rstd_done, 1)

    def tensor_turn(self, pe):
        c = self.c
        for d in range(DC):
            for t in range(NT):
                if d == 0:
                    self.wait_normed(pe, t + 1)
                last = pe.transpose(c.bank(d, P, at=t * P), c.xn[:, t, d * P:(d + 1) * P], c.ident[:])
            last.then_inc(self.turned, 1)

    def scalar_hi(self, act):
        c = self.c
        for d in range(DC):
            self.wait_turned(act, d + 1)
            act.activation(c.xT[0][:, d, :], c.bank(d), ACT.Copy).then_inc(self.hi_done, 1)

    def vector_lo(self, dve):
        c = self.c
        for d in range(DC):
            self.wait_hi(dve, d + 1)
            dve.tensor_tensor(c.xT[1][:, d, :], c.bank(d), c.xT[0][:, d, :], ALU.subtract)\
               .then_inc(self.lo_done, 1)

    def wait_parts(self, eng):
        self.wait_hi(eng, DC)
        self.wait_lo(eng, DC)


def setup_and_quant_product(nc, core, a):
    c = core
    KT = SC // P
    ln = LayerNorm(c, turn=False)
    loaded_x, loaded_small, loaded_ctx, loaded_ctxT = (c.sem(n) for n in (
        "loaded_x", "loaded_small", "loaded_ctx", "loaded_ctxT"))
    ident_steps, gates_done, ctxT_hi, ctxT_lo = (c.sem(n) for n in (
        "ident_steps", "gates_done", "ctxT_hi_done", "ctxT_lo_done"))
    scal_done, q_chain, q1_done, q1_turned, q1T_done = (c.sem(n) for n in (
        "quant_scalars_done", "quant_chain", "q1_done", "q1_turned", "q1T_done"))
    q2_done, colsum_done, colsum_saved, prod_done, x_done = (c.sem(n) for n in (
        "q2_done", "colsum_done", "colsum_saved", "prod_done", "l0x_x_done"))
    with ExitStack() as st:
        ctx_nat = c.sb("context_rows", [P, NB * KT, D], ctx=st)
        ctxT_raw = c.sb("context_T_raw", [P, DC, NB * SC], ctx=st)
        q1 = c.sb("q1", [P, NT, D], BF16, st)
        q2 = c.sb("q2", [P, NB * KT, D], BF16, st)
        q1T = c.sb("q1_T", [P, DC, TOK], BF16, st)
        q1f = c.sb("q1_float", [P, D], F32, st)
        q2f = c.sb("q2_float", [P, NB * KT, D], F32, st)
        qs = c.sb("quant_scalars_in", [P, 4], F32, st)
        inv = c.sb("quant_inverse_scales", [P, 2], F32, st)
        cz = c.sb("quant_centres", [P, 2], F32, st)
        kcc = c.sb("quant_constant_term", [P, 1], F32, st)
        gss = c.sb("quant_out_scale", [P, 1], F32, st)
        rs = c.sb("q1_row_sums", [P, NT], F32, st)
        rs2 = c.sb("q1_row_terms", [P, NT], F32, st)
        csb = c.sb("q2_column_terms", [P, NB, D], F32, st)
        tmp = c.sb("l0x_sum", [P, NT, D], F32, st)
        gin = c.sb("gates_in", [P, 8], F32, st)
        with nc.Block() as block:

            @block.sync
            def _(sp):
                sp.dma_start(c.x[:], a["x"]).then_inc(loaded_x, 16)
                sp.dma_start(gin[:], a["gates"]).then_inc(loaded_small, 16)
                sp.dma_start(qs[:], a["quant"]).then_inc(loaded_small, 16)
                sp.dma_start(ctx_nat[:], a["context"]).then_inc(loaded_ctx, 16)
                sp.dma_start(ctxT_raw[:], a["context_T"]).then_inc(loaded_ctxT, 16)

            @block.gpsimd
            def _(pool):
                pool.memset(c.ident[:], 0.0).then_inc(ident_steps, 1)
                pool.memset(c.ones[:], 1.0).then_inc(ident_steps, 1)
                pool.memset(c.ones16[:], 1.0).then_inc(ident_steps, 1)
                pool.memset(c.minus_half[:], -0.5).then_inc(ident_steps, 1)
                pool.wait_ge(ident_steps, 1)
                pool.affine_select(out=c.ident[:], in_=c.ident[:], compare_op=ALU.not_equal, fill=1.0,
                                   base=0, pattern=[[-1, P]], channel_multiplier=1).then_inc(ident_steps, 1)
                pool.wait_ge(ident_steps, 5)
                pool.tensor_copy(c.ident16[:], c.ident[:]).then_inc(ident_steps, 1)
                ln.gpsimd(pool)
                for d in range(DC):
                    pool.wait_ge(ctxT_hi, d + 1)
                    pool.tensor_tensor(c.ctxT[1][:, d, :], ctxT_raw[:, d, :], c.ctxT[0][:, d, :],
                                       ALU.subtract).then_inc(ctxT_lo, 1)

            @block.scalar
            def _(act):
                act.wait_ge(loaded_small, 32)
                act.activation(c.gates[:], gin[:], ACT.Tanh).then_inc(gates_done, 1)
                for d in range(DC):
                    if d == 0:
                        act.wait_ge(loaded_ctxT, 16)
                    act.activation(c.ctxT[0][:, d, :], ctxT_raw[:, d, :], ACT.Copy).then_inc(ctxT_hi, 1)
                for d in range(DC):
                    act.wait_ge(q1_turned, d + 1)
                    act.activation(q1T[:, d, :], c.bank(d), ACT.Copy).then_inc(q1T_done, 1)

            @block.vector
            def _(dve):
                link = Chain(dve, q_chain)
                dve.wait_ge(loaded_x, 16)
                ln.vector_norm(dve)
                dve.wait_ge(loaded_small, 32)
                link(dve.reciprocal(inv[:], qs[:, 0:4:2]))
                link(dve.tensor_scalar(cz[:], qs[:, 1:4:2], -1.0, 128.0, ALU.mult, ALU.add))
                link(dve.tensor_scalar(kcc[:], cz[:, 0:1], cz[:, 1:2], float(SC), ALU.mult, ALU.mult))
                dve.wait_ge(gates_done, 1)
                link(dve.tensor_scalar(gss[:], qs[:, 0:1], qs[:, 2:3], c.gates[:, 0:1], ALU.mult, ALU.mult))
                for t in range(NT):
                    ln.wait_normed(dve, t + 1)
                    link(dve.tensor_scalar(q1f[:], c.xn[:, t, :], inv[:, 0:1], qs[:, 1:2], ALU.mult, ALU.add))
                    link(dve.tensor_scalar(q1f[:], q1f[:], ROUND, -ROUND, ALU.add, ALU.add))
                    link(dve.tensor_scalar(q1f[:], q1f[:], 0.0, 255.0, ALU.max, ALU.min))
                    dve.tensor_scalar(q1[:, t, :], q1f[:], -128.0, 0.0, ALU.add, ALU.add,
                                      accum_out=rs[:, t:t + 1]).then_inc(q1_done, 1)
                    dve.wait_ge(q1_done, t + 1)
                    link(dve.tensor_scalar(rs2[:, t:t + 1], rs[:, t:t + 1], cz[:, 1:2], None, ALU.mult))
                dve.wait_ge(loaded_ctx, 16)
                for k in range(NB * KT):
                    v = q2f[:, k, :]
                    link(dve.tensor_scalar(v, ctx_nat[:, k, :], inv[:, 1:2], qs[:, 3:4], ALU.mult, ALU.add))
                    link(dve.tensor_scalar(v, v, ROUND, -ROUND, ALU.add, ALU.add))
                    link(dve.tensor_scalar(v, v, 0.0, 255.0, ALU.max, ALU.min))
                    dve.tensor_scalar(q2[:, k, :], v, -128.0, None, ALU.add).then_inc(q2_done, 1)
                for b in range(NB):
                    dve.wait_ge(colsum_done, b + 1)
                    dve.tensor_scalar(csb[:, b, :], c.bank(4 + b), cz[:, 0:1], kcc[:, 0:1],
                                      ALU.mult, ALU.add).then_inc(colsum_saved, 1)
                dve.wait_ge(colsum_saved, NB)
                for t in range(NT):
                    dve.wait_ge(prod_done, t + 1)
                    link(dve.scalar_tensor_tensor(tmp[:, t, :], c.bank(t), rs2[:, t:t + 1],
                                                  csb[:, t // 2, :], ALU.add, ALU.add))
                    dve.scalar_tensor_tensor(c.x[:, t, :], tmp[:, t, :], gss[:, 0:1], c.x[:, t, :],
                                             ALU.mult, ALU.add).then_inc(x_done, 1)

            @block.tensor
            def _(pe):
                pe.wait_ge(ident_steps, 6)
                for d in range(DC):
                    for t in range(NT):
                        if d == 0:
                            pe.wait_ge(q1_done, t + 1)
                        last = pe.matmul(c.bank(d, P, at=t * P), q1[:, t, d * P:(d + 1) * P], c.ident16[:],
                                         start=True, stop=True)
                    last.then_inc(q1_turned, 1)
                for b in range(NB):
                    for k in range(KT):
                        pe.wait_ge(q2_done, b * KT + k + 1)
                        last = pe.matmul(c.bank(4 + b), c.ones16[:], q2[:, b * KT + k, :],
                                         start=k == 0, stop=k == KT - 1)
                    last.then_inc(colsum_done, 1)
                pe.wait_ge(q1T_done, DC)
                for t in range(NT):
                    for k in range(KT):
                        last = pe.matmul(c.bank(t), q1T[:, k, t * P:(t + 1) * P], q2[:, (t // 2) * KT + k, :],
                                         start=k == 0, stop=k == KT - 1)
                    last.then_inc(prod_done, 1)


class Attention:

    UNITS = 16
    LAG = 2
    PV = LAG + 4
    WO = PV + 4
    LAST = WO + 15 - UNITS

    def __init__(self, core, tag, gate, heads, hd, latents, norm=False, rope=False, mask=False):
        self.c, self.tag, self.gate, self.G, self.HD = core, tag, gate, heads, hd
        self.norm, self.rope, self.mask = norm, rope, mask
        self.NK = SC + (SQ if latents else 0)
        self.KB = self.NK // P
        self.TILES = -(-self.NK // BANK)
        self.PER = self.KB // self.TILES
        self.W = (2 + GROUP) * hd
        if norm:
            self.jobs = [("K0", 0, 0), ("Q0", 1, 0), ("K1", 2, 0), ("Q1", 3, 0), ("N", 4, 0), ("R0", 5, 0),
                         ("R1", 5, 1), ("V0", 6, 0), ("V1", 7, 0)]
        elif rope:
            self.jobs = [("K0", 0, 0), ("Q0", 2, 0), ("Q1", 4, 0), ("V0", 6, 0)]
        else:
            self.jobs = [("K0", 0, 0), ("Q0", 1, 0), ("K1", 2, 0), ("Q1", 3, 0), ("V0", 6, 0), ("V1", 7, 0)]
        names = self.names = [j[0] for j in self.jobs]
        self.by = {"act": [n != "N" for n in names], "dve": [True for n in names],
                   "pool": [(norm and n[0] in "KQR") or (rope and n[0] != "V") for n in names]}
        self.total = {e: sum(v) for e, v in self.by.items()}
        self.ln = LayerNorm(core)
        J, T, G = len(self.jobs), self.TILES, self.G
        self.rots = sum(1 for n in names if n[0] != "V") if rope else 0
        signals = {
            "qkv_loaded": 16 * G, "wo_loaded": 16 * G, "extra_loaded": 16 * (2 * norm + 4 * rope + mask),
            "qkv_hi": 3 * G, "qkv_lo": 3 * G, "wo_hi": 4 * G, "wo_lo": 4 * G,
            "job_made": 2 * G * J, "job_act": 2 * G * self.total["act"], "job_dve": 2 * G * self.total["dve"],
            "job_pool": 2 * G * self.total["pool"], "ms_done": 4 * G * norm, "pow_done": 2 * G * norm,
            "rot_summed": 2 * G * self.rots, "scored": 16 * G, "max_done": 16 * G, "bias_done": 16 * G,
            "exp_done": 16 * G, "recip_done": 16 * G, "prob_done": 16 * G, "turned": 16 * G * T,
            "pT_hi": 16 * G * T, "pT_lo": 16 * G * T, "pv_done": 4 * G, "o_hi": 4 * G, "o_lo": 4 * G,
            "wo_made": 8 * G, "x_done": 8 * G}
        self.before, found = {}, []
        for n, per_layer in signals.items():
            sem, before = core.attention_sems.get(n) or (core.sem(f"attn_{n}"), 0)
            self.before[sem.name] = before
            core.attention_sems[n] = (sem, before + per_layer)
            found.append(sem)
        (self.qkv_loaded, self.wo_loaded, self.extra_loaded, self.qkv_hi, self.qkv_lo, self.wo_hi, self.wo_lo,
         self.job_made, self.job_act, self.job_dve, self.job_pool, self.ms_done, self.pow_done, self.rot_summed,
         self.scored, self.max_done, self.bias_done, self.exp_done, self.recip_done, self.prob_done, self.turned,
         self.pT_hi, self.pT_lo, self.pv_done, self.o_hi, self.o_lo, self.wo_made, self.x_done) = found

    def need(self, eng, sem, g, per, more):
        if isinstance(g, int):
            if per * g + more > 0:
                eng.wait_ge(sem, self.before[sem.name] + per * g + more)
        else:
            assert per + more > 0
            eng.wait_ge(sem, g * per + (more + self.before[sem.name]))


    def has(self, g, per, more):
        return not isinstance(g, int) or 0 <= per * g + more < per * self.G

    def score_cols(self, s):
        at = (s % 2) * 2 * BANK
        return at, at + self.NK

    def count(self, engine, j):
        return sum(self.by[engine][:j])

    def slot_jobs(self, g, s, after):
        half = s // 8
        if isinstance(g, int) and (g >= self.G or (g == self.G - 1 and half == 1)):
            return []
        return [(j, n, half + 1) for j, (n, at, late) in enumerate(self.jobs) if at == s % 8 and late == after]

    def job_cols(self, name):
        return {"K0": (0, SC), "K1": (SC, self.NK), "Q0": (0, 2), "Q1": (2, 4), "R0": (0, SC),
                "R1": (SC, self.NK), "V0": (0, SC // P), "V1": (SC // P, self.KB)}[name]


    def bank7_before(self, g, s, place):
        shift = 0
        while True:
            place -= 1
            if place < 0:
                s, place = s - 1, 2
            if s < 0:
                s, shift = s + self.UNITS, shift - 1
            at = g + shift if isinstance(g, int) else g
            if isinstance(g, int) and at < 0:
                return "job", len(self.jobs) - 1, 0
            if place == 1:
                n = (s - self.WO) // 2
                if s % 2 == 0 and self.has(at, 8, n):
                    return "wo", 8 * shift + n
            else:
                jobs = self.slot_jobs(at, s, place // 2)
                if jobs:
                    return "job", jobs[-1][0], jobs[-1][2] + 2 * shift

    def wait_bank7(self, pe, g, last):
        if last[0] == "wo":
            self.need(pe, self.x_done, g, 8, last[1] + 1)
            return
        j, ahead = last[1:]
        if self.names[j] == "N":
            self.need(pe, self.ms_done, g, 4, 2 * ahead + 1)
            return
        self.need(pe, self.job_dve, g, 2 * self.total["dve"],
                  ahead * self.total["dve"] + self.count("dve", j + 1))
        name = self.jobs[j][0]
        if name[0] in "KQV" and not (self.rope and name[0] != "V"):
            self.need(pe, self.job_act, g, 2 * self.total["act"],
                      ahead * self.total["act"] + self.count("act", j + 1))

    def pe_job(self, pe, g, ahead, j, name, last7):
        c, b = self.c, ahead % 2
        HD = self.HD
        if last7:
            self.wait_bank7(pe, g, last7)
        if name[0] in "KVQ":
            part = 3 * (ahead // 2) + 1 + "KQV".index(name[0])
            self.need(pe, self.qkv_hi, g, 3, part)
            self.need(pe, self.qkv_lo, g, 3, part)
        if name[0] == "R":
            self.need(pe, self.job_dve, g, 2 * self.total["dve"],
                      ahead * self.total["dve"] + self.count("dve", self.names.index("N") + 1))
        wk, wv, wq = ([w[:, :, i * HD:n * HD] for w in self.qkv] for i, n in ((0, 1), (1, 2), (2, 6)))
        if name[0] == "K":
            lo, hi = self.job_cols(name)
            src = c.ctxT if name == "K0" else c.xT
            base = b * SC if name == "K0" else b * SQ
            for d in range(DC):
                last = three(pe, c.bank(7, hi - lo, HD), [w[:, d, :] for w in wk],
                             [x[:, d, base:base + hi - lo] for x in src], d == 0, d == DC - 1)
        elif name[0] == "Q":
            for i, h in enumerate(range(*self.job_cols(name))):
                for d in range(DC):
                    last = three(pe, c.bank(7, SQ, HD, at=i * SQ), [w[:, d, h * HD:(h + 1) * HD] for w in wq],
                                 [x[:, d, b * SQ:(b + 1) * SQ] for x in c.xT], d == 0, d == DC - 1)
        elif name[0] == "V":
            for i, k in enumerate(range(*self.job_cols(name))):
                src = c.ctxT if name == "V0" else c.xT
                at = b * SC + k * P if name == "V0" else b * SQ + i * P
                for d in range(DC):
                    last = three(pe, c.bank(7, HD, at=i * HD), [x[:, d, at:at + P] for x in src],
                                 [w[:, d, :] for w in wv], d == 0, d == DC - 1)
        elif name == "N":
            for sem, e in ((self.job_act, "act"), (self.job_pool, "pool")):
                self.need(pe, sem, g, 2 * self.total[e], ahead * self.total[e] + self.count(e, j))
            for i in range(self.KB + 8):
                sq, at = (self.k_sq, i) if i < self.KB else (self.q_sq, i - self.KB)
                for part in (1, 2):
                    last = pe.matmul(c.bank(7, 1, at=i), sq[part][:, at * P:(at + 1) * P], c.ones16[:, 0:1],
                                     start=part == 1, stop=part == 2)
        else:
            lo, hi = self.job_cols(name)
            for i, k in enumerate(range(lo // P, hi // P)):
                for part in range(2):
                    last = pe.matmul(c.bank(7, P, at=i * P), self.r_parts[part][:, k:k + 1].to_broadcast([P, P]),
                                     c.ident16[:], start=part == 0, stop=part == 1)
        last.then_inc(self.job_made, 1)

    def pe_turn(self, pe, g, s, i):
        c, U, u = self.c, self.UNITS, s - self.LAG
        if self.has(g, U, u):
            if i == 0:
                self.need(pe, self.prob_done, g, U, u + 1)
            m = u * self.TILES + i
            self.need(pe, self.pT_hi, g, U * self.TILES, m - 1)
            self.need(pe, self.pT_lo, g, U * self.TILES, m - 1)
            for k in range(self.PER):
                kb = i * self.PER + k
                last = pe.transpose(c.bank(4 + m % 2, P, at=k * P), self.E[u % 4][:, kb * P:(kb + 1) * P], c.ident[:])
            last.then_inc(self.turned, 1)

    def pe_slot(self, pe, g, s, live):
        c, U = self.c, self.UNITS
        HD = self.HD
        if live:
            b, t, h = s // 8, s % 8 // 4, s % 4
            if s % 8 == 0:
                for sem, e in ((self.job_act, "act"), (self.job_dve, "dve"), (self.job_pool, "pool")):
                    if self.total[e]:
                        self.need(pe, sem, g, 2 * self.total[e], (b + 1) * self.total[e])
            self.need(pe, self.max_done if self.mask else self.exp_done, g, U, s - 1)
            lo, hi = self.score_cols(s)
            q = [w[0:HD, h, t * P:(t + 1) * P] for w in self.qT[b]]
            cuts = [lo] + [m for m in (BANK, 3 * BANK) if lo < m < hi] + [hi]
            for u, v in zip(cuts, cuts[1:]):
                last = three(pe, c.ps[:, u:v], q, [w[0:HD, u - lo:v - lo] for w in self.kT[b]], True, True)
            last.then_inc(self.scored, 1)
        for j, name, ahead in self.slot_jobs(g, s, 0):
            self.pe_job(pe, g, ahead, j, name, self.bank7_before(g, s, 0))
        self.pe_turn(pe, g, s, 0)
        q, piece = (s - self.PV) // 4, (s - self.PV) % 4
        if self.has(g, 4, q):
            if piece == 0:
                for sem in (self.pT_hi, self.pT_lo):
                    self.need(pe, sem, g, U * self.TILES, 4 * (q + 1) * self.TILES)
                self.need(pe, self.o_hi, g, 4, q)
                self.need(pe, self.o_lo, g, 4, q)
            v, pT = self.v[q % 4 // 2], self.pT[q % 2]
            steps = [(k, x, y) for k in range(self.KB) for x, y in ((0, 0), (0, 1), (1, 0))]
            for i in range(piece * len(steps) // 4, (piece + 1) * len(steps) // 4):
                k, x, y = steps[i]
                last = pe.matmul(c.bank(6, BANK, HD), v[x][:, k, :], pT[y][:, k, :],
                                 start=i == 0, stop=i == len(steps) - 1)
            if piece == 3:
                last.then_inc(self.pv_done, 1)
        n = (s - self.WO) // 2
        if s % 2 == 0 and self.has(g, 8, n):
            self.wait_bank7(pe, g, self.bank7_before(g, s, 1))
            if n % 2 == 0:
                self.need(pe, self.o_hi, g, 4, n // 2 + 1)
                self.need(pe, self.o_lo, g, 4, n // 2 + 1)
            if n // 2 % 4 == 0:
                self.need(pe, self.wo_hi, g, 4, 4 * (n // 8) + 2 * (n % 2) + 2)
                self.need(pe, self.wo_lo, g, 4, 4 * (n // 8) + 2 * (n % 2) + 2)
            for h in (2 * (n % 2), 2 * (n % 2) + 1):
                last = three(pe, c.bank(7), [o[0:HD, h * P:(h + 1) * P] for o in self.oT[n // 2 % 2]],
                             [w[0:HD, h, :] for w in self.wo], h % 2 == 0, h % 2 == 1)
            last.then_inc(self.wo_made, 1)
        if self.TILES == 2:
            self.pe_turn(pe, g, s, 1)
        for j, name, ahead in self.slot_jobs(g, s, 1):
            self.pe_job(pe, g, ahead, j, name, self.bank7_before(g, s, 2))


    def piece_cols(self, part):
        HD = self.HD
        return (slice(0, HD), slice(2 * HD, self.W), slice(HD, 2 * HD))[part]

    def split_parts(self, g, s):
        last = isinstance(g, int) and g >= self.G - 1
        return [] if last else {3: [0], 5: [1], 7: [2]}.get(s, [])

    def act_split_qkv(self, act, g, more, part):
        if part == 0:
            self.need(act, self.qkv_loaded, g, 16, 16 * (more + 1))
        if more:
            j = max(i for i, n in enumerate(self.names) if n[0] == "KQV"[part])
            self.need(act, self.job_made, g, 2 * len(self.jobs), len(self.jobs) + j + 1)
        cols = self.piece_cols(part)
        act.activation(self.qkv[0][:, :, cols], self.qkv_raw[:, :, cols], ACT.Copy).then_inc(self.qkv_hi, 1)

    def act_job(self, act, g, ahead, j, name):
        c, b, HD = self.c, ahead % 2, self.HD
        if name == "N":
            return
        if name[0] == "R":
            lo, hi = self.job_cols(name)
            self.need(act, self.job_dve, g, 2 * self.total["dve"],
                 ahead * self.total["dve"] + self.count("dve", j + 1))
            last = act.activation(self.kT[b][0][:, lo:hi], self.k_raw[:, lo:hi], ACT.Copy)
        elif self.rope and name[0] != "V":
            rots = self.rots
            r = ahead * rots + sum(1 for n, *_ in self.jobs[:j] if n[0] != "V")
            self.need(act, self.rot_summed, g, 2 * rots, r + 1)
            last = act.activation(self.target(name, b, 0), self.rot[r % 2][:], ACT.Copy)
        else:
            self.need(act, self.job_made, g, 2 * len(self.jobs), ahead * len(self.jobs) + j + 1)
            if name[0] == "K":
                lo, hi = self.job_cols(name)
                if self.norm:
                    act.activation(self.k_sq[0][:, lo:hi], c.bank(7, hi - lo), ACT.Square)
                    last = act.activation(self.k_sq[1][:, lo:hi], c.bank(7, hi - lo), ACT.Square)
                else:
                    last = act.activation(self.kT[b][0][0:HD, lo:hi], c.bank(7, hi - lo, HD), ACT.Copy)
            elif name[0] == "Q":
                if self.norm:
                    lo, hi = self.job_cols(name)
                    act.activation(self.q_sq[0][:, lo * SQ:hi * SQ], c.bank(7), ACT.Square)
                    act.activation(self.q_sq[1][:, lo * SQ:hi * SQ], c.bank(7), ACT.Square)
                    last = act.activation(self.target(name, b, 0), c.bank(7), ACT.Copy, scale=self.qw[:, 0:1])
                else:
                    last = act.activation(self.target(name, b, 0), c.bank(7, BANK, HD), ACT.Copy)
            else:
                lo, hi = self.job_cols(name)
                last = act.activation(self.target(name, b, 0), c.bank(7, (hi - lo) * HD), ACT.Copy)
        last.then_inc(self.job_act, 1)

    def target(self, name, b, part):
        lo, hi = self.job_cols(name)
        if name[0] == "K":
            return self.kT[b][part][0:self.HD, lo:hi]
        if name[0] == "Q":
            return self.qT[b][part][0:self.HD, lo:hi, :].rearrange("p h q -> p (h q)")
        return self.v[b][part][:, lo:hi, :].rearrange("p k d -> p (k d)")

    def act_turned(self, act, g, s, i):
        U, u = self.UNITS, s - self.LAG
        if self.has(g, U, u):
            q, h = u // 4, u % 4
            m = u * self.TILES + i
            self.need(act, self.turned, g, U * self.TILES, m + 1)
            if h == 0 and i == 0:
                self.need(act, self.pv_done, g, 4, q - 1)
            act.activation(self.pT[q % 2][0][:, i * self.PER:(i + 1) * self.PER, h * P:(h + 1) * P],
                           self.c.bank(4 + m % 2, self.PER * P).rearrange("p (k q) -> p k q", q=P),
                           ACT.Copy).then_inc(self.pT_hi, 1)

    def act_slot(self, act, g, s, live):
        c, U, HD = self.c, self.UNITS, self.HD
        if live:
            b, t, h = s // 8, s % 8 // 4, s % 4
            self.need(act, self.bias_done, g, U, s + 1)
            lo, hi = self.score_cols(s)
            E = self.E[s % 4]
            if self.norm:
                scale = self.q_scale[b][:, h * 2 + t:h * 2 + t + 1]
            else:
                scale = 1.0 if self.mask else float(HD) ** -0.5
            act.activation(E[:], E[:] if self.mask else c.ps[:, lo:hi], ACT.Exp, bias=self.bias[:, s:s + 1],
                           scale=scale, accum_out=self.sums[:, s:s + 1]).then_inc(self.exp_done, 1)
        for j, name, ahead in self.slot_jobs(g, s, 0):
            self.act_job(act, g, ahead, j, name)
        self.act_turned(act, g, s, 0)
        if live and 7 <= s < 7 + GROUP:
            h = s - 7
            if h == 0:
                self.need(act, self.wo_loaded, g, 16, 16)
            if h % 2 == 0:
                self.need(act, self.wo_made, g, 8, h // 2 - 1)
            act.activation(self.wo[0][0:HD, h, :], self.wo_raw[0:HD, h, :], ACT.Copy).then_inc(self.wo_hi, 1)
        q = (s - self.WO + 1) // 4
        if (s - self.WO + 1) % 4 == 0 and self.has(g, 4, q):
            self.need(act, self.pv_done, g, 4, q + 1)
            self.need(act, self.wo_made, g, 8, 2 * (q - 1))
            act.activation(self.oT[q % 2][0][0:HD, :], c.bank(6, BANK, HD), ACT.Copy).then_inc(self.o_hi, 1)
        if self.TILES == 2:
            self.act_turned(act, g, s, 1)
        for j, name, ahead in self.slot_jobs(g, s, 1):
            self.act_job(act, g, ahead, j, name)
        for part in self.split_parts(g, s):
            self.act_split_qkv(act, g, 1, part)


    def dve_job(self, dve, g, ahead, j, name, part=None):
        c, b, HD = self.c, ahead % 2, self.HD
        made = (2 * len(self.jobs), ahead * len(self.jobs) + j + 1)
        act_counts = (2 * self.total["act"], ahead * self.total["act"] + self.count("act", j + 1))
        if name == "N":
            if part == 0:
                self.need(dve, self.job_made, g, *made)
                dve.tensor_scalar(self.ms[:], c.bank(7, self.KB + 8), 1.0 / HD, 1e-6, ALU.mult, ALU.add)\
                   .then_inc(self.ms_done, 1)
                return
            self.need(dve, self.pow_done, g, 2, ahead + 1)
            dve.tensor_copy(self.r_parts[0][:], self.r[:, 0:self.KB]).then_inc(self.ms_done, 1)
            dve.tensor_scalar(self.q_scale[b][:], self.r[:, self.KB:], float(HD) ** -0.5, None, ALU.mult)
            dve.tensor_scalar(self.q_scale_neg[b][:], self.r[:, self.KB:], -float(HD) ** -0.5, None, ALU.mult)
            self.need(dve, self.ms_done, g, 4, 2 * ahead + 2)
            last = dve.tensor_tensor(self.r_parts[1][:], self.r[:, 0:self.KB], self.r_parts[0][:], ALU.subtract)
        elif name[0] == "R":
            lo, hi = self.job_cols(name)
            self.need(dve, self.job_made, g, *made)
            last = dve.tensor_tensor(self.k_raw[:, lo:hi], self.k_raw[:, lo:hi], c.bank(7, hi - lo), ALU.mult)
        elif self.rope and name[0] != "V":
            rots = self.rots
            r = ahead * rots + sum(1 for n, *_ in self.jobs[:j] if n[0] != "V")
            cos, sin = (self.k_cos, self.k_sin) if name[0] == "K" else (self.q_cos, self.q_sin)
            self.need(dve, self.job_made, g, *made)
            self.need(dve, self.job_pool, g, 2 * rots, r - 1)
            H = HD // 2
            dve.tensor_tensor(self.rot[r % 2][:], c.bank(7), cos[:], ALU.mult)
            dve.tensor_tensor(self.rot2[r % 2][0:H, :], c.ps[H:HD, 7 * BANK:8 * BANK], sin[H:HD, :], ALU.mult)
            last = dve.tensor_tensor(self.rot2[r % 2][H:HD, :], c.ps[0:H, 7 * BANK:8 * BANK], sin[0:H, :], ALU.mult)
        elif name[0] == "K" and self.norm:
            lo, hi = self.job_cols(name)
            self.need(dve, self.job_act, g, *act_counts)
            self.need(dve, self.job_pool, g, 2 * self.total["pool"], ahead * self.total["pool"])
            last = dve.tensor_scalar(self.k_raw[:, lo:hi], c.bank(7, hi - lo), self.kw[:, 0:1], None, ALU.mult)
        else:
            lo, hi = self.job_cols(name)
            self.need(dve, self.job_act, g, *act_counts)
            if name[0] == "Q" and self.norm:
                last = dve.scalar_tensor_tensor(self.target(name, b, 1), c.bank(7), self.qw[:, 0:1],
                                                self.target(name, b, 0), ALU.mult, ALU.subtract)
            else:
                n, parts = {"K": (hi - lo, HD), "Q": (BANK, HD), "V": ((hi - lo) * HD, P)}[name[0]]
                last = dve.tensor_tensor(self.target(name, b, 1), c.bank(7, n, parts), self.target(name, b, 0),
                                         ALU.subtract)
        last.then_inc(self.job_dve, 1)

    def dve_turned(self, dve, g, s, i):
        U, u = self.UNITS, s - self.LAG
        if self.has(g, U, u):
            q, h = u // 4, u % 4
            m = u * self.TILES + i
            self.need(dve, self.pT_hi, g, U * self.TILES, m + 1)
            blocks = slice(i * self.PER, (i + 1) * self.PER)
            dve.tensor_tensor(self.pT[q % 2][1][:, blocks, h * P:(h + 1) * P],
                              self.c.bank(4 + m % 2, self.PER * P).rearrange("p (k q) -> p k q", q=P),
                              self.pT[q % 2][0][:, blocks, h * P:(h + 1) * P],
                              ALU.subtract).then_inc(self.pT_lo, 1)

    def dve_slot(self, dve, g, s, live):
        c, U, HD = self.c, self.UNITS, self.HD
        if live:
            b, t, h = s // 8, s % 8 // 4, s % 4
            lo, hi = self.score_cols(s)
            self.need(dve, self.scored, g, U, s + 1)
            top = self.top[:, s:s + 1]
            if self.mask:
                dve.memset(self.bias[:, s:s + 1], 0.0)
                dve.tensor_tensor_reduce(out=self.E[s % 4][:], in0=c.ps[:, lo:hi], in1=self.mask_sb[:, 2 * b + t, :],
                                         scale=1.0, scalar=-3.0e38, op0=ALU.add, op1=ALU.max,
                                         accum_out=top).then_inc(self.max_done, 1)
            else:
                dve.reduce_max(top, c.ps[:, lo:hi], AX.X).then_inc(self.max_done, 1)
            self.need(dve, self.max_done, g, U, s + 1)
            by = self.q_scale_neg[b][:, h * 2 + t:h * 2 + t + 1] if self.norm else \
                (-1.0 if self.mask else -float(HD) ** -0.5)
            dve.tensor_scalar(self.bias[:, s:s + 1], top, by, None, ALU.mult).then_inc(self.bias_done, 1)
        if self.has(g, U, s - 1):
            u = (s - 1) % U
            self.need(dve, self.exp_done, g, U, s)
            dve.reciprocal(self.recip[:, u:u + 1], self.sums[:, u:u + 1]).then_inc(self.recip_done, 1)
            self.need(dve, self.recip_done, g, U, s)
            dve.tensor_scalar(self.E[u % 4][:], self.E[u % 4][:], self.recip[:, u:u + 1], None, ALU.mult)\
               .then_inc(self.prob_done, 1)
        for j, name, ahead in self.slot_jobs(g, s, 0):
            self.dve_job(dve, g, ahead, j, name, 0)
        self.dve_turned(dve, g, s, 0)
        q = (s - self.WO + 1) // 4
        if (s - self.WO + 1) % 4 == 0 and self.has(g, 4, q):
            self.need(dve, self.o_hi, g, 4, q + 1)
            dve.tensor_tensor(self.oT[q % 2][1][0:HD, :], c.bank(6, BANK, HD), self.oT[q % 2][0][0:HD, :],
                              ALU.subtract).then_inc(self.o_lo, 1)
        n = (s - self.WO) // 2
        if s % 2 == 0 and self.has(g, 8, n):
            t = n // 2 % 4
            self.need(dve, self.wo_made, g, 8, n + 1)
            dve.scalar_tensor_tensor(c.x[:, t, :], c.bank(7), c.gates[:, self.gate:self.gate + 1],
                                     c.x[:, t, :], ALU.mult, ALU.add).then_inc(self.x_done, 1)
        if self.TILES == 2:
            self.dve_turned(dve, g, s, 1)
        if self.norm:
            for j, name, ahead in self.slot_jobs(g, s, 0):
                if name == "N":
                    self.dve_job(dve, g, ahead, j, name, 1)
        for j, name, ahead in self.slot_jobs(g, s, 1):
            self.dve_job(dve, g, ahead, j, name, 0)


    def pool_split_qkv(self, pool, g, more, part):
        cols = self.piece_cols(part)
        self.need(pool, self.qkv_hi, g, 3, 3 * more + part + 1)
        pool.tensor_tensor(self.qkv[1][:, :, cols], self.qkv_raw[:, :, cols], self.qkv[0][:, :, cols],
                           ALU.subtract).then_inc(self.qkv_lo, 1)

    def pool_job(self, pool, g, ahead, j, name):
        b, HD = ahead % 2, self.HD
        if name == "N":
            self.need(pool, self.ms_done, g, 4, 2 * ahead + 1)
            pool.tensor_tensor(self.r[:], self.ms[:], self.c.minus_half[:, 0:self.KB + 8], ALU.pow)\
                .then_inc(self.pow_done, 1)
            return
        if not self.by["pool"][j]:
            return
        dst = None
        if name[0] == "R":
            src = self.k_raw[:, slice(*self.job_cols(name))]
            name = "K" + name[1]
        elif self.norm:
            lo, hi = self.job_cols(name)
            sq, cols = (self.k_sq, slice(lo, hi)) if name[0] == "K" else (self.q_sq, slice(lo * SQ, hi * SQ))
            dst, src = (sq[2][:, cols], sq[1][:, cols]), sq[0][:, cols]
        else:
            rots = self.rots
            r = ahead * rots + sum(1 for n, *_ in self.jobs[:j] if n[0] != "V")
            self.need(pool, self.job_dve, g, 2 * self.total["dve"],
                 ahead * self.total["dve"] + self.count("dve", j + 1))
            src = self.rot[r % 2][:]
            pool.tensor_tensor(src, src, self.rot2[r % 2][:], ALU.add).then_inc(self.rot_summed, 1)
        self.need(pool, self.job_act, g, 2 * self.total["act"],
             ahead * self.total["act"] + self.count("act", j + 1))
        low, high = dst or (self.target(name, b, 1), self.target(name, b, 0))
        pool.tensor_tensor(low, src, high, ALU.subtract).then_inc(self.job_pool, 1)

    def pool_slot(self, pool, g, s, live):
        for j, name, ahead in self.slot_jobs(g, s, 0):
            self.pool_job(pool, g, ahead, j, name)
        if live and 7 <= s < 7 + GROUP:
            h = s - 7
            self.need(pool, self.wo_hi, g, 4, h + 1)
            pool.tensor_tensor(self.wo[1][0:self.HD, h, :], self.wo_raw[0:self.HD, h, :],
                               self.wo[0][0:self.HD, h, :], ALU.subtract).then_inc(self.wo_lo, 1)
        for j, name, ahead in self.slot_jobs(g, s, 1):
            self.pool_job(pool, g, ahead, j, name)
        for part in self.split_parts(g, s):
            self.pool_split_qkv(pool, g, 1, part)


    def rounds(self, eng, slot):
        for s in range(self.UNITS):
            slot(eng, 0, s, True)
        with eng.Fori(1, self.G - 1) as g:
            for s in range(self.UNITS):
                slot(eng, g, s, True)
        for s in range(self.UNITS):
            slot(eng, self.G - 1, s, True)
        for s in range(self.LAST):
            slot(eng, self.G, s, False)

    def run(self, w_qkv, w_o, extra):
        c, HD, ln = self.c, self.HD, self.ln
        with ExitStack() as st:
            sb = lambda name, shape, dt=F32: c.sb(f"{self.tag}_{name}", shape, dt, st)
            pair = lambda name, shape: [sb(f"{name}_{p}", shape, BF16) for p in ("hi", "lo")]
            self.qkv_raw, self.qkv = sb("qkv_raw", [P, DC, self.W]), pair("qkv", [P, DC, self.W])
            self.wo_raw, self.wo = sb("wo_raw", [P, GROUP, D]), pair("wo", [P, GROUP, D])
            self.kT = [pair(f"kT{b}", [P, self.NK]) for b in range(NB)]
            self.qT = [pair(f"qT{b}", [P, GROUP, SQ]) for b in range(NB)]
            self.v = [pair(f"v{b}", [P, self.KB, HD]) for b in range(NB)]
            self.E = [sb(f"probs{i}", [P, self.NK]) for i in range(4)]
            self.pT = [pair(f"pT{i}", [P, self.KB, GROUP * P]) for i in range(2)]
            self.oT = [pair(f"oT{i}", [P, GROUP * P]) for i in range(2)]
            self.top, self.bias, self.sums, self.recip = (
                sb(n, [P, self.UNITS]) for n in ("score_max", "exp_bias", "exp_sums", "exp_recip"))
            loads = []
            if self.norm:
                self.k_sq, self.q_sq = ([sb(n, [P, w])] + pair(n, [P, w]) for n, w in (
                    ("k_sq", self.NK), ("q_sq", GROUP * SQ)))
                self.k_raw, self.r_parts = sb("k_raw", [P, self.NK]), pair("inv_rms", [P, self.KB])
                self.ms, self.r = sb("mean_sq", [P, self.KB + 8]), sb("inv_rms", [P, self.KB + 8])
                self.q_scale = [sb(f"q_scale{b}", [P, 8]) for b in range(NB)]
                self.q_scale_neg = [sb(f"q_scale_neg{b}", [P, 8]) for b in range(NB)]
                self.qw, self.kw = sb("q_norm_w", [P, 1]), sb("k_norm_w", [P, 1])
                loads = [(self.qw, "qw"), (self.kw, "kw")]
            if self.rope:
                self.rot, self.rot2 = ([sb(f"{n}{i}", [P, BANK]) for i in range(2)] for n in ("rot", "rot_swap"))
                self.k_cos, self.k_sin, self.q_cos, self.q_sin = (
                    sb(n, [P, BANK]) for n in ("k_cos", "k_sin", "q_cos", "q_sin"))
                loads = [(self.k_cos, "k_cos"), (self.k_sin, "k_sin"), (self.q_cos, "q_cos"), (self.q_sin, "q_sin")]
            if self.mask:
                self.mask_sb = sb("mask", [P, NT, self.NK])
                loads.append((self.mask_sb, "mask"))
            WQKV, WO = DC * self.W, GROUP * D
            with c.nc.Block() as block:

                @block.sync
                def _(sp):
                    def load_qkv(at, n):
                        sp.dma_start(self.qkv_raw[:].rearrange("p d n -> p (d n)"), w_qkv[:, at])\
                          .then_inc(self.qkv_loaded, 16)

                    def load_wo(at):
                        sp.dma_start(self.wo_raw[0:HD].rearrange("p h n -> p (h n)"), w_o[:, at])\
                          .then_inc(self.wo_loaded, 16)

                    load_qkv(slice(0, WQKV), 0)
                    for dst, name in loads:
                        sp.dma_start(dst[:], extra[name]).then_inc(self.extra_loaded, 16)
                    self.need(sp, self.qkv_lo, 0, 0, 3)
                    load_qkv(slice(WQKV, 2 * WQKV), 1)
                    load_wo(slice(0, WO))
                    with sp.Fori(1, self.G - 1) as g:
                        self.need(sp, self.qkv_lo, g, 3, 3)
                        load_qkv(bass.ds(g * WQKV + WQKV, WQKV), g)
                        self.need(sp, self.wo_lo, g, 4, 0)
                        load_wo(bass.ds(g * WO, WO))
                    self.need(sp, self.wo_lo, self.G - 1, 4, 0)
                    load_wo(slice((self.G - 1) * WO, self.G * WO))

                @block.gpsimd
                def _(pool):
                    ln.gpsimd(pool)
                    for part in range(3):
                        self.pool_split_qkv(pool, 0, 0, part)
                    for j, (name, *_) in enumerate(self.jobs):
                        self.pool_job(pool, 0, 0, j, name)
                    self.rounds(pool, self.pool_slot)

                @block.scalar
                def _(act):
                    for part in range(3):
                        self.act_split_qkv(act, 0, 0, part)
                    ln.scalar_hi(act)
                    if loads:
                        self.need(act, self.extra_loaded, 0, 0, 16 * len(loads))
                    for j, (name, *_) in enumerate(self.jobs):
                        self.act_job(act, 0, 0, j, name)
                    self.rounds(act, self.act_slot)

                @block.vector
                def _(dve):
                    ln.vector_norm(dve)
                    ln.vector_lo(dve)
                    if loads:
                        self.need(dve, self.extra_loaded, 0, 0, 16 * len(loads))
                    for j, (name, *_) in enumerate(self.jobs):
                        self.dve_job(dve, 0, 0, j, name, 0)
                        if name == "N":
                            self.dve_job(dve, 0, 0, j, name, 1)
                    self.rounds(dve, self.dve_slot)

                @block.tensor
                def _(pe):
                    ln.tensor_turn(pe)
                    ln.wait_parts(pe)
                    for j, (name, *_) in enumerate(self.jobs):
                        self.pe_job(pe, 0, 0, j, name, ("job", j - 1, 0) if j else None)
                    self.rounds(pe, self.pe_slot)


class Pieces:

    def __init__(self, core, tag, st):
        self.c, self.tag, self.st, self.items = core, tag, st, []
        self.hi_done, self.lo_done = core.sem(f"{tag}_w_hi"), core.sem(f"{tag}_w_lo")

    def add(self, name, shape):
        raw = self.c.sb(f"{self.tag}_{name}_raw", shape, F32, self.st)
        hi, lo = (self.c.sb(f"{self.tag}_{name}_{p}", shape, BF16, self.st) for p in ("hi", "lo"))
        self.items.append((raw, hi, lo, self.c.sem(f"{self.tag}_{name}_loaded")))
        return raw, [hi, lo]

    def load(self, sp, i, src):
        sp.dma_start(self.items[i][0][:], src).then_inc(self.items[i][3], 16)

    def scalar_hi(self, act, i):
        raw, hi, _, loaded = self.items[i]
        act.wait_ge(loaded, 16)
        act.activation(hi[:], raw[:], ACT.Copy).then_inc(self.hi_done, 1)

    def gpsimd_lo(self, pool, i):
        raw, hi, lo, _ = self.items[i]
        pool.wait_ge(self.hi_done, i + 1)
        pool.tensor_tensor(lo[:], raw[:], hi[:], ALU.subtract).then_inc(self.lo_done, 1)

    def wait(self, pe, i):
        pe.wait_ge(self.hi_done, i + 1)
        pe.wait_ge(self.lo_done, i + 1)


def lora_experts(nc, core, a):
    c, E, R, K = core, 8, 64, 128
    ln = LayerNorm(c)
    S = lambda n: c.sem(f"l0f_{n}")
    small, mean_done, chain_sem, q_done, q_rep, score_done, bias_done, exp_done, coef_done = (S(n) for n in (
        "small_loaded", "mean_done", "chain", "q_done", "q_repeated", "scores_done", "bias_done", "exp_done",
        "coef_done"))
    h_done, h_scaled, h_hi, h_lo, out_done, x_done = (S(n) for n in (
        "h_done", "h_scaled", "h_hi", "h_lo", "out_done", "x_done"))
    with ExitStack() as st:
        w = Pieces(c, "l0f", st)
        _, down = w.add("down", [P, DC, E * R])
        _, worg = w.add("worg", [P, DC, D])
        _, up = w.add("up", [P, E * R // P, D])
        sb = lambda name, shape, dt=F32: c.sb(f"l0f_{name}", shape, dt, st)
        wq, keys = sb("wq", [P, DC, K]), sb("keys", [K, E])
        xm, q_all, coef = sb("x_mean", [P, DC, NB]), sb("q_all", [K, NB, P]), sb("coef", [P, NB, E])
        top, bias, sums, rec = (sb(n, [P, NB]) for n in ("top", "bias", "sums", "recip"))
        rowc = sb("row_coef", [P, NB, E * R // P])
        hf = sb("h_float", [P, E * R // P, TOK])
        hT = [sb(f"h_{p}", [P, E * R // P, TOK], BF16) for p in ("hi", "lo")]
        M = E * R // P
        with nc.Block() as block:

            @block.sync
            def _(sp):
                w.load(sp, 0, a["l0_down"])
                sp.dma_start(wq[:], a["l0_wq"]).then_inc(small, 16)
                sp.dma_start(keys[:], a["l0_keys"]).then_inc(small, 16)
                w.load(sp, 1, a["l0_worg"])
                w.load(sp, 2, a["l0_up"])

            @block.gpsimd
            def _(pool):
                ln.gpsimd(pool)
                for i in range(3):
                    w.gpsimd_lo(pool, i)
                for m in range(M):
                    pool.wait_ge(h_hi, m + 1)
                    pool.tensor_tensor(hT[1][:, m, :], hf[:, m, :], hT[0][:, m, :], ALU.subtract).then_inc(h_lo, 1)

            @block.scalar
            def _(act):
                w.scalar_hi(act, 0)
                ln.scalar_hi(act)
                for i in (1, 2):
                    w.scalar_hi(act, i)
                for b in range(NB):
                    act.wait_ge(bias_done, 1)
                    act.activation(coef[:, b, :], c.bank(5, E, at=b * E), ACT.Exp, bias=bias[:, b:b + 1],
                                   scale=float(K) ** -0.5, accum_out=sums[:, b:b + 1]).then_inc(exp_done, 1)
                for m in range(M):
                    act.wait_ge(h_scaled, m + 1)
                    act.activation(hT[0][:, m, :], hf[:, m, :], ACT.Copy).then_inc(h_hi, 1)

            @block.vector
            def _(dve):
                link = Chain(dve, chain_sem)
                ln.vector_norm(dve)
                ln.vector_lo(dve)
                for d in range(DC):
                    dve.reduce_sum(xm[:, d, :], c.bank(d).rearrange("p (b s) -> p b s", b=NB), AX.X)\
                       .then_inc(mean_done, 1)
                dve.wait_ge(q_done, 1)
                for b in range(NB):
                    dve.tensor_scalar(q_all[:, b, :], c.bank(4, 1, at=b).to_broadcast([K, P]), 1.0 / SQ, None,
                                      ALU.mult).then_inc(q_rep, 1)
                dve.wait_ge(score_done, 1)
                link(dve.reduce_max(top[:], c.bank(5, NB * E).rearrange("p (b e) -> p b e", b=NB), AX.X))
                dve.tensor_scalar(bias[:], top[:], -float(K) ** -0.5, None, ALU.mult).then_inc(bias_done, 1)
                dve.wait_ge(exp_done, NB)
                link(dve.reciprocal(rec[:], sums[:]))
                link(dve.tensor_tensor(coef[:], coef[:], rec[:].unsqueeze(2).to_broadcast([P, NB, E]), ALU.mult))
                dve.tensor_copy(rowc[0:R], coef[0:R, :, 0:E:2]).then_inc(coef_done, 1)
                dve.tensor_copy(rowc[R:P], coef[R:P, :, 1:E:2]).then_inc(coef_done, 1)
                dve.wait_ge(coef_done, 2)
                for m in range(M):
                    dve.wait_ge(h_done, m + 1)
                    for b in range(NB):
                        last = dve.tensor_scalar(hf[:, m, b * SQ:(b + 1) * SQ], c.bank(m, SQ, at=b * SQ),
                                                 rowc[:, b, m:m + 1], None, ALU.mult)
                    last.then_inc(h_scaled, 1)
                for t in range(NT):
                    dve.wait_ge(out_done, t + 1)
                    dve.scalar_tensor_tensor(c.x[:, t, :], c.bank(4 + t), c.gates[:, 1:2], c.x[:, t, :],
                                             ALU.mult, ALU.add).then_inc(x_done, 1)

            @block.tensor
            def _(pe):
                ln.tensor_turn(pe)
                ln.wait_parts(pe)
                pe.wait_ge(mean_done, DC)
                pe.wait_ge(small, 32)
                for d in range(DC):
                    last = pe.matmul(c.bank(4, NB), wq[:, d, :], xm[:, d, :], start=d == 0, stop=d == DC - 1)
                last.then_inc(q_done, 1)
                w.wait(pe, 0)
                for m in range(M):
                    for d in range(DC):
                        last = three(pe, c.bank(m), [v[:, d, m * P:(m + 1) * P] for v in down],
                                     [v[:, d, :] for v in c.xT], d == 0, d == DC - 1)
                    last.then_inc(h_done, 1)
                    if m == 0:
                        pe.wait_ge(q_rep, NB)
                        for b in range(NB):
                            last = pe.matmul(c.bank(5, E, at=b * E), q_all[:, b, :], keys[:], start=True, stop=True)
                        last.then_inc(score_done, 1)
                pe.wait_ge(coef_done, 2)
                w.wait(pe, 1)
                for t in range(NT):
                    for d in range(DC):
                        three(pe, c.bank(4 + t), [v[:, d, t * P:(t + 1) * P] for v in c.xT],
                              [v[:, d, :] for v in worg], d == 0, False)
                w.wait(pe, 2)
                pe.wait_ge(h_lo, M)
                for t in range(NT):
                    for m in range(M):
                        last = three(pe, c.bank(4 + t), [v[:, m, t * P:(t + 1) * P] for v in hT],
                                     [v[:, m, :] for v in up], False, m == M - 1)
                    last.then_inc(out_done, 1)


def sparse_rows(nc, core, a):
    c, F, SP_, RANK = core, 1792, 32, 16
    BL, M = F // SP_, F // P
    ln = LayerNorm(c)
    S = lambda n: c.sem(f"l1f_{n}")
    small, zeroed, xf_done, u_done, u_saved, inter_done, chain_sem, eq_done, key_done, mask_done = (S(n) for n in (
        "small_loaded", "zeroed", "x_float_done", "u_done", "u_saved", "inter_done", "chain", "eq_done",
        "key_done", "mask_done"))
    mT_done, mT_saved, h_done, h_masked, h_hi, h_lo, out_used, out_done, x_done = (S(n) for n in (
        "mask_turned", "mask_T_saved", "h_done", "h_masked", "h_hi", "h_lo", "out_used", "out_done", "x_done"))
    with ExitStack() as st:
        w = Pieces(c, "l1f", st)
        sb = lambda name, shape, dt=F32: c.sb(f"l1f_{name}", shape, dt, st)
        w1 = [w.add(f"w1_{d}", [P, F])[1] for d in range(DC)]
        w2 = [w.add(f"w2_{i}", [P, M // 2, D])[1] for i in range(2)]
        c1, c2 = sb("c1", [P, DC, P]), sb("c2", [P, F])
        u = sb("u", [P, TOK])
        mx, eq, key = sb("block_max", [P, BL]), sb("at_max", [P, BL, SP_], BF16), sb("key", [P, BL, SP_], BF16)
        key_max, rev = sb("key_max", [P, BL], BF16), sb("place_value", [P, SP_])
        mask = sb("chosen", [P, NT, F], BF16)
        mT = [sb(f"chosen_T{i}", [P, TOK], BF16) for i in range(2)]
        hf = [sb(f"h_float{i}", [P, TOK]) for i in range(2)]
        hT = [[sb(f"h{i}_{p}", [P, TOK], BF16) for p in ("hi", "lo")] for i in range(2)]
        inter = c.ps[:, 0:F].rearrange("p (n s) -> p n s", s=SP_)
        with nc.Block() as block:

            @block.sync
            def _(sp):
                sp.wait_ge(zeroed, 2)
                sp.dma_start(c1[:, :, 0:RANK], a["l1_c1"]).then_inc(small, 16)
                sp.dma_start(c2[0:RANK, :], a["l1_c2"]).then_inc(small, 16)
                sp.dma_start(rev[:], a["place_value"]).then_inc(small, 16)
                for d in range(DC):
                    w.load(sp, d, a["l1_w1"][:, d, :])
                for i in range(2):
                    w.load(sp, DC + i, a["l1_w2"][:, i * M // 2:(i + 1) * M // 2, :])

            @block.gpsimd
            def _(pool):
                pool.memset(c1[:], 0.0).then_inc(zeroed, 1)
                pool.memset(c2[:], 0.0).then_inc(zeroed, 1)
                ln.gpsimd(pool)
                for i in range(DC + 2):
                    w.gpsimd_lo(pool, i)
                for m in range(M):
                    pool.wait_ge(h_hi, m + 1)
                    pool.tensor_tensor(hT[m % 2][1][:], hf[m % 2][:], hT[m % 2][0][:], ALU.subtract).then_inc(h_lo, 1)

            @block.scalar
            def _(act):
                ln.scalar_hi(act)
                for d in range(DC):
                    ln.wait_lo(act, d + 1)
                    act.activation(c.xn[:, d, :], c.bank(d), ACT.Copy).then_inc(xf_done, 1)
                act.wait_ge(u_done, 1)
                act.activation(u[:], c.bank(4), ACT.Copy).then_inc(u_saved, 1)
                for i in range(DC + 2):
                    w.scalar_hi(act, i)
                for m in range(M):
                    act.wait_ge(mT_done, m + 1)
                    if m >= 2:
                        act.wait_ge(h_masked, m - 1)
                    act.activation(mT[m % 2][:], c.bank(2 + m % 2), ACT.Copy).then_inc(mT_saved, 1)
                    act.wait_ge(h_masked, m + 1)
                    if m >= 2:
                        act.wait_ge(out_used, m - 1)
                    act.activation(hT[m % 2][0][:], hf[m % 2][:], ACT.Copy).then_inc(h_hi, 1)

            @block.vector
            def _(dve):
                link = Chain(dve, chain_sem)
                ln.vector_norm(dve)
                ln.vector_lo(dve)
                dve.wait_ge(small, 48)
                for t in range(NT):
                    dve.wait_ge(inter_done, t + 1)
                    link(dve.reduce_max(mx[:], inter, AX.X))
                    dve.tensor_tensor(eq[:], inter, mx[:].unsqueeze(2).to_broadcast([P, BL, SP_]),
                                      ALU.is_equal).then_inc(eq_done, 1)
                    dve.wait_ge(eq_done, t + 1)
                    link(dve.tensor_tensor(key[:], eq[:], rev[:].unsqueeze(1).to_broadcast([P, BL, SP_]), ALU.mult))
                    link(dve.reduce_max(key_max[:], key[:], AX.X))
                    dve.tensor_tensor(mask[:, t, :].rearrange("p (n s) -> p n s", s=SP_), key[:],
                                      key_max[:].unsqueeze(2).to_broadcast([P, BL, SP_]), ALU.is_equal)\
                       .then_inc(mask_done, 1)
                for m in range(M):
                    dve.wait_ge(h_done, m + 1)
                    dve.wait_ge(mT_saved, m + 1)
                    if m >= 2:
                        dve.wait_ge(h_lo, m - 1)
                    dve.scalar_tensor_tensor(hf[m % 2][:], c.bank(m % 2), 0.0, mT[m % 2][:], ALU.max, ALU.mult)\
                       .then_inc(h_masked, 1)
                for t in range(NT):
                    dve.wait_ge(out_done, t + 1)
                    dve.scalar_tensor_tensor(c.x[:, t, :], c.bank(4 + t), c.gates[:, 3:4], c.x[:, t, :],
                                             ALU.mult, ALU.add).then_inc(x_done, 1)

            @block.tensor
            def _(pe):
                ln.tensor_turn(pe)
                pe.wait_ge(small, 48)
                for d in range(DC):
                    pe.wait_ge(xf_done, d + 1)
                    last = pe.matmul(c.bank(4), c1[:, d, :], c.xn[:, d, :], start=d == 0, stop=d == DC - 1)
                last.then_inc(u_done, 1)
                pe.wait_ge(u_saved, 1)
                for t in range(NT):
                    if t:
                        pe.wait_ge(eq_done, t)
                    for n in range(0, F, BANK):
                        last = pe.matmul(c.ps[:, n:min(n + BANK, F)], u[:, t * P:(t + 1) * P],
                                         c2[:, n:min(n + BANK, F)], start=True, stop=True)
                    last.then_inc(inter_done, 1)
                pe.wait_ge(eq_done, NT)
                w.wait(pe, DC + 1)

                def add_out(m):
                    pe.wait_ge(h_lo, m + 1)
                    for t in range(NT):
                        last = three(pe, c.bank(4 + t), [v[:, t * P:(t + 1) * P] for v in hT[m % 2]],
                                     [v[:, m % (M // 2), :] for v in w2[m // (M // 2)]], m == 0, m == M - 1)
                        if m == M - 1:
                            last.then_inc(out_done, 1)
                    if m < M - 1:
                        last.then_inc(out_used, 1)

                for m in range(M):
                    if m >= 2:
                        pe.wait_ge(mT_saved, m - 1)
                    for t in range(NT):
                        if m == 0:
                            pe.wait_ge(mask_done, t + 1)
                        last = pe.matmul(c.bank(2 + m % 2, P, at=t * P), mask[:, t, m * P:(m + 1) * P], c.ident16[:],
                                         start=True, stop=True)
                    last.then_inc(mT_done, 1)
                    if m >= 2:
                        pe.wait_ge(h_masked, m - 1)
                    for d in range(DC):
                        last = three(pe, c.bank(m % 2), [v[:, m * P:(m + 1) * P] for v in w1[d]],
                                     [v[:, d, :] for v in c.xT], d == 0, d == DC - 1)
                    last.then_inc(h_done, 1)
                    if m:
                        add_out(m - 1)
                add_out(M - 1)


def gated_lora(nc, core, a):
    c, E, R = core, 4, 8
    G = E * R + E
    ln = LayerNorm(c)
    S = lambda n: c.sem(f"l2f_{n}")
    small, zeroed, ga_done, chain_sem, sub_done, exp_done, gp_done, gp_turned, gp_hi, gp_lo, out_done, x_done = (
        S(n) for n in ("small_loaded", "zeroed", "proj_done", "chain", "sub_done", "exp_done", "mix_done",
                       "mix_turned", "mix_hi", "mix_lo", "out_done", "x_done"))
    with ExitStack() as st:
        w = Pieces(c, "l2f", st)
        _, ar = w.add("a_wr", [P, DC, G])
        _, wt = w.add("w", [P, DC, D])
        bm_raw, bm = w.add("bm", [P, D])
        sb = lambda name, shape, dt=F32: c.sb(f"l2f_{name}", shape, dt, st)
        bias = sb("bias", [P, D])
        top, sums = sb("top", [P, NT]), sb("sums", [P, NT])
        e = sb("gate", [P, NT, E])
        gp = sb("mix", [P, NT, P])
        gpT = [sb(f"mix_T_{p}", [P, TOK], BF16) for p in ("hi", "lo")]
        tmp = sb("out", [P, NT, D])
        ga = c.bank(4, NT * G).rearrange("p (t g) -> p t g", t=NT)
        with nc.Block() as block:

            @block.sync
            def _(sp):
                w.load(sp, 0, a["l2_awr"])
                w.load(sp, 1, a["l2_w"])
                sp.wait_ge(zeroed, 2)
                sp.dma_start(bm_raw[0:E * R, :], a["l2_bm"]).then_inc(w.items[2][3], 16)
                sp.dma_start(bias[:], a["l2_b"]).then_inc(small, 16)

            @block.gpsimd
            def _(pool):
                pool.memset(gp[:], 0.0).then_inc(zeroed, 1)
                pool.memset(bm_raw[:], 0.0).then_inc(zeroed, 1)
                ln.gpsimd(pool)
                for i in range(3):
                    w.gpsimd_lo(pool, i)

            @block.scalar
            def _(act):
                w.scalar_hi(act, 0)
                ln.scalar_hi(act)
                for i in (1, 2):
                    w.scalar_hi(act, i)
                act.wait_ge(sub_done, 1)
                act.activation(e[:], e[:], ACT.Exp).then_inc(exp_done, 1)
                act.wait_ge(gp_turned, 1)
                act.activation(gpT[0][:], c.bank(5), ACT.Copy).then_inc(gp_hi, 1)

            @block.vector
            def _(dve):
                link = Chain(dve, chain_sem)
                each = lambda v, n: v[:].unsqueeze(2).to_broadcast([P, NT, n])
                ln.vector_norm(dve)
                ln.vector_lo(dve)
                dve.wait_ge(ga_done, 1)
                link(dve.reduce_max(top[:], ga[:, :, E * R:], AX.X))
                dve.tensor_tensor(e[:], ga[:, :, E * R:], each(top, E), ALU.subtract).then_inc(sub_done, 1)
                dve.wait_ge(exp_done, 1)
                link(dve.reduce_sum(sums[:], e[:], AX.X))
                link(dve.reciprocal(sums[:], sums[:]))
                link(dve.tensor_scalar(sums[:], sums[:], 2.0, None, ALU.mult))
                link(dve.tensor_tensor(e[:], e[:], each(sums, E), ALU.mult))
                dve.wait_ge(zeroed, 1)
                for t in range(NT):
                    dve.tensor_tensor(gp[:, t, 0:E * R].rearrange("p (e r) -> p e r", e=E),
                                      ga[:, t, 0:E * R].rearrange("p (e r) -> p e r", e=E),
                                      e[:, t, :].unsqueeze(2).to_broadcast([P, E, R]), ALU.mult).then_inc(gp_done, 1)
                dve.wait_ge(gp_hi, 1)
                dve.tensor_tensor(gpT[1][:], c.bank(5), gpT[0][:], ALU.subtract).then_inc(gp_lo, 1)
                dve.wait_ge(small, 16)
                for t in range(NT):
                    dve.wait_ge(out_done, t + 1)
                    link(dve.tensor_tensor(tmp[:, t, :], c.bank(t), bias[:], ALU.add))
                    dve.scalar_tensor_tensor(c.x[:, t, :], tmp[:, t, :], c.gates[:, 5:6], c.x[:, t, :],
                                             ALU.mult, ALU.add).then_inc(x_done, 1)

            @block.tensor
            def _(pe):
                ln.tensor_turn(pe)
                ln.wait_parts(pe)
                w.wait(pe, 0)
                for t in range(NT):
                    for d in range(DC):
                        last = three(pe, c.bank(4, G, at=t * G), [v[:, d, t * P:(t + 1) * P] for v in c.xT],
                                     [v[:, d, :] for v in ar], d == 0, d == DC - 1)
                last.then_inc(ga_done, 1)
                w.wait(pe, 1)
                for t in range(NT):
                    for d in range(DC):
                        three(pe, c.bank(t), [v[:, d, t * P:(t + 1) * P] for v in c.xT],
                              [v[:, d, :] for v in wt], d == 0, False)
                pe.wait_ge(gp_done, NT)
                for t in range(NT):
                    last = pe.transpose(c.bank(5, P, at=t * P), gp[:, t, :], c.ident[:])
                last.then_inc(gp_turned, 1)
                w.wait(pe, 2)
                pe.wait_ge(gp_lo, 1)
                for t in range(NT):
                    last = three(pe, c.bank(t), [v[:, t * P:(t + 1) * P] for v in gpT], [v[:] for v in bm],
                                 False, True)
                    last.then_inc(out_done, 1)


def routed_experts(nc, core, a):
    c, E, M = core, 3, D // P
    VIS = int(SQ * 0.3)
    ln = LayerNorm(c)
    S = lambda n: c.sem(f"l3f_{n}")
    small, sel_done, abs_done, tot_done, gate_made, chain_sem, sub_done, exp_done, pick_done, pick_rep, coef_done = (
        S(n) for n in ("small_loaded", "row0_done", "abs_done", "totals_done", "gate_made", "chain", "sub_done",
                       "exp_done", "picks_done", "picks_repeated", "coef_done"))
    pre_done, act_done, a_hi, a_lo, out_done, x_done = (
        S(n) for n in ("pre_done", "act_done", "act_hi", "act_lo", "out_done", "x_done"))
    with ExitStack() as st:
        w = Pieces(c, "l3f", st)
        w1, w2 = [], []
        for e in range(E):
            w1.append(w.add(f"w1_{e}", [P, DC, D])[1])
            w2.append(w.add(f"w2_{e}", [P, M, D])[1])
        _, gw = w.add("gate_w", [P, DC, E])
        order = [0, 2, 1, 4, 3, 5]
        sb = lambda name, shape, dt=F32: c.sb(f"l3f_{name}", shape, dt, st)
        b1, b2 = sb("b1", [P, E, M]), sb("b2", [P, E, D])
        gw_last, gb, place = sb("gate_w_last", [P, E]), sb("gate_b", [P, E]), sb("place_value", [P, E])
        row0, junk = sb("row0", [P, P]), sb("junk", [P, SQ])
        absum, tot = sb("abs_sums", [P, DC, 4]), sb("abs_totals", [P, 4])
        ratio, gb2 = sb("ratio", [P, NB]), sb("gate_const", [P, NB, E])
        s, key, s2 = sb("scores", [P, NT, E]), sb("key", [P, NT, E]), sb("scores2", [P, NT, E])
        picks = sb("picks", [P, 2, NT, E])
        pick0 = sb("picks_of_token0", [P, 2, NB, E])
        v1, v2, t4, u4 = (sb(n, [P, NT]) for n in ("value1", "value2", "t4", "u4"))
        coef, coef2 = sb("coef", [P, NT, E]), sb("coef2", [P, NT, E])
        af = [sb(f"act_float{i}", [P, TOK]) for i in range(2)]
        aT = [[sb(f"act{i}_{p}", [P, M, TOK], BF16) for p in ("hi", "lo")] for i in range(2)]
        tmp = [sb(f"out{i}", [P, D]) for i in range(2)]
        with nc.Block() as block:

            @block.sync
            def _(sp):
                w.load(sp, 6, a["l3_gate_w"])
                for dst, name in ((b1, "l3_b1"), (b2, "l3_b2"), (gw_last, "l3_gate_w_last"), (gb, "l3_gate_b"),
                                  (place, "place3")):
                    sp.dma_start(dst[:], a[name]).then_inc(small, 16)
                for i in order:
                    w.load(sp, i, a["l3_w1" if i % 2 == 0 else "l3_w2"][:, i // 2])

            @block.gpsimd
            def _(pool):
                pool.memset(row0[:], 0.0).then_inc(sel_done, 1)
                pool.wait_ge(sel_done, 1)
                pool.memset(row0[0:1, :], 1.0).then_inc(sel_done, 1)
                ln.gpsimd(pool)
                for n, i in enumerate([6] + order):
                    raw, hi, lo, _ = w.items[i]
                    pool.wait_ge(w.hi_done, n + 1)
                    pool.tensor_tensor(lo[:], raw[:], hi[:], ALU.subtract).then_inc(w.lo_done, 1)
                for n in range(E * M):
                    e, m = n // M, n % M
                    pool.wait_ge(a_hi, n + 1)
                    pool.tensor_tensor(aT[e % 2][1][:, m, :], af[n % 2][:], aT[e % 2][0][:, m, :], ALU.subtract)\
                        .then_inc(a_lo, 1)

            @block.scalar
            def _(act):
                w.scalar_hi(act, 6)
                ln.scalar_hi(act)
                for d in range(DC):
                    ln.wait_lo(act, d + 1)
                    for b in range(NB):
                        for k, (lo, hi) in enumerate(((0, VIS), (VIS, SQ))):
                            n = 2 * b + k
                            act.wait_ge(abs_done, 4 * d + n) if 4 * d + n else None
                            act.activation(junk[:, 0:hi - lo], c.bank(d, hi - lo, at=b * SQ + lo), ACT.Abs,
                                           accum_out=absum[:, d, n:n + 1]).then_inc(abs_done, 1)
                for i in order[:1]:
                    w.scalar_hi(act, i)
                act.wait_ge(sub_done, 1)
                act.activation(s[:], s[:], ACT.Exp).then_inc(exp_done, 1)
                for i in order[1:]:
                    w.scalar_hi(act, i)
                act.wait_ge(small, 80)
                for n in range(E * M):
                    e, m = n // M, n % M
                    act.wait_ge(pre_done, n + 1)
                    if n >= 2:
                        act.wait_ge(a_lo, n - 1)
                    act.activation(af[n % 2][:], c.bank(m), (ACT.Tanh, ACT.Gelu, ACT.Silu)[e],
                                   bias=b1[:, e, m:m + 1]).then_inc(act_done, 1)
                    act.wait_ge(act_done, n + 1)
                    if e == 2:
                        act.wait_ge(out_done, NT)
                    act.activation(aT[e % 2][0][:, m, :], af[n % 2][:], ACT.Copy).then_inc(a_hi, 1)

            @block.vector
            def _(dve):
                link = Chain(dve, chain_sem)
                each = lambda v: v[:].unsqueeze(2).to_broadcast([P, NT, E])
                places = place[:].unsqueeze(1).to_broadcast([P, NT, E])

                def pick(src, value, i):
                    link(dve.reduce_max(value[:], src[:], AX.X))
                    link(dve.tensor_tensor(key[:], src[:], each(value), ALU.is_equal))
                    link(dve.tensor_tensor(key[:], key[:], places, ALU.mult))
                    link(dve.reduce_max(t4[:], key[:], AX.X))
                    link(dve.tensor_tensor(picks[:, i], key[:], each(t4), ALU.is_equal))

                ln.vector_norm(dve)
                ln.vector_lo(dve)
                dve.wait_ge(tot_done, 1)
                dve.wait_ge(small, 80)
                link(dve.reduce_sum(tot[:], c.bank(4, DC * 4).rearrange("p (d n) -> p n d", d=DC), AX.X))
                link(dve.tensor_scalar(ratio[:], tot[:, 0:4:2], 1.0 / (VIS * D), 1e-8, ALU.mult, ALU.add))
                link(dve.reciprocal(ratio[:], ratio[:]))
                link(dve.tensor_scalar(tot[:, 1:4:2], tot[:, 1:4:2], 1.0 / ((SQ - VIS) * D), None, ALU.mult))
                link(dve.tensor_tensor(ratio[:], ratio[:], tot[:, 1:4:2], ALU.mult))
                for b in range(NB):
                    link(dve.scalar_tensor_tensor(gb2[:, b, :], gw_last[:], ratio[:, b:b + 1], gb[:],
                                                  ALU.mult, ALU.add))
                dve.wait_ge(gate_made, 1)
                for b in range(NB):
                    link(dve.tensor_tensor(s[:, 2 * b:2 * b + 2, :],
                                           c.bank(5, 2 * E, at=2 * E * b).rearrange("p (t e) -> p t e", e=E),
                                           gb2[:, b, :].unsqueeze(1).to_broadcast([P, 2, E]), ALU.add))
                link(dve.reduce_max(t4[:], s[:], AX.X))
                dve.tensor_tensor(s[:], s[:], each(t4), ALU.subtract).then_inc(sub_done, 1)
                dve.wait_ge(exp_done, 1)
                link(dve.reduce_sum(t4[:], s[:], AX.X))
                link(dve.reciprocal(t4[:], t4[:]))
                link(dve.tensor_tensor(s[:], s[:], each(t4), ALU.mult))
                pick(s, v1, 0)
                link(dve.scalar_tensor_tensor(s2[:], picks[:, 0], -4.0, s[:], ALU.mult, ALU.add))
                pick(s2, v2, 1)
                link(dve.tensor_tensor(u4[:], v1[:], v2[:], ALU.add))
                link(dve.tensor_scalar(u4[:], u4[:], 1e-8, None, ALU.add))
                link(dve.reciprocal(u4[:], u4[:]))
                link(dve.tensor_scalar(u4[:], u4[:], c.gates[:, 7:8], None, ALU.mult))
                link(dve.tensor_tensor(v1[:], v1[:], u4[:], ALU.mult))
                dve.tensor_tensor(v2[:], v2[:], u4[:], ALU.mult).then_inc(pick_done, 1)
                dve.wait_ge(pick_rep, 1)
                link(dve.tensor_copy(pick0[:], c.bank(6, 2 * NT * E).rearrange(
                    "p (i b t e) -> p i b t e", i=2, b=NB, t=2)[:, :, :, 0, :]))
                for b in range(NB):
                    rows = slice(2 * b, 2 * b + 2)
                    of0 = lambda i: pick0[:, i, b, :].unsqueeze(1).to_broadcast([P, 2, E])
                    w_of = lambda v: v[:, rows].unsqueeze(2).to_broadcast([P, 2, E])
                    link(dve.tensor_tensor(coef[:, rows, :], of0(0), w_of(v1), ALU.mult))
                    link(dve.tensor_tensor(coef2[:, rows, :], of0(1), w_of(v2), ALU.mult))
                dve.tensor_tensor(coef[:], coef[:], coef2[:], ALU.add).then_inc(coef_done, 1)
                dve.wait_ge(coef_done, 1)
                for n in range(E * NT):
                    e, t = n // NT, n % NT
                    dve.wait_ge(out_done, n + 1)
                    link(dve.tensor_tensor(tmp[n % 2][:], c.bank(4 + t), b2[:, e, :], ALU.add))
                    dve.scalar_tensor_tensor(c.x[:, t, :], tmp[n % 2][:], coef[:, t, e:e + 1], c.x[:, t, :],
                                             ALU.mult, ALU.add).then_inc(x_done, 1)

            @block.tensor
            def _(pe):
                def ready(n):
                    pe.wait_ge(w.hi_done, n)
                    pe.wait_ge(w.lo_done, n)

                def up(e):
                    ready(2 + order.index(2 * e))
                    for m in range(M):
                        n = e * M + m
                        if n >= M:
                            pe.wait_ge(act_done, n - M + 1)
                        for d in range(DC):
                            last = three(pe, c.bank(m), [v[:, d, m * P:(m + 1) * P] for v in w1[e]],
                                         [v[:, d, :] for v in c.xT], d == 0, d == DC - 1)
                        last.then_inc(pre_done, 1)

                def down(e):
                    ready(2 + order.index(2 * e + 1))
                    pe.wait_ge(a_lo, (e + 1) * M)
                    for t in range(NT):
                        if e:
                            pe.wait_ge(x_done, (e - 1) * NT + t + 1)
                        for m in range(M):
                            last = three(pe, c.bank(4 + t), [v[:, m, t * P:(t + 1) * P] for v in aT[e % 2]],
                                         [v[:, m, :] for v in w2[e]], m == 0, m == M - 1)
                        last.then_inc(out_done, 1)

                ln.tensor_turn(pe)
                ln.wait_parts(pe)
                ready(1)
                for t in range(NT):
                    for d in range(DC):
                        last = three(pe, c.bank(5, E, at=t * E), [v[:, d, t * P:(t + 1) * P] for v in c.xT],
                                     [v[:, d, :] for v in gw], d == 0, d == DC - 1)
                last.then_inc(gate_made, 1)
                pe.wait_ge(abs_done, 4 * DC)
                pe.matmul(c.bank(4, DC * 4), c.ones[:], absum[:].rearrange("p d n -> p (d n)"),
                          start=True, stop=True).then_inc(tot_done, 1)
                up(0)
                pe.wait_ge(pick_done, 1)
                pe.wait_ge(sel_done, 2)
                pe.matmul(c.bank(6, 2 * NT * E), row0[:], picks[:].rearrange("p i t e -> p (i t e)"),
                          start=True, stop=True).then_inc(pick_rep, 1)
                up(1)
                pe.wait_ge(coef_done, 1)
                down(0)
                up(2)
                down(1)
                down(2)


def store(nc, core, out):
    stored = core.sem("stored")
    with nc.Block() as block:

        @block.sync
        def _(sp):
            sp.dma_start(out, core.x[:]).then_inc(stored, 16)
            sp.wait_ge(stored, 16)


def build(nc, a, out):
    with ExitStack() as ctx:
        core = Core(nc, ctx)
        setup_and_quant_product(nc, core, a)
        lora_experts(nc, core, a)
        Attention(core, "l1x", 2, 8, 128, True, norm=True).run(
            a["l1_qkv"], a["l1_wo"], {"qw": a["l1_qw"], "kw": a["l1_kw"]})
        sparse_rows(nc, core, a)
        Attention(core, "l2x", 4, 8, 128, False, rope=True, mask=True).run(
            a["l2_qkv"], a["l2_wo"], {n: a[n] for n in ("k_cos", "k_sin", "q_cos", "q_sin", "mask")})
        gated_lora(nc, core, a)
        Attention(core, "l3x", 6, 4, 96, True).run(a["l3_qkv"], a["l3_wo"], {})
        routed_experts(nc, core, a)
        store(nc, core, out)


def columns(w):
    k, n = w.shape
    return w.reshape(k // P, P, n).transpose(1, 0, 2)


def heads_together(wk, wv, wq, hd):
    rounds = wk.shape[1] // hd
    parts = [w.reshape(DC, P, rounds, -1) for w in (wk, wv, wq)]
    return np.concatenate(parts, 3).transpose(1, 2, 0, 3).reshape(P, -1)


def heads_out(wo, hd):
    return wo.reshape(-1, hd, D).transpose(1, 0, 2).reshape(hd, -1)


def rotation_tables(hd):
    inv = (1.0 / 10000.0 ** (np.arange(0, hd, 2, dtype=np.float32) / np.float32(hd))).astype(np.float32)
    ang = (np.arange(SC, dtype=np.float32)[None, :] * inv[:, None]).astype(np.float32)
    cos, sin = np.cos(ang).astype(np.float32), np.sin(ang).astype(np.float32)
    k_cos, k_sin = np.concatenate([cos, cos]), np.concatenate([sin, -sin])
    scale = np.float32(hd) ** np.float32(-0.5)
    q_cos, q_sin = (np.tile(w[:, :SQ] * scale, (1, 2)).astype(np.float32) for w in (k_cos, k_sin))
    return {"k_cos": k_cos, "k_sin": k_sin, "q_cos": q_cos, "q_sin": q_sin}


def lay_out(v):
    rows = lambda w: np.broadcast_to(w, (P, *w.shape))
    d = {
        "x": v["x"].reshape(NT, P, D).transpose(1, 0, 2),
        "context": v["ctx_4096"].reshape(-1, P, D).transpose(1, 0, 2),
        "context_T": columns(v["ctx_4096"].reshape(-1, D).T),
        "gates": rows(np.stack([v["g_xattn"], v["g_ffn"]], 1).reshape(8)),
        "quant": rows(np.concatenate([v["L0_xattn_x1_scale"], v["L0_xattn_x1_zp"],
                                      v["L0_xattn_x2_scale"], v["L0_xattn_x2_zp"]])),
    }
    d["l1_qkv"] = heads_together(v["L1_xattn_Wk"], v["L1_xattn_Wv"], v["L1_xattn_Wq"], 128)
    d["l1_wo"] = heads_out(v["L1_xattn_Wo"], 128)
    d["l1_qw"], d["l1_kw"] = v["L1_xattn_q_norm_w"][:, None], v["L1_xattn_k_norm_w"][:, None]
    d["l2_qkv"] = heads_together(v["L2_xattn_wk"], v["L2_xattn_wv"], v["L2_xattn_wq"], 128)
    d["l2_wo"] = heads_out(v["L2_xattn_wo"], 128)
    d.update(rotation_tables(128))
    d["mask"] = v["mask_BxSxS2_ff0"].reshape(NT, P, SC).transpose(1, 0, 2)
    d["l3_qkv"] = heads_together(v["L3_xattn_Wk"].T, v["L3_xattn_Wv"].T, v["L3_xattn_Wq"].T, 96)
    d["l3_wo"] = heads_out(v["L3_xattn_Wo"].T, 96)
    d["l0_down"] = columns(v["L0_ffn_lora_down"].transpose(1, 0, 2).reshape(D, -1))
    d["l0_up"] = columns(v["L0_ffn_lora_up"].reshape(-1, D))
    d["l0_worg"], d["l0_wq"] = columns(v["L0_ffn_W_org"].T), columns(v["L0_ffn_Wq"].T)
    d["l0_keys"] = v["L0_ffn_lora_keys"].T
    d["l1_c1"], d["l1_c2"] = columns(v["L1_ffn_c1_w"].T), v["L1_ffn_c2_w"].T
    d["l1_w1"], d["l1_w2"] = columns(v["L1_ffn_w1"].T), columns(v["L1_ffn_w2t"])
    d["place_value"] = rows(np.arange(32, 0, -1, dtype=np.float32))
    d["l2_awr"] = np.concatenate([columns(v["L2_ffn_A"].reshape(-1, D).T), columns(v["L2_ffn_Wr"].T)], 2)
    d["l2_w"], d["l2_b"] = columns(v["L2_ffn_W"].T), rows(v["L2_ffn_b"])
    d["l2_bm"] = v["L2_ffn_Bm"].transpose(0, 2, 1).reshape(-1, D)
    per_expert = lambda w: w.reshape(3, DC, P, D).transpose(2, 0, 1, 3)
    d["l3_w1"], d["l3_w2"] = per_expert(v["L3_ffn_w1"]), per_expert(v["L3_ffn_w2"])
    d["l3_b1"] = v["L3_ffn_b1"].reshape(3, DC, P).transpose(2, 0, 1)
    d["l3_b2"] = rows(v["L3_ffn_b2"])
    d["l3_gate_w"], d["l3_gate_w_last"] = columns(v["L3_ffn_gate_w"][:D]), rows(v["L3_ffn_gate_w"][D])
    d["l3_gate_b"] = rows(v["L3_ffn_gate_b"])
    d["place3"] = rows(np.arange(3, 0, -1, dtype=np.float32))
    return {k: np.ascontiguousarray(w) for k, w in d.items()}


def kernel(**inputs):
    import concourse.bacc as bacc
    from concourse.bass_utils import run_bass_kernel_spmd as run

    nc = bacc.Bacc("TRN2", target_bir_lowering=False, num_devices=1)
    arrays = lay_out({k: np.asarray(w) for k, w in inputs.items()})
    a = {k: nc.dram_tensor(k + "_dram", w.shape, mybir.dt.from_np(w.dtype), kind="ExternalInput").ap()
         for k, w in arrays.items()}
    out = nc.dram_tensor("out_dram", (P, NT, D), F32, kind="ExternalOutput").ap()
    build(nc, a, out)
    r = run(nc, [{k + "_dram": w for k, w in arrays.items()}], core_ids=[0])
    return r.results[0]["out_dram"].transpose(1, 0, 2).reshape(NB, SQ, D)
```

```python
from contextlib import ExitStack

import numpy as np

import concourse.bass as bass
from concourse import mybir

F32 = mybir.dt.float32
BF16 = mybir.dt.bfloat16
ALU = mybir.AluOpType
ACT = mybir.ActivationFunctionType
AX = mybir.AxisListType

P = 128
D = 512
DC = D // P
NB = 2
SQ = 256
TOK = NB * SQ
NT = TOK // P
SC = 512
BANK = 512
GROUP = 4
ROUND = 12582912.0


def three(pe, out, lhs, rhs, first, last):
    (lh, ll), (rh, rl) = lhs, rhs
    pe.matmul(out, lh, rh, start=first, stop=False)
    pe.matmul(out, lh, rl, start=False, stop=False)
    return pe.matmul(out, ll, rh, start=False, stop=last)


class Chain:

    def __init__(self, eng, sem):
        self.eng, self.sem, self.n = eng, sem, 0

    def __call__(self, ins):
        self.n += 1
        ins.then_inc(self.sem, 1)
        self.eng.wait_ge(self.sem, self.n)


class Core:

    def __init__(self, nc, ctx):
        self.nc, self.ctx = nc, ctx
        self.norms = self.turns = 0
        self.attention_sems = {}
        self.ps = ctx.enter_context(nc.psum_tensor("psum", [P, 8 * BANK], F32))
        self.x = self.sb("x_state", [P, NT, D])
        self.xn = self.sb("x_normed", [P, NT, D])
        self.xT = [self.sb(f"x_normed_T_{part}", [P, DC, TOK], BF16) for part in ("hi", "lo")]
        self.ctxT = [self.sb(f"context_T_{part}", [P, DC, NB * SC], BF16) for part in ("hi", "lo")]
        self.qkv_raw = self.sb("round_weights", [P, DC * (2 + GROUP) * P])
        self.qkv = [self.sb(f"round_weights_{part}", [P, DC * (2 + GROUP) * P], BF16) for part in ("hi", "lo")]
        self.ident = self.sb("identity", [P, P])
        self.ones = self.sb("ones", [P, P])
        self.ident16 = self.sb("identity_bf16", [P, P], BF16)
        self.ones16 = self.sb("ones_bf16", [P, P], BF16)
        self.minus_half = self.sb("minus_half", [P, 16])
        self.gates = self.sb("gates", [P, 8])
        self.stats = self.sb("ln_stats", [P, NT, 6])
        self.meanvar = self.sb("ln_meanvar", [P, NT, 2])
        self.var_eps = self.sb("ln_var_eps", [P, NT])
        self.rstd = self.sb("ln_rstd", [P, NT])

    def sb(self, name, shape, dt=F32, ctx=None):
        return (ctx or self.ctx).enter_context(self.nc.sbuf_tensor(name, shape, dt))

    def sem(self, name):
        return self.ctx.enter_context(self.nc.semaphore(name))

    def bank(self, b, n=BANK, parts=P, at=0):
        return self.ps[0:parts, b * BANK + at:b * BANK + at + n]


class LayerNorm:

    def __init__(self, core, turn=True):
        self.c, self.n, self.turns = core, core.norms, core.turns
        core.norms, core.turns = core.norms + 1, core.turns + turn
        if self.n == 0:
            core.ln_sems = [core.sem(f"ln_{s}") for s in (
                "stats_done", "rstd_done", "normed", "turned", "hi_done", "lo_done")]
        self.stats_done, self.rstd_done, self.normed, self.turned, self.hi_done, self.lo_done = core.ln_sems

    def wait_stats(self, eng, k):
        eng.wait_ge(self.stats_done, 2 * NT * self.n + k)

    def wait_rstd(self, eng, k):
        eng.wait_ge(self.rstd_done, 2 * NT * self.n + k)

    def wait_normed(self, eng, k):
        eng.wait_ge(self.normed, NT * self.n + k)

    def wait_turned(self, eng, k):
        eng.wait_ge(self.turned, DC * self.turns + k)

    def wait_hi(self, eng, k):
        eng.wait_ge(self.hi_done, DC * self.turns + k)

    def wait_lo(self, eng, k):
        eng.wait_ge(self.lo_done, DC * self.turns + k)

    STATS = [1, 2] + [2 * t for t in range(2, NT)]
    AGGR = [2 * t + 3 for t in range(NT - 1)] + [2 * NT]

    def vector_norm(self, dve):
        c = self.c
        for t in range(NT + 1):
            if t < NT:
                dve.bn_stats(c.stats[:, t, :], c.x[:, t, :]).then_inc(self.stats_done, 1)
            if t:
                self.wait_stats(dve, self.STATS[t - 1])
                dve.bn_aggr(c.meanvar[:, t - 1, :], c.stats[:, t - 1, :]).then_inc(self.stats_done, 1)
        self.wait_stats(dve, 2 * NT)
        for t in range(NT):
            self.wait_rstd(dve, 2 * t + 2)
            dve.tensor_scalar(c.xn[:, t, :], c.x[:, t, :], c.meanvar[:, t, 0:1], c.rstd[:, t:t + 1],
                              ALU.subtract, ALU.mult).then_inc(self.normed, 1)

    def gpsimd(self, pool):
        c = self.c
        for t in range(NT):
            self.wait_stats(pool, self.AGGR[t])
            pool.tensor_scalar(c.var_eps[:, t:t + 1], c.meanvar[:, t, 1:2], 1e-5, None, ALU.add)\
                .then_inc(self.rstd_done, 1)
            self.wait_rstd(pool, 2 * t + 1)
            pool.tensor_tensor(c.rstd[:, t:t + 1], c.var_eps[:, t:t + 1], c.minus_half[:, 0:1], ALU.pow)\
                .then_inc(self.rstd_done, 1)

    def tensor_turn(self, pe):
        c = self.c
        for d in range(DC):
            for t in range(NT):
                if d == 0:
                    self.wait_normed(pe, t + 1)
                last = pe.transpose(c.bank(d, P, at=t * P), c.xn[:, t, d * P:(d + 1) * P], c.ident[:])
            last.then_inc(self.turned, 1)

    def scalar_hi(self, act):
        c = self.c
        for d in range(DC):
            self.wait_turned(act, d + 1)
            act.activation(c.xT[0][:, d, :], c.bank(d), ACT.Copy).then_inc(self.hi_done, 1)

    def vector_lo(self, dve):
        c = self.c
        for d in range(DC):
            self.wait_hi(dve, d + 1)
            dve.tensor_tensor(c.xT[1][:, d, :], c.bank(d), c.xT[0][:, d, :], ALU.subtract)\
               .then_inc(self.lo_done, 1)

    def wait_parts(self, eng):
        self.wait_hi(eng, DC)
        self.wait_lo(eng, DC)


def setup_and_quant_product(nc, core, a):
    c = core
    KT = SC // P
    BY_VECTOR = 5
    ln = LayerNorm(c, turn=False)
    loaded_x, loaded_small, loaded_ctx, loaded_ctxT = (c.sem(n) for n in (
        "loaded_x", "loaded_small", "loaded_ctx", "loaded_ctxT"))
    ident_steps, gates_done, ctxT_hi, ctxT_lo = (c.sem(n) for n in (
        "ident_steps", "gates_done", "ctxT_hi_done", "ctxT_lo_done"))
    scal_done, q_chain, q1_done, q1_turned, q1T_done = (c.sem(n) for n in (
        "quant_scalars_done", "quant_chain", "q1_done", "q1_turned", "q1T_done"))
    q2_done, colsum_done, colsum_saved, prod_done, x_done = (c.sem(n) for n in (
        "q2_done", "colsum_done", "colsum_saved", "prod_done", "l0x_x_done"))
    inv_done, q2_done_pool, q2_chain = (c.sem(n) for n in ("inv_done", "q2_done_pool", "q2_chain"))
    with ExitStack() as st:
        ctx_nat = c.sb("context_rows", [P, NB * KT, D], ctx=st)
        ctxT_raw = c.sb("context_T_raw", [P, DC, NB * SC], ctx=st)
        q1 = c.sb("q1", [P, NT, D], BF16, st)
        q2 = c.sb("q2", [P, NB * KT, D], BF16, st)
        q1T = c.sb("q1_T", [P, DC, TOK], BF16, st)
        q1f = c.sb("q1_float", [P, D], F32, st)
        q2f = c.sb("q2_float", [P, NB * KT, D], F32, st)
        qs = c.sb("quant_scalars_in", [P, 4], F32, st)
        inv = c.sb("quant_inverse_scales", [P, 2], F32, st)
        cz = c.sb("quant_centres", [P, 2], F32, st)
        kcc = c.sb("quant_constant_term", [P, 1], F32, st)
        gss = c.sb("quant_out_scale", [P, 1], F32, st)
        rs = c.sb("q1_row_sums", [P, NT], F32, st)
        rs2 = c.sb("q1_row_terms", [P, NT], F32, st)
        csb = c.sb("q2_column_terms", [P, NB, D], F32, st)
        tmp = c.sb("l0x_sum", [P, NT, D], F32, st)
        gin = c.sb("gates_in", [P, 8], F32, st)

        def quantise_context(eng, link, k, done):
            v = q2f[:, k, :]
            link(eng.tensor_scalar(v, ctx_nat[:, k, :], inv[:, 1:2], qs[:, 3:4], ALU.mult, ALU.add))
            link(eng.tensor_scalar(v, v, 0.0, 255.0, ALU.max, ALU.min))
            eng.tensor_scalar(q2[:, k, :], v, ROUND, -ROUND - 128.0, ALU.add, ALU.add).then_inc(done, 1)

        with nc.Block() as block:

            @block.sync
            def _(sp):
                sp.dma_start(c.x[:], a["x"]).then_inc(loaded_x, 16)
                sp.dma_start(gin[:], a["gates"]).then_inc(loaded_small, 16)
                sp.dma_start(qs[:], a["quant"]).then_inc(loaded_small, 16)
                sp.dma_start(ctx_nat[:], a["context"]).then_inc(loaded_ctx, 16)
                sp.dma_start(ctxT_raw[:], a["context_T"]).then_inc(loaded_ctxT, 16)

            @block.gpsimd
            def _(pool):
                pool.memset(c.ident[:], 0.0).then_inc(ident_steps, 1)
                pool.memset(c.ones[:], 1.0).then_inc(ident_steps, 1)
                pool.memset(c.ones16[:], 1.0).then_inc(ident_steps, 1)
                pool.memset(c.minus_half[:], -0.5).then_inc(ident_steps, 1)
                pool.wait_ge(ident_steps, 1)
                pool.affine_select(out=c.ident[:], in_=c.ident[:], compare_op=ALU.not_equal, fill=1.0,
                                   base=0, pattern=[[-1, P]], channel_multiplier=1).then_inc(ident_steps, 1)
                pool.wait_ge(ident_steps, 5)
                pool.tensor_copy(c.ident16[:], c.ident[:]).then_inc(ident_steps, 1)
                ln.gpsimd(pool)
                pool.wait_ge(loaded_ctx, 16)
                pool.wait_ge(loaded_small, 32)
                pool.wait_ge(inv_done, 1)
                pool_link = Chain(pool, q2_chain)
                for k in range(BY_VECTOR, NB * KT):
                    quantise_context(pool, pool_link, k, q2_done_pool)
                for d in range(DC):
                    pool.wait_ge(ctxT_hi, d + 1)
                    pool.tensor_tensor(c.ctxT[1][:, d, :], ctxT_raw[:, d, :], c.ctxT[0][:, d, :],
                                       ALU.subtract).then_inc(ctxT_lo, 1)

            @block.scalar
            def _(act):
                act.wait_ge(loaded_small, 32)
                act.activation(c.gates[:], gin[:], ACT.Tanh).then_inc(gates_done, 1)
                for d in range(DC):
                    if d == 0:
                        act.wait_ge(loaded_ctxT, 16)
                    act.activation(c.ctxT[0][:, d, :], ctxT_raw[:, d, :], ACT.Copy).then_inc(ctxT_hi, 1)
                for d in range(DC):
                    act.wait_ge(q1_turned, d + 1)
                    act.activation(q1T[:, d, :], c.bank(d), ACT.Copy).then_inc(q1T_done, 1)

            @block.vector
            def _(dve):
                link = Chain(dve, q_chain)
                dve.wait_ge(loaded_x, 16)
                ln.vector_norm(dve)
                dve.wait_ge(loaded_small, 32)
                dve.reciprocal(inv[:], qs[:, 0:4:2]).then_inc(inv_done, 1)
                dve.wait_ge(inv_done, 1)
                link(dve.tensor_scalar(cz[:], qs[:, 1:4:2], -1.0, 128.0, ALU.mult, ALU.add))
                link(dve.tensor_scalar(kcc[:], cz[:, 0:1], cz[:, 1:2], float(SC), ALU.mult, ALU.mult))
                dve.wait_ge(gates_done, 1)
                link(dve.tensor_scalar(gss[:], qs[:, 0:1], qs[:, 2:3], c.gates[:, 0:1], ALU.mult, ALU.mult))
                for t in range(NT):
                    ln.wait_normed(dve, t + 1)
                    link(dve.tensor_scalar(q1f[:], c.xn[:, t, :], inv[:, 0:1], qs[:, 1:2], ALU.mult, ALU.add))
                    link(dve.tensor_scalar(q1f[:], q1f[:], 0.0, 255.0, ALU.max, ALU.min))
                    link(dve.tensor_scalar(q1f[:], q1f[:], ROUND, -ROUND, ALU.add, ALU.add))
                    dve.tensor_scalar(q1[:, t, :], q1f[:], -128.0, 0.0, ALU.add, ALU.add,
                                      accum_out=rs[:, t:t + 1]).then_inc(q1_done, 1)
                    dve.wait_ge(q1_done, t + 1)
                    link(dve.tensor_scalar(rs2[:, t:t + 1], rs[:, t:t + 1], cz[:, 1:2], None, ALU.mult))
                dve.wait_ge(loaded_ctx, 16)
                for k in range(BY_VECTOR):
                    quantise_context(dve, link, k, q2_done)
                for b in range(NB):
                    dve.wait_ge(colsum_done, b + 1)
                    dve.tensor_scalar(csb[:, b, :], c.bank(4 + b), cz[:, 0:1], kcc[:, 0:1],
                                      ALU.mult, ALU.add).then_inc(colsum_saved, 1)
                dve.wait_ge(colsum_saved, NB)
                for t in range(NT):
                    dve.wait_ge(prod_done, t + 1)
                    link(dve.scalar_tensor_tensor(tmp[:, t, :], c.bank(t), rs2[:, t:t + 1],
                                                  csb[:, t // 2, :], ALU.add, ALU.add))
                    dve.scalar_tensor_tensor(c.x[:, t, :], tmp[:, t, :], gss[:, 0:1], c.x[:, t, :],
                                             ALU.mult, ALU.add).then_inc(x_done, 1)

            @block.tensor
            def _(pe):
                pe.wait_ge(ident_steps, 6)
                for d in range(DC):
                    for t in range(NT):
                        if d == 0:
                            pe.wait_ge(q1_done, t + 1)
                        last = pe.matmul(c.bank(d, P, at=t * P), q1[:, t, d * P:(d + 1) * P], c.ident16[:],
                                         start=True, stop=True)
                    last.then_inc(q1_turned, 1)
                for b in range(NB):
                    for k in range(KT):
                        n = b * KT + k
                        by_vector = n < BY_VECTOR
                        pe.wait_ge(q2_done if by_vector else q2_done_pool, n + 1 - (0 if by_vector else BY_VECTOR))
                        last = pe.matmul(c.bank(4 + b), c.ones16[:], q2[:, b * KT + k, :],
                                         start=k == 0, stop=k == KT - 1)
                    last.then_inc(colsum_done, 1)
                pe.wait_ge(q1T_done, DC)
                for t in range(NT):
                    for k in range(KT):
                        last = pe.matmul(c.bank(t), q1T[:, k, t * P:(t + 1) * P], q2[:, (t // 2) * KT + k, :],
                                         start=k == 0, stop=k == KT - 1)
                    last.then_inc(prod_done, 1)


class Attention:

    UNITS = 16
    LAG = 2
    PV = LAG + 4
    WO = PV + 4
    LAST = WO + 15 - UNITS

    def __init__(self, core, tag, gate, heads, hd, latents, w_qkv, norm=False, rope=False, mask=False):
        self.w_qkv = w_qkv
        self.c, self.tag, self.gate, self.G, self.HD = core, tag, gate, heads, hd
        self.norm, self.rope, self.mask = norm, rope, mask
        self.NK = SC + (SQ if latents else 0)
        self.KB = self.NK // P
        self.TILES = -(-self.NK // BANK)
        self.PER = self.KB // self.TILES
        self.wo_bank = 7 if self.TILES == 2 else 1
        self.W = (2 + GROUP) * hd
        if norm:
            self.jobs = [("Q0", 0, 0), ("Q1", 1, 0), ("K0", 2, 0), ("K1", 3, 0), ("N", 4, 1), ("R0", 6, 0),
                         ("R1", 6, 1), ("V0", 7, 0), ("V1", 7, 1)]
        elif rope:
            self.jobs = [("K0", 0, 0), ("Q0", 2, 0), ("Q1", 4, 0), ("V0", 6, 0)]
        else:
            self.jobs = [("K0", 0, 0), ("Q0", 1, 0), ("K1", 2, 0), ("Q1", 3, 0), ("V0", 6, 0), ("V1", 7, 0)]
        names = self.names = [j[0] for j in self.jobs]
        self.pieces = ["Q0", "Q1", "K", "V"] if norm else ["K", "Q0", "Q1", "V"]
        self.split_at = (2, 3, 5, 9) if norm else (3, 4, 5, 9)
        self.by = {"raw": [n[0] == "V" or (n[0] in "KQ" and not rope) for n in names], "act": [n != "N" for n in names],
                   "dve": [(norm or rope) and n[0] != "V" for n in names], "pool": [n != "N" for n in names]}
        self.total = {e: sum(v) for e, v in self.by.items()}
        per_chunk = lambda v: v[:, 0:DC * self.W].rearrange("p (d n) -> p d n", d=DC)
        self.qkv_raw, self.qkv = per_chunk(core.qkv_raw), [per_chunk(v) for v in core.qkv]
        J, T, G = len(self.jobs), self.TILES, self.G
        self.rots = sum(1 for n in names if n[0] != "V") if rope else 0
        signals = {
            "qkv_loaded": 16 * G, "wo_loaded": 16 * G, "extra_loaded": 16 * (2 * norm + 4 * rope + mask),
            "qkv_hi": 4 * G, "qkv_lo": 4 * G, "wo_hi": 4 * G, "wo_lo": 4 * G,
            "job_made": 2 * G * J, "job_raw": 2 * G * self.total["raw"], "job_act": 2 * G * self.total["act"], "job_dve": 2 * G * self.total["dve"],
            "job_pool": 2 * G * self.total["pool"], "ms_done": 4 * G * norm, "pow_done": 2 * G * norm,
            "rot_summed": 2 * G * self.rots, "scored": 16 * G, "max_done": 16 * G, "bias_done": 16 * G,
            "exp_done": 16 * G, "recip_done": 16 * G, "prob_done": 16 * G, "turned": 16 * G * T,
            "pT_hi": 16 * G * T, "pT_lo": 16 * G * T, "pv_done": 4 * G, "o_hi": 4 * G, "o_lo": 4 * G,
            "wo_made": 8 * G, "x_done": 8 * G}
        self.before, found = {}, []
        for n, per_layer in signals.items():
            sem, before = core.attention_sems.get(n) or (core.sem(f"attn_{n}"), 0)
            self.before[sem.name] = before
            core.attention_sems[n] = (sem, before + per_layer)
            found.append(sem)
        (self.qkv_loaded, self.wo_loaded, self.extra_loaded, self.qkv_hi, self.qkv_lo, self.wo_hi, self.wo_lo,
         self.job_made, self.job_raw, self.job_act, self.job_dve, self.job_pool, self.ms_done, self.pow_done, self.rot_summed,
         self.scored, self.max_done, self.bias_done, self.exp_done, self.recip_done, self.prob_done, self.turned,
         self.pT_hi, self.pT_lo, self.pv_done, self.o_hi, self.o_lo, self.wo_made, self.x_done) = found

    def need(self, eng, sem, g, per, more):
        if isinstance(g, int):
            if per * g + more > 0:
                eng.wait_ge(sem, self.before[sem.name] + per * g + more)
        else:
            assert per + more > 0
            eng.wait_ge(sem, g * per + (more + self.before[sem.name]))


    def has(self, g, per, more):
        return not isinstance(g, int) or 0 <= per * g + more < per * self.G

    def score_cols(self, s):
        at = (s % 2) * 2 * BANK
        return at, at + self.NK

    def count(self, engine, j):
        return sum(self.by[engine][:j])

    def job_bank(self, j):
        return 3 if self.TILES == 1 and j % 2 else 7

    def through(self, engine, ahead, j):
        return 2 * self.total[engine], ahead * self.total[engine] + self.count(engine, j + 1)

    def back(self, kinds, ahead, j, n):
        while n:
            ahead, j = (ahead, j - 1) if j else (ahead - 1, len(self.jobs) - 1)
            n -= self.names[j][0] in kinds
        return ahead, j

    def raw(self, ahead, j):
        return self.job_sb[(ahead * self.total["raw"] + self.count("raw", j)) % 2]

    def slot_jobs(self, g, s, after):
        half = s // 8
        if isinstance(g, int) and (g >= self.G or (g == self.G - 1 and half == 1)):
            return []
        return [(j, n, half + 1) for j, (n, at, late) in enumerate(self.jobs) if at == s % 8 and late == after]

    def last_jobs(self, g, s):
        return self.slot_jobs(g, s - 1, 0) + self.slot_jobs(g, s - 1, 1) if s % 8 else []

    def job_cols(self, name):
        return {"K0": (0, SC), "K1": (SC, self.NK), "Q0": (0, 2), "Q1": (2, 4), "R0": (0, SC),
                "R1": (SC, self.NK), "V0": (0, SC // P), "V1": (SC // P, self.KB)}[name]


    def bank7_before(self, g, s, place, job=0):
        shift = 0
        while True:
            place -= 1
            if place < 0:
                s, place = s - 1, 2
            if s < 0:
                s, shift = s + self.UNITS, shift - 1
            at = g + shift if isinstance(g, int) else g
            if isinstance(g, int) and at < 0:
                j = len(self.jobs) - 1
                while self.job_bank(j) != self.job_bank(job):
                    j -= 1
                return "job", j, 0
            if place == 1:
                n = (s - self.WO) // 2
                if self.wo_bank == 7 and s % 2 == 0 and self.has(at, 8, n):
                    return "wo", 8 * shift + n
            else:
                jobs = self.slot_jobs(at, s, place // 2)
                if jobs and self.job_bank(jobs[-1][0]) == self.job_bank(job):
                    return "job", jobs[-1][0], jobs[-1][2] + 2 * shift

    def wait_bank7(self, pe, g, last):
        if last[0] == "wo":
            self.need(pe, self.x_done, g, 8, last[1] + 1)
            return
        j, ahead = last[1:]
        if self.names[j] == "N":
            self.need(pe, self.ms_done, g, 4, 2 * ahead + 1)
            return
        if not self.by["raw"][j]:
            self.need(pe, self.job_dve, g, *self.through("dve", ahead, j))
        else:
            self.need(pe, self.job_raw, g, *self.through("raw", ahead, j))

    def pe_job(self, pe, g, ahead, j, name, last7):
        c, b = self.c, ahead % 2
        HD = self.HD
        if last7:
            self.wait_bank7(pe, g, last7)
        if name[0] in "KVQ":
            part = 4 * (ahead // 2) + 1 + self.pieces.index(name if name[0] == "Q" else name[0])
            self.need(pe, self.qkv_hi, g, 4, part)
            self.need(pe, self.qkv_lo, g, 4, part)
        if name[0] == "R":
            self.need(pe, self.job_dve, g, 2 * self.total["dve"],
                      ahead * self.total["dve"] + self.count("dve", self.names.index("N") + 1))
        wk, wv, wq = ([w[:, :, i * HD:n * HD] for w in self.qkv] for i, n in ((0, 1), (1, 2), (2, 6)))
        if name[0] == "K":
            lo, hi = self.job_cols(name)
            src = c.ctxT if name == "K0" else c.xT
            base = b * SC if name == "K0" else b * SQ
            for d in range(DC):
                last = three(pe, c.bank(self.job_bank(j), hi - lo, HD), [w[:, d, :] for w in wk],
                             [x[:, d, base:base + hi - lo] for x in src], d == 0, d == DC - 1)
        elif name[0] == "Q":
            for i, h in enumerate(range(*self.job_cols(name))):
                for d in range(DC):
                    last = three(pe, c.bank(self.job_bank(j), SQ, HD, at=i * SQ), [w[:, d, h * HD:(h + 1) * HD] for w in wq],
                                 [x[:, d, b * SQ:(b + 1) * SQ] for x in c.xT], d == 0, d == DC - 1)
        elif name[0] == "V":
            for i, k in enumerate(range(*self.job_cols(name))):
                src = c.ctxT if name == "V0" else c.xT
                at = b * SC + k * P if name == "V0" else b * SQ + i * P
                for d in range(DC):
                    last = three(pe, c.bank(self.job_bank(j), HD, at=i * HD), [x[:, d, at:at + P] for x in src],
                                 [w[:, d, :] for w in wv], d == 0, d == DC - 1)
        elif name == "N":
            for sem, e in ((self.job_act, "act"), (self.job_pool, "pool")):
                self.need(pe, sem, g, 2 * self.total[e], ahead * self.total[e] + self.count(e, j))
            for i in range(self.KB + 8):
                sq, at = (self.k_sq, i) if i < self.KB else (self.q_sq, i - self.KB)
                for part in (1, 2):
                    last = pe.matmul(c.bank(self.job_bank(j), 1, at=i), sq[part][:, at * P:(at + 1) * P], c.ones16[:, 0:1],
                                     start=part == 1, stop=part == 2)
        else:
            lo, hi = self.job_cols(name)
            for i, k in enumerate(range(lo // P, hi // P)):
                for part in range(2):
                    last = pe.matmul(c.bank(self.job_bank(j), P, at=i * P), self.r_parts[part][:, k:k + 1].to_broadcast([P, P]),
                                     c.ident16[:], start=part == 0, stop=part == 1)
        last.then_inc(self.job_made, 1)

    def pe_turn(self, pe, g, s, i):
        c, U, u = self.c, self.UNITS, s - self.LAG
        if self.has(g, U, u):
            if i == 0:
                self.need(pe, self.prob_done, g, U, u + 1)
            m = u * self.TILES + i
            self.need(pe, self.pT_hi, g, U * self.TILES, m - 1)
            self.need(pe, self.pT_lo, g, U * self.TILES, m - 1)
            for k in range(self.PER):
                kb = i * self.PER + k
                last = pe.transpose(c.bank(4 + m % 2, P, at=k * P), self.E[u % 4][:, kb * P:(kb + 1) * P], c.ident[:])
            last.then_inc(self.turned, 1)

    def pe_slot(self, pe, g, s, live):
        c, U = self.c, self.UNITS
        HD = self.HD
        if live:
            b, t, h = s // 8, s % 8 // 4, s % 4
            if s % 8 == 0:
                for sem, e in ((self.job_act, "act"), (self.job_dve, "dve"), (self.job_pool, "pool")):
                    if e != "dve" or self.norm or self.rope:
                        self.need(pe, sem, g, 2 * self.total[e], b * self.total[e] + self.count(e, self.names.index("V0")))
            self.need(pe, self.max_done if self.mask else self.exp_done, g, U, s - 1)
            lo, hi = self.score_cols(s)
            q = [w[0:HD, h, t * P:(t + 1) * P] for w in self.qT[b]]
            cuts = [lo] + [m for m in (BANK, 3 * BANK) if lo < m < hi] + [hi]
            for u, v in zip(cuts, cuts[1:]):
                last = three(pe, c.ps[:, u:v], q, [w[0:HD, u - lo:v - lo] for w in self.kT[b]], True, True)
            last.then_inc(self.scored, 1)
        for j, name, ahead in self.slot_jobs(g, s, 0):
            self.pe_job(pe, g, ahead, j, name, self.bank7_before(g, s, 0, j))
        self.pe_turn(pe, g, s, 0)
        q, piece = (s - self.PV) // 4, (s - self.PV) % 4
        if self.has(g, 4, q):
            if piece == 0:
                for sem in (self.pT_hi, self.pT_lo):
                    self.need(pe, sem, g, U * self.TILES, 4 * (q + 1) * self.TILES)
                self.need(pe, self.o_hi, g, 4, q)
                self.need(pe, self.o_lo, g, 4, q)
                if q % 2 == 0:
                    for sem, e in ((self.job_act, "act"), (self.job_pool, "pool")):
                        self.need(pe, sem, g, 2 * self.total[e], (q // 2 + 1) * self.total[e])
            v, pT = self.v[q % 4 // 2], self.pT[q % 2]
            steps = [(k, x, y) for k in range(self.KB) for x, y in ((0, 0), (0, 1), (1, 0))]
            for i in range(piece * len(steps) // 4, (piece + 1) * len(steps) // 4):
                k, x, y = steps[i]
                last = pe.matmul(c.bank(6, BANK, HD), v[x][:, k, :], pT[y][:, k, :],
                                 start=i == 0, stop=i == len(steps) - 1)
            if piece == 3:
                last.then_inc(self.pv_done, 1)
        if self.TILES == 2:
            self.pe_turn(pe, g, s, 1)
        n = (s - self.WO) // 2
        if s % 2 == 0 and self.has(g, 8, n):
            if self.wo_bank == 7:
                self.wait_bank7(pe, g, self.bank7_before(g, s, 1))
            else:
                self.need(pe, self.x_done, g, 8, n)
            if n % 2 == 0:
                self.need(pe, self.o_hi, g, 4, n // 2 + 1)
                self.need(pe, self.o_lo, g, 4, n // 2 + 1)
            if n // 2 % 4 == 0:
                self.need(pe, self.wo_hi, g, 4, 4 * (n // 8) + 2 * (n % 2) + 2)
                self.need(pe, self.wo_lo, g, 4, 4 * (n // 8) + 2 * (n % 2) + 2)
            for h in (2 * (n % 2), 2 * (n % 2) + 1):
                last = three(pe, c.bank(self.wo_bank), [o[0:HD, h * P:(h + 1) * P] for o in self.oT[n // 2 % 2]],
                             [w[0:HD, h, :] for w in self.wo], h % 2 == 0, h % 2 == 1)
            last.then_inc(self.wo_made, 1)
        for j, name, ahead in self.slot_jobs(g, s, 1):
            self.pe_job(pe, g, ahead, j, name, self.bank7_before(g, s, 2, j))


    def piece_cols(self, part):
        HD = self.HD
        lo, hi = {"K": (0, 1), "V": (1, 2), "Q0": (2, 4), "Q1": (4, 6)}[self.pieces[part]]
        return slice(lo * HD, hi * HD)

    def split_parts(self, g, s):
        last = isinstance(g, int) and g >= self.G - 1
        return [part for part, at in enumerate(self.split_at) if at == s and not last]

    def act_split_qkv(self, act, g, more, part):
        if part == 0:
            self.need(act, self.qkv_loaded, g, 16, 16 * (more + 1))
        if more:
            j = max(i for i, n in enumerate(self.names) if n.startswith(self.pieces[part]))
            self.need(act, self.job_made, g, 2 * len(self.jobs), len(self.jobs) + j + 1)
        cols = self.piece_cols(part)
        act.activation(self.qkv[0][:, :, cols], self.qkv_raw[:, :, cols], ACT.Copy).then_inc(self.qkv_hi, 1)

    def derived(self, name):
        return name[0] == "R" or (self.rope and name[0] in "KQ")

    def act_raw(self, act, g, ahead, j, name):
        if not self.by["raw"][j]:
            return
        self.need(act, self.job_made, g, 2 * len(self.jobs), ahead * len(self.jobs) + j + 1)
        ahead2, j2 = self.back("V" if self.rope else "KQV", ahead, j, 2)
        for sem, e in ((self.job_dve, "dve"), (self.job_pool, "pool")):
            if self.by[e][j2]:
                self.need(act, sem, g, *self.through(e, ahead2, j2))
        lo, hi = self.job_cols(name)
        n, parts = {"K": (hi - lo, self.HD), "Q": (BANK, self.HD), "V": ((hi - lo) * self.HD, P)}[name[0]]
        act.activation(self.raw(ahead, j)[0:parts, 0:n], self.c.bank(self.job_bank(j), n, parts), ACT.Copy).then_inc(self.job_raw, 1)

    def act_job(self, act, g, ahead, j, name):
        c, b, HD = self.c, ahead % 2, self.HD
        if name == "N":
            return
        if name[0] == "R":
            lo, hi = self.job_cols(name)
            self.need(act, self.job_dve, g, 2 * self.total["dve"],
                 ahead * self.total["dve"] + self.count("dve", j + 1))
            last = act.activation(self.kT[b][0][:, lo:hi], self.k_raw[:, lo:hi], ACT.Copy)
        elif self.rope and name[0] != "V":
            r = ahead * self.rots + self.count("dve", j)
            self.need(act, self.rot_summed, g, 2 * self.rots, r + 1)
            last = act.activation(self.target(name, b, 0), self.rot[r % 2][:], ACT.Copy)
        else:
            raw = self.raw(ahead, j)
            self.need(act, self.job_raw, g, *self.through("raw", ahead, j))
            if name[0] == "K":
                lo, hi = self.job_cols(name)
                if self.norm:
                    act.activation(self.k_sq[0][:, lo:hi], raw[:, 0:hi - lo], ACT.Square)
                    last = act.activation(self.k_sq[1][:, lo:hi], raw[:, 0:hi - lo], ACT.Square)
                else:
                    last = act.activation(self.kT[b][0][0:HD, lo:hi], raw[0:HD, 0:hi - lo], ACT.Copy)
            elif name[0] == "Q":
                if self.norm:
                    lo, hi = self.job_cols(name)
                    act.activation(self.target(name, b, 0), raw[:], ACT.Copy, scale=self.qw[:, 0:1])
                    act.activation(self.q_sq[0][:, lo * SQ:hi * SQ], raw[:], ACT.Square)
                    last = act.activation(self.q_sq[1][:, lo * SQ:hi * SQ], raw[:], ACT.Square)
                else:
                    last = act.activation(self.target(name, b, 0), raw[0:HD, :], ACT.Copy)
            else:
                lo, hi = self.job_cols(name)
                last = act.activation(self.target(name, b, 0), raw[:, 0:(hi - lo) * HD], ACT.Copy)
        last.then_inc(self.job_act, 1)

    def target(self, name, b, part):
        lo, hi = self.job_cols(name)
        if name[0] == "K":
            return self.kT[b][part][0:self.HD, lo:hi]
        if name[0] == "Q":
            return self.qT[b][part][0:self.HD, lo:hi, :].rearrange("p h q -> p (h q)")
        return self.v[b][part][:, lo:hi, :].rearrange("p k d -> p (k d)")

    def act_turned(self, act, g, s, i):
        U, u = self.UNITS, s - self.LAG
        if self.has(g, U, u):
            q, h = u // 4, u % 4
            m = u * self.TILES + i
            self.need(act, self.turned, g, U * self.TILES, m + 1)
            if h == 0 and i == 0:
                self.need(act, self.pv_done, g, 4, q - 1)
            act.activation(self.pT[q % 2][0][:, i * self.PER:(i + 1) * self.PER, h * P:(h + 1) * P],
                           self.c.bank(4 + m % 2, self.PER * P).rearrange("p (k q) -> p k q", q=P),
                           ACT.Copy).then_inc(self.pT_hi, 1)

    def act_slot(self, act, g, s, live):
        c, U, HD = self.c, self.UNITS, self.HD
        if live:
            b, t, h = s // 8, s % 8 // 4, s % 4
            self.need(act, self.bias_done, g, U, s + 1)
            lo, hi = self.score_cols(s)
            E = self.E[s % 4]
            if self.norm:
                scale = self.q_scale[b][:, h * 2 + t:h * 2 + t + 1]
            else:
                scale = 1.0 if self.mask else float(HD) ** -0.5
            act.activation(E[:], E[:] if self.mask else c.ps[:, lo:hi], ACT.Exp, bias=self.bias[:, s:s + 1],
                           scale=scale, accum_out=self.sums[:, s:s + 1]).then_inc(self.exp_done, 1)
        for j, name, ahead in self.slot_jobs(g, s, 0):
            self.act_raw(act, g, ahead, j, name)
        for j, name, ahead in self.last_jobs(g, s):
            if self.norm and self.derived(name):
                self.act_job(act, g, ahead, j, name)
        self.act_turned(act, g, s, 0)
        if live and 7 <= s < 7 + GROUP:
            h = s - 7
            if h == 0:
                self.need(act, self.wo_loaded, g, 16, 16)
            if h % 2 == 0:
                self.need(act, self.wo_made, g, 8, h // 2 - 1)
            act.activation(self.wo[0][0:HD, h, :], self.wo_raw[0:HD, h, :], ACT.Copy).then_inc(self.wo_hi, 1)
        q = (s - self.WO + 1) // 4
        if (s - self.WO + 1) % 4 == 0 and self.has(g, 4, q):
            self.need(act, self.pv_done, g, 4, q + 1)
            self.need(act, self.wo_made, g, 8, 2 * (q - 1))
            act.activation(self.oT[q % 2][0][0:HD, :], c.bank(6, BANK, HD), ACT.Copy).then_inc(self.o_hi, 1)
        if self.TILES == 2:
            self.act_turned(act, g, s, 1)
        for j, name, ahead in self.slot_jobs(g, s, 1):
            self.act_raw(act, g, ahead, j, name)
        for j, name, ahead in self.last_jobs(g, s):
            if self.rope and self.derived(name):
                self.act_job(act, g, ahead, j, name)
        for j, name, ahead in self.slot_jobs(g, s, 0) + self.slot_jobs(g, s, 1):
            if not self.derived(name):
                self.act_job(act, g, ahead, j, name)
        for part in self.split_parts(g, s):
            self.act_split_qkv(act, g, 1, part)


    def dve_job(self, dve, g, ahead, j, name, part=None):
        c, b, HD = self.c, ahead % 2, self.HD
        if not self.by["dve"][j]:
            return
        made = (2 * len(self.jobs), ahead * len(self.jobs) + j + 1)
        act_counts = (2 * self.total["act"], ahead * self.total["act"] + self.count("act", j + 1))
        if name == "N":
            if part == 0:
                self.need(dve, self.job_made, g, *made)
                dve.tensor_scalar(self.ms[:], c.bank(7, self.KB + 8), 1.0 / HD, 1e-6, ALU.mult, ALU.add)\
                   .then_inc(self.ms_done, 1)
                return
            self.need(dve, self.pow_done, g, 2, ahead + 1)
            dve.tensor_copy(self.r_parts[0][:], self.r[:, 0:self.KB]).then_inc(self.ms_done, 1)
            dve.tensor_scalar(self.q_scale[b][:], self.r[:, self.KB:], float(HD) ** -0.5, None, ALU.mult)
            dve.tensor_scalar(self.q_scale_neg[b][:], self.r[:, self.KB:], -float(HD) ** -0.5, None, ALU.mult)
            self.need(dve, self.ms_done, g, 4, 2 * ahead + 2)
            last = dve.tensor_tensor(self.r_parts[1][:], self.r[:, 0:self.KB], self.r_parts[0][:], ALU.subtract)
        elif name[0] == "R":
            lo, hi = self.job_cols(name)
            self.need(dve, self.job_made, g, *made)
            last = dve.tensor_tensor(self.k_raw[:, lo:hi], self.k_raw[:, lo:hi], c.bank(7, hi - lo), ALU.mult)
        elif self.rope:
            r = ahead * self.rots + self.count("dve", j)
            H = HD // 2
            cos, sin = (self.k_cos, self.k_sin) if name[0] == "K" else (self.q_cos, self.q_sin)
            self.need(dve, self.job_made, g, *made)
            self.need(dve, self.job_pool, g, *self.through("pool", *self.back("KQ", ahead, j, 2)))
            made = c.bank(self.job_bank(j))
            dve.tensor_tensor(self.rot[r % 2][:], made, cos[:], ALU.mult)
            dve.tensor_tensor(self.rot2[r % 2][0:H, :], made[H:HD, :], sin[H:HD, :], ALU.mult)
            last = dve.tensor_tensor(self.rot2[r % 2][H:HD, :], made[0:H, :], sin[0:H, :], ALU.mult)
        elif name[0] == "K":
            lo, hi = self.job_cols(name)
            self.need(dve, self.job_raw, g, *self.through("raw", ahead, j))
            self.need(dve, self.job_pool, g, *self.through("pool", ahead - 1, self.names.index("R1")))
            last = dve.tensor_scalar(self.k_raw[:, lo:hi], self.raw(ahead, j)[:, 0:hi - lo], self.kw[:, 0:1], None,
                                     ALU.mult)
        else:
            self.need(dve, self.job_act, g, *act_counts)
            last = dve.scalar_tensor_tensor(self.target(name, b, 1), self.raw(ahead, j)[:], self.qw[:, 0:1],
                                            self.target(name, b, 0), ALU.mult, ALU.subtract)
        last.then_inc(self.job_dve, 1)

    def dve_turned(self, dve, g, s, i):
        U, u = self.UNITS, s - self.LAG
        if self.has(g, U, u):
            q, h = u // 4, u % 4
            m = u * self.TILES + i
            self.need(dve, self.pT_hi, g, U * self.TILES, m + 1)
            blocks = slice(i * self.PER, (i + 1) * self.PER)
            dve.tensor_tensor(self.pT[q % 2][1][:, blocks, h * P:(h + 1) * P],
                              self.c.bank(4 + m % 2, self.PER * P).rearrange("p (k q) -> p k q", q=P),
                              self.pT[q % 2][0][:, blocks, h * P:(h + 1) * P],
                              ALU.subtract).then_inc(self.pT_lo, 1)

    def dve_add(self, dve, g, s):
        c, n = self.c, (s - self.WO) // 2
        if s % 2 == 0 and self.has(g, 8, n):
            t = n // 2 % 4
            self.need(dve, self.wo_made, g, 8, n + 1)
            dve.scalar_tensor_tensor(c.x[:, t, :], c.bank(self.wo_bank), c.gates[:, self.gate:self.gate + 1],
                                     c.x[:, t, :], ALU.mult, ALU.add).then_inc(self.x_done, 1)

    def dve_slot(self, dve, g, s, live):
        c, U, HD = self.c, self.UNITS, self.HD
        if live:
            b, t, h = s // 8, s % 8 // 4, s % 4
            lo, hi = self.score_cols(s)
            self.need(dve, self.scored, g, U, s + 1)
            top = self.top[:, s:s + 1]
            if self.mask:
                dve.memset(self.bias[:, s:s + 1], 0.0)
                dve.tensor_tensor_reduce(out=self.E[s % 4][:], in0=c.ps[:, lo:hi], in1=self.mask_sb[:, 2 * b + t, :],
                                         scale=1.0, scalar=-3.0e38, op0=ALU.add, op1=ALU.max,
                                         accum_out=top).then_inc(self.max_done, 1)
            else:
                dve.reduce_max(top, c.ps[:, lo:hi], AX.X).then_inc(self.max_done, 1)
            self.need(dve, self.max_done, g, U, s + 1)
            by = self.q_scale_neg[b][:, h * 2 + t:h * 2 + t + 1] if self.norm else \
                (-1.0 if self.mask else -float(HD) ** -0.5)
            dve.tensor_scalar(self.bias[:, s:s + 1], top, by, None, ALU.mult).then_inc(self.bias_done, 1)
        for j, name, ahead in self.slot_jobs(g, s, 0):
            if name[0] in "NR":
                self.dve_job(dve, g, ahead, j, name, 0)
        if self.has(g, U, s - 1):
            u = (s - 1) % U
            self.need(dve, self.exp_done, g, U, s)
            dve.reciprocal(self.recip[:, u:u + 1], self.sums[:, u:u + 1]).then_inc(self.recip_done, 1)
            self.need(dve, self.recip_done, g, U, s)
            dve.tensor_scalar(self.E[u % 4][:], self.E[u % 4][:], self.recip[:, u:u + 1], None, ALU.mult)\
               .then_inc(self.prob_done, 1)
        for j, name, ahead in self.last_jobs(g, s):
            if self.norm and name[0] in "KQ":
                self.dve_job(dve, g, ahead, j, name, 0)
        for j, name, ahead in self.slot_jobs(g, s, 0):
            if self.rope and name[0] in "KQ":
                self.dve_job(dve, g, ahead, j, name, 0)
        early = self.norm and not self.slot_jobs(g, s, 0)
        if early:
            self.dve_add(dve, g, s)
        self.dve_turned(dve, g, s, 0)
        q = (s - self.WO + 1) // 4
        if (s - self.WO + 1) % 4 == 0 and self.has(g, 4, q):
            self.need(dve, self.o_hi, g, 4, q + 1)
            dve.tensor_tensor(self.oT[q % 2][1][0:HD, :], c.bank(6, BANK, HD), self.oT[q % 2][0][0:HD, :],
                              ALU.subtract).then_inc(self.o_lo, 1)
        if self.TILES == 2:
            self.dve_turned(dve, g, s, 1)
        if not early:
            self.dve_add(dve, g, s)
        for j, name, ahead in self.last_jobs(g, s):
            if name == "N":
                self.dve_job(dve, g, ahead, j, name, 1)
        for j, name, ahead in self.slot_jobs(g, s, 1):
            if name == "N" or name[0] == "R":
                self.dve_job(dve, g, ahead, j, name, 0)


    def pool_split_qkv(self, pool, g, more, part):
        cols = self.piece_cols(part)
        self.need(pool, self.qkv_hi, g, 4, 4 * more + part + 1)
        pool.tensor_tensor(self.qkv[1][:, :, cols], self.qkv_raw[:, :, cols], self.qkv[0][:, :, cols],
                           ALU.subtract).then_inc(self.qkv_lo, 1)

    def pool_job(self, pool, g, ahead, j, name):
        b, HD = ahead % 2, self.HD
        if name == "N":
            self.need(pool, self.ms_done, g, 4, 2 * ahead + 1)
            pool.tensor_tensor(self.r[:], self.ms[:], self.c.minus_half[:, 0:self.KB + 8], ALU.pow)\
                .then_inc(self.pow_done, 1)
            return
        dst = None
        if name[0] == "R":
            src = self.k_raw[:, slice(*self.job_cols(name))]
            name = "K" + name[1]
        elif self.norm and name[0] in "KQ":
            lo, hi = self.job_cols(name)
            sq, cols = (self.k_sq, slice(lo, hi)) if name[0] == "K" else (self.q_sq, slice(lo * SQ, hi * SQ))
            dst, src = (sq[2][:, cols], sq[1][:, cols]), sq[0][:, cols]
        elif self.rope and name[0] in "KQ":
            r = ahead * self.rots + self.count("dve", j)
            self.need(pool, self.job_dve, g, *self.through("dve", ahead, j))
            src = self.rot[r % 2][:]
            pool.tensor_tensor(src, src, self.rot2[r % 2][:], ALU.add).then_inc(self.rot_summed, 1)
        else:
            lo, hi = self.job_cols(name)
            n, parts = {"K": (hi - lo, HD), "Q": (BANK, HD), "V": ((hi - lo) * HD, P)}[name[0]]
            src = self.raw(ahead, j)[0:parts, 0:n]
        self.need(pool, self.job_act, g, *self.through("act", ahead, j))
        low, high = dst or (self.target(name, b, 1), self.target(name, b, 0))
        pool.tensor_tensor(low, src, high, ALU.subtract).then_inc(self.job_pool, 1)

    def pool_slot(self, pool, g, s, live):
        for j, name, ahead in self.slot_jobs(g, s, 0):
            self.pool_job(pool, g, ahead, j, name)
        if live and 7 <= s < 7 + GROUP:
            h = s - 7
            self.need(pool, self.wo_hi, g, 4, h + 1)
            pool.tensor_tensor(self.wo[1][0:self.HD, h, :], self.wo_raw[0:self.HD, h, :],
                               self.wo[0][0:self.HD, h, :], ALU.subtract).then_inc(self.wo_lo, 1)
        for j, name, ahead in self.slot_jobs(g, s, 1):
            self.pool_job(pool, g, ahead, j, name)
        for part in self.split_parts(g, s):
            self.pool_split_qkv(pool, g, 1, part)


    def rounds(self, eng, slot):
        for s in range(self.UNITS):
            slot(eng, 0, s, True)
        with eng.Fori(1, self.G - 1) as g:
            for s in range(self.UNITS):
                slot(eng, g, s, True)
        for s in range(self.UNITS):
            slot(eng, self.G - 1, s, True)
        for s in range(self.LAST):
            slot(eng, self.G, s, False)


    def load_qkv(self, sp, at):
        sp.dma_start(self.c.qkv_raw[:, 0:DC * self.W], self.w_qkv[:, at]).then_inc(self.qkv_loaded, 16)

    def first_load(self, sp):
        self.load_qkv(sp, slice(0, DC * self.W))

    def first_hi(self, act):
        for part in range(4):
            self.act_split_qkv(act, 0, 0, part)

    def first_lo(self, pool):
        for part in range(4):
            self.pool_split_qkv(pool, 0, 0, part)

    def run(self, w_o, extra):
        c, HD, ln = self.c, self.HD, LayerNorm(self.c)
        with ExitStack() as st:
            sb = lambda name, shape, dt=F32: c.sb(f"{self.tag}_{name}", shape, dt, st)
            pair = lambda name, shape: [sb(f"{name}_{p}", shape, BF16) for p in ("hi", "lo")]
            self.wo_raw, self.wo = sb("wo_raw", [P, GROUP, D]), pair("wo", [P, GROUP, D])
            self.kT = [pair(f"kT{b}", [P, self.NK]) for b in range(NB)]
            self.qT = [pair(f"qT{b}", [P, GROUP, SQ]) for b in range(NB)]
            self.v = [pair(f"v{b}", [P, self.KB, HD]) for b in range(NB)]
            self.job_sb = [sb(f"job{i}", [P, BANK]) for i in range(2)]
            self.E = [sb(f"probs{i}", [P, self.NK]) for i in range(4)]
            self.pT = [pair(f"pT{i}", [P, self.KB, GROUP * P]) for i in range(2)]
            self.oT = [pair(f"oT{i}", [P, GROUP * P]) for i in range(2)]
            self.top, self.bias, self.sums, self.recip = (
                sb(n, [P, self.UNITS]) for n in ("score_max", "exp_bias", "exp_sums", "exp_recip"))
            loads = []
            if self.norm:
                self.k_sq, self.q_sq = ([sb(n, [P, w])] + pair(n, [P, w]) for n, w in (
                    ("k_sq", self.NK), ("q_sq", GROUP * SQ)))
                self.k_raw, self.r_parts = sb("k_raw", [P, self.NK]), pair("inv_rms", [P, self.KB])
                self.ms, self.r = sb("mean_sq", [P, self.KB + 8]), sb("inv_rms", [P, self.KB + 8])
                self.q_scale = [sb(f"q_scale{b}", [P, 8]) for b in range(NB)]
                self.q_scale_neg = [sb(f"q_scale_neg{b}", [P, 8]) for b in range(NB)]
                self.qw, self.kw = sb("q_norm_w", [P, 1]), sb("k_norm_w", [P, 1])
                loads = [(self.qw, "qw"), (self.kw, "kw")]
            if self.rope:
                self.rot, self.rot2 = ([sb(f"{n}{i}", [P, BANK]) for i in range(2)] for n in ("rot", "rot_swap"))
                self.k_cos, self.k_sin, self.q_cos, self.q_sin = (
                    sb(n, [P, BANK]) for n in ("k_cos", "k_sin", "q_cos", "q_sin"))
                loads = [(self.k_cos, "k_cos"), (self.k_sin, "k_sin"), (self.q_cos, "q_cos"), (self.q_sin, "q_sin")]
            if self.mask:
                self.mask_sb = sb("mask", [P, NT, self.NK])
                loads.append((self.mask_sb, "mask"))
            WQKV, WO = DC * self.W, GROUP * D
            with c.nc.Block() as block:

                @block.sync
                def _(sp):
                    def load_wo(at):
                        sp.dma_start(self.wo_raw[0:HD].rearrange("p h n -> p (h n)"), w_o[:, at])\
                          .then_inc(self.wo_loaded, 16)

                    for dst, name in loads:
                        sp.dma_start(dst[:], extra[name]).then_inc(self.extra_loaded, 16)
                    self.load_qkv(sp, slice(WQKV, 2 * WQKV))
                    load_wo(slice(0, WO))
                    with sp.Fori(1, self.G - 1) as g:
                        self.need(sp, self.qkv_lo, g, 4, 4)
                        self.load_qkv(sp, bass.ds(g * WQKV + WQKV, WQKV))
                        self.need(sp, self.wo_lo, g, 4, 0)
                        load_wo(bass.ds(g * WO, WO))
                    self.need(sp, self.wo_lo, self.G - 1, 4, 0)
                    load_wo(slice((self.G - 1) * WO, self.G * WO))

                @block.gpsimd
                def _(pool):
                    ln.gpsimd(pool)
                    for j, (name, *_) in enumerate(self.jobs):
                        self.pool_job(pool, 0, 0, j, name)
                    self.rounds(pool, self.pool_slot)

                @block.scalar
                def _(act):
                    ln.scalar_hi(act)
                    if loads:
                        self.need(act, self.extra_loaded, 0, 0, 16 * len(loads))
                    for j, (name, *_) in enumerate(self.jobs):
                        self.act_raw(act, 0, 0, j, name)
                        self.act_job(act, 0, 0, j, name)
                    self.rounds(act, self.act_slot)

                @block.vector
                def _(dve):
                    ln.vector_norm(dve)
                    ln.vector_lo(dve)
                    if loads:
                        self.need(dve, self.extra_loaded, 0, 0, 16 * len(loads))
                    for j, (name, *_) in enumerate(self.jobs):
                        self.dve_job(dve, 0, 0, j, name, 0)
                        if name == "N":
                            self.dve_job(dve, 0, 0, j, name, 1)
                    self.rounds(dve, self.dve_slot)

                @block.tensor
                def _(pe):
                    if self.names[0] != "K0":
                        ln.tensor_turn(pe)
                        ln.wait_parts(pe)
                    for j, (name, *_) in enumerate(self.jobs):
                        before = [i for i in range(j) if self.job_bank(i) == self.job_bank(j)]
                        self.pe_job(pe, 0, 0, j, name, ("job", before[-1], 0) if before else None)
                        if name == self.names[0] == "K0":
                            ln.tensor_turn(pe)
                            ln.wait_parts(pe)
                    self.rounds(pe, self.pe_slot)


class Pieces:

    def __init__(self, core, tag, st):
        self.c, self.tag, self.st, self.items = core, tag, st, []
        self.hi_done, self.lo_done = core.sem(f"{tag}_w_hi"), core.sem(f"{tag}_w_lo")

    def add(self, name, shape, raw=None):
        if raw is None:
            raw = self.c.sb(f"{self.tag}_{name}_raw", shape, F32, self.st)
        hi, lo = (self.c.sb(f"{self.tag}_{name}_{p}", shape, BF16, self.st) for p in ("hi", "lo"))
        self.items.append((raw, hi, lo, self.c.sem(f"{self.tag}_{name}_loaded")))
        return raw, [hi, lo]

    def load(self, sp, i, src):
        sp.dma_start(self.items[i][0][:], src).then_inc(self.items[i][3], 16)

    def scalar_hi(self, act, i):
        raw, hi, _, loaded = self.items[i]
        act.wait_ge(loaded, 16)
        act.activation(hi[:], raw[:], ACT.Copy).then_inc(self.hi_done, 1)

    def low(self, eng, i, done=None):
        raw, hi, lo, _ = self.items[i]
        eng.wait_ge(self.hi_done, i + 1)
        eng.tensor_tensor(lo[:], raw[:], hi[:], ALU.subtract).then_inc(done or self.lo_done, 1)

    def wait(self, pe, i):
        pe.wait_ge(self.hi_done, i + 1)
        pe.wait_ge(self.lo_done, i + 1)


def lora_experts(nc, core, a, after):
    c, E, R, K = core, 8, 64, 128
    ln = LayerNorm(c)
    S = lambda n: c.sem(f"l0f_{n}")
    small, mean_done, chain_sem, q_done, q_rep, score_done, bias_done, exp_done, coef_done = (S(n) for n in (
        "small_loaded", "mean_done", "chain", "q_done", "q_repeated", "scores_done", "bias_done", "exp_done",
        "coef_done"))
    h_done, h_scaled, h_hi, h_lo, out_done, x_done = (S(n) for n in (
        "h_done", "h_scaled", "h_hi", "h_lo", "out_done", "x_done"))
    with ExitStack() as st:
        w = Pieces(c, "l0f", st)
        _, down = w.add("down", [P, DC, E * R])
        _, worg = w.add("worg", [P, DC, D])
        _, up = w.add("up", [P, E * R // P, D])
        sb = lambda name, shape, dt=F32: c.sb(f"l0f_{name}", shape, dt, st)
        wq, keys = sb("wq", [P, DC, K]), sb("keys", [K, E])
        xm, q_all, coef = sb("x_mean", [P, DC, NB]), sb("q_all", [K, NB, P]), sb("coef", [P, NB, E])
        top, bias, sums, rec = (sb(n, [P, NB]) for n in ("top", "bias", "sums", "recip"))
        rowc = sb("row_coef", [P, NB, E * R // P])
        hf = sb("h_float", [P, E * R // P, TOK])
        hT = [sb(f"h_{p}", [P, E * R // P, TOK], BF16) for p in ("hi", "lo")]
        M = E * R // P
        with nc.Block() as block:

            @block.sync
            def _(sp):
                w.load(sp, 0, a["l0_down"])
                sp.dma_start(wq[:], a["l0_wq"]).then_inc(small, 16)
                sp.dma_start(keys[:], a["l0_keys"]).then_inc(small, 16)
                w.load(sp, 1, a["l0_worg"])
                w.load(sp, 2, a["l0_up"])
                after.first_load(sp)

            @block.gpsimd
            def _(pool):
                ln.gpsimd(pool)
                for i in range(3):
                    w.low(pool, i)
                for m in range(M):
                    pool.wait_ge(h_hi, m + 1)
                    pool.tensor_tensor(hT[1][:, m, :], hf[:, m, :], hT[0][:, m, :], ALU.subtract).then_inc(h_lo, 1)
                after.first_lo(pool)

            @block.scalar
            def _(act):
                w.scalar_hi(act, 0)
                ln.scalar_hi(act)
                for i in (1, 2):
                    w.scalar_hi(act, i)
                for b in range(NB):
                    act.wait_ge(bias_done, 1)
                    act.activation(coef[:, b, :], c.bank(5, E, at=b * E), ACT.Exp, bias=bias[:, b:b + 1],
                                   scale=float(K) ** -0.5, accum_out=sums[:, b:b + 1]).then_inc(exp_done, 1)
                for m in range(M):
                    act.wait_ge(h_scaled, m + 1)
                    act.activation(hT[0][:, m, :], hf[:, m, :], ACT.Copy).then_inc(h_hi, 1)
                after.first_hi(act)

            @block.vector
            def _(dve):
                link = Chain(dve, chain_sem)
                ln.vector_norm(dve)
                ln.vector_lo(dve)
                for d in range(DC):
                    dve.reduce_sum(xm[:, d, :], c.bank(d).rearrange("p (b s) -> p b s", b=NB), AX.X)\
                       .then_inc(mean_done, 1)
                dve.wait_ge(q_done, 1)
                for b in range(NB):
                    dve.tensor_scalar(q_all[:, b, :], c.bank(4, 1, at=b).to_broadcast([K, P]), 1.0 / SQ, None,
                                      ALU.mult).then_inc(q_rep, 1)
                dve.wait_ge(score_done, 1)
                link(dve.reduce_max(top[:], c.bank(5, NB * E).rearrange("p (b e) -> p b e", b=NB), AX.X))
                dve.tensor_scalar(bias[:], top[:], -float(K) ** -0.5, None, ALU.mult).then_inc(bias_done, 1)
                dve.wait_ge(exp_done, NB)
                link(dve.reciprocal(rec[:], sums[:]))
                link(dve.tensor_tensor(coef[:], coef[:], rec[:].unsqueeze(2).to_broadcast([P, NB, E]), ALU.mult))
                dve.tensor_copy(rowc[0:R], coef[0:R, :, 0:E:2]).then_inc(coef_done, 1)
                dve.tensor_copy(rowc[R:P], coef[R:P, :, 1:E:2]).then_inc(coef_done, 1)
                dve.wait_ge(coef_done, 2)
                for m in range(M):
                    dve.wait_ge(h_done, m + 1)
                    for b in range(NB):
                        last = dve.tensor_scalar(hf[:, m, b * SQ:(b + 1) * SQ], c.bank(m, SQ, at=b * SQ),
                                                 rowc[:, b, m:m + 1], None, ALU.mult)
                    last.then_inc(h_scaled, 1)
                for t in range(NT):
                    dve.wait_ge(out_done, t + 1)
                    dve.scalar_tensor_tensor(c.x[:, t, :], c.bank(4 + t), c.gates[:, 1:2], c.x[:, t, :],
                                             ALU.mult, ALU.add).then_inc(x_done, 1)

            @block.tensor
            def _(pe):
                ln.tensor_turn(pe)
                ln.wait_parts(pe)
                pe.wait_ge(mean_done, DC)
                pe.wait_ge(small, 32)
                for d in range(DC):
                    last = pe.matmul(c.bank(4, NB), wq[:, d, :], xm[:, d, :], start=d == 0, stop=d == DC - 1)
                last.then_inc(q_done, 1)
                w.wait(pe, 0)
                for m in range(M):
                    for d in range(DC):
                        last = three(pe, c.bank(m), [v[:, d, m * P:(m + 1) * P] for v in down],
                                     [v[:, d, :] for v in c.xT], d == 0, d == DC - 1)
                    last.then_inc(h_done, 1)
                    if m == 0:
                        pe.wait_ge(q_rep, NB)
                        for b in range(NB):
                            last = pe.matmul(c.bank(5, E, at=b * E), q_all[:, b, :], keys[:], start=True, stop=True)
                        last.then_inc(score_done, 1)
                pe.wait_ge(coef_done, 2)
                w.wait(pe, 1)
                for t in range(NT):
                    for d in range(DC):
                        three(pe, c.bank(4 + t), [v[:, d, t * P:(t + 1) * P] for v in c.xT],
                              [v[:, d, :] for v in worg], d == 0, False)
                w.wait(pe, 2)
                pe.wait_ge(h_lo, M)
                for t in range(NT):
                    for m in range(M):
                        last = three(pe, c.bank(4 + t), [v[:, m, t * P:(t + 1) * P] for v in hT],
                                     [v[:, m, :] for v in up], False, m == M - 1)
                    last.then_inc(out_done, 1)


def sparse_rows(nc, core, a, after):
    c, F, SP_, RANK = core, 1792, 32, 16
    BL, M = F // SP_, F // P
    ln = LayerNorm(c)
    S = lambda n: c.sem(f"l1f_{n}")
    small, zeroed, xf_done, u_done, u_saved, inter_done, chain_sem, eq_done, key_done, mask_done = (S(n) for n in (
        "small_loaded", "zeroed", "x_float_done", "u_done", "u_saved", "inter_done", "chain", "eq_done",
        "key_done", "mask_done"))
    mT_done, h_done, h_saved, h_masked, h_hi, h_lo, out_used, out_done, x_done = (S(n) for n in (
        "mask_turned", "h_done", "h_saved", "h_masked", "h_hi", "h_lo", "out_used", "out_done", "x_done"))
    with ExitStack() as st:
        w = Pieces(c, "l1f", st)
        lo_by_vector = S("w_lo_by_vector")
        sb = lambda name, shape, dt=F32: c.sb(f"l1f_{name}", shape, dt, st)
        w1_raw = sb("w1_raw", [P, DC * F])
        w1 = [w.add(f"w1_{d}", [P, F], w1_raw[:, d * F:(d + 1) * F])[1] for d in range(DC)]
        h_all = w1_raw[:].rearrange("p (m t) -> p m t", t=TOK)
        w2_raw = sb("w2_raw", [P, M // 2, D])
        w2 = [w.add(f"w2_{i}", [P, M // 2, D], w2_raw)[1] for i in range(2)]
        c1, c2 = sb("c1", [P, DC, P]), sb("c2", [P, F])
        u = sb("u", [P, TOK])
        mx, eq, key = sb("block_max", [P, BL]), sb("at_max", [P, BL, SP_], BF16), sb("key", [P, BL, SP_], BF16)
        key_max, rev = sb("key_max", [P, BL], BF16), sb("place_value", [P, SP_])
        mask = sb("chosen", [P, NT, F], BF16)
        hf = [sb(f"h_float{i}", [P, TOK]) for i in range(2)]
        hT = [[sb(f"h{i}_{p}", [P, TOK], BF16) for p in ("hi", "lo")] for i in range(2)]
        inter = c.ps[:, 0:F].rearrange("p (n s) -> p n s", s=SP_)
        with nc.Block() as block:

            @block.sync
            def _(sp):
                for d in range(2):
                    w.load(sp, d, a["l1_w1"][:, d, :])
                sp.wait_ge(zeroed, 2)
                sp.dma_start(c1[:, :, 0:RANK], a["l1_c1"]).then_inc(small, 16)
                sp.dma_start(c2[0:RANK, :], a["l1_c2"]).then_inc(small, 16)
                sp.dma_start(rev[:], a["place_value"]).then_inc(small, 16)
                for d in range(2, DC):
                    w.load(sp, d, a["l1_w1"][:, d, :])
                w.load(sp, DC, a["l1_w2"][:, 0:M // 2, :])
                after.first_load(sp)
                sp.wait_ge(w.lo_done, 3)
                w.load(sp, DC + 1, a["l1_w2"][:, M // 2:M, :])

            @block.gpsimd
            def _(pool):
                pool.memset(c1[:], 0.0).then_inc(zeroed, 1)
                pool.memset(c2[:], 0.0).then_inc(zeroed, 1)
                ln.gpsimd(pool)
                for i in (0, 2, DC, DC + 1):
                    w.low(pool, i)
                after.first_lo(pool)
                for m in range(M):
                    pool.wait_ge(h_hi, m + 1)
                    pool.tensor_tensor(hT[m % 2][1][:], hf[m % 2][:], hT[m % 2][0][:], ALU.subtract).then_inc(h_lo, 1)

            @block.scalar
            def _(act):
                w.scalar_hi(act, 0)
                ln.scalar_hi(act)
                for d in range(DC):
                    ln.wait_lo(act, d + 1)
                    act.activation(c.xn[:, d, :], c.bank(d), ACT.Copy).then_inc(xf_done, 1)
                w.scalar_hi(act, 1)
                act.wait_ge(u_done, 1)
                act.activation(u[:], c.bank(4), ACT.Copy).then_inc(u_saved, 1)
                for i in range(2, DC + 1):
                    w.scalar_hi(act, i)
                for m in range(M):
                    act.wait_ge(h_done, m + 1)
                    act.activation(h_all[:, m, :], c.bank(6 + m % 2), ACT.Relu).then_inc(h_saved, 1)
                    if m == 7:
                        w.scalar_hi(act, DC + 1)
                    if m == 9:
                        after.first_hi(act)
                for m in range(M):
                    act.wait_ge(h_masked, m + 1)
                    if m >= 2:
                        act.wait_ge(out_used, m - 1)
                    act.activation(hT[m % 2][0][:], hf[m % 2][:], ACT.Copy).then_inc(h_hi, 1)

            @block.vector
            def _(dve):
                link = Chain(dve, chain_sem)
                ln.vector_norm(dve)
                ln.vector_lo(dve)
                for i in (1, 3):
                    w.low(dve, i, lo_by_vector)
                dve.wait_ge(small, 48)
                for t in range(NT):
                    dve.wait_ge(inter_done, t + 1)
                    link(dve.reduce_max(mx[:], inter, AX.X))
                    dve.tensor_tensor(eq[:], inter, mx[:].unsqueeze(2).to_broadcast([P, BL, SP_]),
                                      ALU.is_equal).then_inc(eq_done, 1)
                    dve.wait_ge(eq_done, t + 1)
                    link(dve.tensor_tensor(key[:], eq[:], rev[:].unsqueeze(1).to_broadcast([P, BL, SP_]), ALU.mult))
                    link(dve.reduce_max(key_max[:], key[:], AX.X))
                    dve.tensor_tensor(mask[:, t, :].rearrange("p (n s) -> p n s", s=SP_), key[:],
                                      key_max[:].unsqueeze(2).to_broadcast([P, BL, SP_]), ALU.is_equal)\
                       .then_inc(mask_done, 1)
                for m in range(M):
                    dve.wait_ge(h_saved, m + 1)
                    dve.wait_ge(mT_done, m + 1)
                    if m >= 2:
                        dve.wait_ge(h_lo, m - 1)
                    dve.tensor_tensor(hf[m % 2][:], h_all[:, m, :], c.bank(m % 2), ALU.mult).then_inc(h_masked, 1)
                for t in range(NT):
                    dve.wait_ge(out_done, t + 1)
                    dve.scalar_tensor_tensor(c.x[:, t, :], c.bank(4 + t), c.gates[:, 3:4], c.x[:, t, :],
                                             ALU.mult, ALU.add).then_inc(x_done, 1)

            @block.tensor
            def _(pe):
                ln.tensor_turn(pe)
                pe.wait_ge(small, 48)
                for d in range(DC):
                    pe.wait_ge(xf_done, d + 1)
                    last = pe.matmul(c.bank(4), c1[:, d, :], c.xn[:, d, :], start=d == 0, stop=d == DC - 1)
                last.then_inc(u_done, 1)
                pe.wait_ge(u_saved, 1)
                for t in range(NT):
                    if t:
                        pe.wait_ge(eq_done, t)
                    for n in range(0, F, BANK):
                        last = pe.matmul(c.ps[:, n:min(n + BANK, F)], u[:, t * P:(t + 1) * P],
                                         c2[:, n:min(n + BANK, F)], start=True, stop=True)
                    last.then_inc(inter_done, 1)
                    pe.wait_ge(w.lo_done, 2)
                    pe.wait_ge(lo_by_vector, 2)
                    for m in range(max(4 * t - 2, 0), 4 * t + 2):
                        if m >= 2:
                            pe.wait_ge(h_saved, m - 1)
                        for d in range(DC):
                            last = three(pe, c.bank(6 + m % 2), [v[:, m * P:(m + 1) * P] for v in w1[d]],
                                         [v[:, d, :] for v in c.xT], d == 0, d == DC - 1)
                        last.then_inc(h_done, 1)

                def turn_choices(m):
                    if m >= 2:
                        pe.wait_ge(h_masked, m - 1)
                    for t in range(NT):
                        if m == 0:
                            pe.wait_ge(mask_done, t + 1)
                        last = pe.matmul(c.bank(m % 2, P, at=t * P), mask[:, t, m * P:(m + 1) * P], c.ident16[:],
                                         start=True, stop=True)
                    last.then_inc(mT_done, 1)

                pe.wait_ge(eq_done, NT)
                turn_choices(0)
                turn_choices(1)
                pe.wait_ge(h_saved, M)
                pe.wait_ge(w.lo_done, 3)
                for m in range(M):
                    if m + 2 < M:
                        turn_choices(m + 2)
                    pe.wait_ge(h_lo, m + 1)
                    if m == M // 2:
                        pe.wait_ge(w.lo_done, 4)
                    for t in range(NT):
                        last = three(pe, c.bank(4 + t), [v[:, t * P:(t + 1) * P] for v in hT[m % 2]],
                                     [v[:, m % (M // 2), :] for v in w2[m // (M // 2)]], m == 0, m == M - 1)
                        if m == M - 1:
                            last.then_inc(out_done, 1)
                    if m < M - 1:
                        last.then_inc(out_used, 1)


def gated_lora(nc, core, a, after):
    c, E, R = core, 4, 8
    G = E * R + E
    ln = LayerNorm(c)
    S = lambda n: c.sem(f"l2f_{n}")
    small, zeroed, ga_done, chain_sem, sub_done, exp_done, gp_done, gp_turned, gp_hi, gp_lo, out_done, x_done = (
        S(n) for n in ("small_loaded", "zeroed", "proj_done", "chain", "sub_done", "exp_done", "mix_done",
                       "mix_turned", "mix_hi", "mix_lo", "out_done", "x_done"))
    with ExitStack() as st:
        w = Pieces(c, "l2f", st)
        lo_by_vector = S("w_lo_by_vector")
        _, ar = w.add("a_wr", [P, DC, G])
        _, wt = w.add("w", [P, DC, D])
        bm_raw, bm = w.add("bm", [P, D])
        sb = lambda name, shape, dt=F32: c.sb(f"l2f_{name}", shape, dt, st)
        bias = sb("bias", [P, D])
        top, sums = sb("top", [P, NT]), sb("sums", [P, NT])
        e = sb("gate", [P, NT, E])
        gp = sb("mix", [P, NT, P])
        gpT = [sb(f"mix_T_{p}", [P, TOK], BF16) for p in ("hi", "lo")]
        tmp = sb("out", [P, NT, D])
        ga = c.bank(4, NT * G).rearrange("p (t g) -> p t g", t=NT)
        with nc.Block() as block:

            @block.sync
            def _(sp):
                w.load(sp, 0, a["l2_awr"])
                w.load(sp, 1, a["l2_w"])
                sp.wait_ge(zeroed, 2)
                sp.dma_start(bm_raw[0:E * R, :], a["l2_bm"]).then_inc(w.items[2][3], 16)
                sp.dma_start(bias[:], a["l2_b"]).then_inc(small, 16)
                after.first_load(sp)

            @block.gpsimd
            def _(pool):
                pool.memset(gp[:], 0.0).then_inc(zeroed, 1)
                pool.memset(bm_raw[:], 0.0).then_inc(zeroed, 1)
                ln.gpsimd(pool)
                for i in (0, 2):
                    w.low(pool, i)
                after.first_lo(pool)

            @block.scalar
            def _(act):
                w.scalar_hi(act, 0)
                ln.scalar_hi(act)
                for i in (1, 2):
                    w.scalar_hi(act, i)
                act.wait_ge(sub_done, 1)
                act.activation(e[:], e[:], ACT.Exp).then_inc(exp_done, 1)
                act.wait_ge(gp_turned, 1)
                act.activation(gpT[0][:], c.bank(5), ACT.Copy).then_inc(gp_hi, 1)
                after.first_hi(act)

            @block.vector
            def _(dve):
                link = Chain(dve, chain_sem)
                each = lambda v, n: v[:].unsqueeze(2).to_broadcast([P, NT, n])
                ln.vector_norm(dve)
                ln.vector_lo(dve)
                w.low(dve, 1, lo_by_vector)
                dve.wait_ge(ga_done, 1)
                link(dve.reduce_max(top[:], ga[:, :, E * R:], AX.X))
                dve.tensor_tensor(e[:], ga[:, :, E * R:], each(top, E), ALU.subtract).then_inc(sub_done, 1)
                dve.wait_ge(exp_done, 1)
                link(dve.reduce_sum(sums[:], e[:], AX.X))
                link(dve.reciprocal(sums[:], sums[:]))
                link(dve.tensor_scalar(sums[:], sums[:], 2.0, None, ALU.mult))
                link(dve.tensor_tensor(e[:], e[:], each(sums, E), ALU.mult))
                dve.wait_ge(zeroed, 1)
                for t in range(NT):
                    dve.tensor_tensor(gp[:, t, 0:E * R].rearrange("p (e r) -> p e r", e=E),
                                      ga[:, t, 0:E * R].rearrange("p (e r) -> p e r", e=E),
                                      e[:, t, :].unsqueeze(2).to_broadcast([P, E, R]), ALU.mult).then_inc(gp_done, 1)
                dve.wait_ge(gp_hi, 1)
                dve.tensor_tensor(gpT[1][:], c.bank(5), gpT[0][:], ALU.subtract).then_inc(gp_lo, 1)
                dve.wait_ge(small, 16)
                for t in range(NT):
                    dve.wait_ge(out_done, t + 1)
                    link(dve.tensor_tensor(tmp[:, t, :], c.bank(t), bias[:], ALU.add))
                    dve.scalar_tensor_tensor(c.x[:, t, :], tmp[:, t, :], c.gates[:, 5:6], c.x[:, t, :],
                                             ALU.mult, ALU.add).then_inc(x_done, 1)

            @block.tensor
            def _(pe):
                ln.tensor_turn(pe)
                ln.wait_parts(pe)
                w.wait(pe, 0)
                for t in range(NT):
                    for d in range(DC):
                        last = three(pe, c.bank(4, G, at=t * G), [v[:, d, t * P:(t + 1) * P] for v in c.xT],
                                     [v[:, d, :] for v in ar], d == 0, d == DC - 1)
                last.then_inc(ga_done, 1)
                pe.wait_ge(lo_by_vector, 1)
                for t in range(NT):
                    for d in range(DC):
                        three(pe, c.bank(t), [v[:, d, t * P:(t + 1) * P] for v in c.xT],
                              [v[:, d, :] for v in wt], d == 0, False)
                pe.wait_ge(gp_done, NT)
                for t in range(NT):
                    last = pe.transpose(c.bank(5, P, at=t * P), gp[:, t, :], c.ident[:])
                last.then_inc(gp_turned, 1)
                pe.wait_ge(w.lo_done, 2)
                pe.wait_ge(gp_lo, 1)
                for t in range(NT):
                    last = three(pe, c.bank(t), [v[:, t * P:(t + 1) * P] for v in gpT], [v[:] for v in bm],
                                 False, True)
                    last.then_inc(out_done, 1)


def routed_experts(nc, core, a):
    c, E, M = core, 3, D // P
    VIS = int(SQ * 0.3)
    ln = LayerNorm(c)
    S = lambda n: c.sem(f"l3f_{n}")
    small, sel_done, abs_done, tot_done, gate_made, chain_sem, sub_done, exp_done, pick_done, pick_rep, coef_done = (
        S(n) for n in ("small_loaded", "row0_done", "abs_done", "totals_done", "gate_made", "chain", "sub_done",
                       "exp_done", "picks_done", "picks_repeated", "coef_done"))
    pre_done, act_done, a_hi, a_lo, out_done, x_done = (
        S(n) for n in ("pre_done", "act_done", "act_hi", "act_lo", "out_done", "x_done"))
    with ExitStack() as st:
        w = Pieces(c, "l3f", st)
        by_vector = S("w1_0_by_vector")
        w1, w2 = [], []
        for e in range(E):
            w1.append(w.add(f"w1_{e}", [P, DC, D])[1])
            w2.append(w.add(f"w2_{e}", [P, M, D])[1])
        _, gw = w.add("gate_w", [P, DC, E])
        order = [0, 2, 1, 4, 3, 5]
        sb = lambda name, shape, dt=F32: c.sb(f"l3f_{name}", shape, dt, st)
        b1, b2 = sb("b1", [P, E, M]), sb("b2", [P, E, D])
        gw_last, gb, place = sb("gate_w_last", [P, E]), sb("gate_b", [P, E]), sb("place_value", [P, E])
        row0, junk = sb("row0", [P, P]), sb("junk", [P, SQ])
        absum, tot = sb("abs_sums", [P, DC, 4]), sb("abs_totals", [P, 4])
        ratio, gb2 = sb("ratio", [P, NB]), sb("gate_const", [P, NB, E])
        s, key, s2 = sb("scores", [P, NT, E]), sb("key", [P, NT, E]), sb("scores2", [P, NT, E])
        picks = sb("picks", [P, 2, NT, E])
        pick0 = sb("picks_of_token0", [P, 2, NB, E])
        v1, v2, t4, u4 = (sb(n, [P, NT]) for n in ("value1", "value2", "t4", "u4"))
        coef, coef2 = sb("coef", [P, NT, E]), sb("coef2", [P, NT, E])
        af = [sb(f"act_float{i}", [P, TOK]) for i in range(2)]
        aT = [[sb(f"act{i}_{p}", [P, M, TOK], BF16) for p in ("hi", "lo")] for i in range(2)]
        tmp = [sb(f"out{i}", [P, D]) for i in range(2)]
        with nc.Block() as block:

            @block.sync
            def _(sp):
                w.load(sp, 6, a["l3_gate_w"])
                for dst, name in ((b1, "l3_b1"), (b2, "l3_b2"), (gw_last, "l3_gate_w_last"), (gb, "l3_gate_b"),
                                  (place, "place3")):
                    sp.dma_start(dst[:], a[name]).then_inc(small, 16)
                for i in order:
                    w.load(sp, i, a["l3_w1" if i % 2 == 0 else "l3_w2"][:, i // 2])

            @block.gpsimd
            def _(pool):
                pool.memset(row0[:], 0.0).then_inc(sel_done, 1)
                pool.wait_ge(sel_done, 1)
                pool.memset(row0[0:1, :], 1.0).then_inc(sel_done, 1)
                ln.gpsimd(pool)
                for n, i in enumerate([6] + order[1:]):
                    raw, hi, lo, _ = w.items[i]
                    pool.wait_ge(w.hi_done, n + 1)
                    pool.tensor_tensor(lo[:], raw[:], hi[:], ALU.subtract).then_inc(w.lo_done, 1)
                for n in range(E * M):
                    e, m = n // M, n % M
                    pool.wait_ge(a_hi, n + 1)
                    pool.tensor_tensor(aT[e % 2][1][:, m, :], af[n % 2][:], aT[e % 2][0][:, m, :], ALU.subtract)\
                        .then_inc(a_lo, 1)

            @block.scalar
            def _(act):
                w.scalar_hi(act, 6)
                ln.scalar_hi(act)
                for d in range(DC):
                    ln.wait_lo(act, d + 1)
                    for b in range(NB):
                        for k, (lo, hi) in enumerate(((0, VIS), (VIS, SQ))):
                            n = 2 * b + k
                            act.wait_ge(abs_done, 4 * d + n) if 4 * d + n else None
                            act.activation(junk[:, 0:hi - lo], c.bank(d, hi - lo, at=b * SQ + lo), ACT.Abs,
                                           accum_out=absum[:, d, n:n + 1]).then_inc(abs_done, 1)
                for i in order[1:2]:
                    w.scalar_hi(act, i)
                act.wait_ge(sub_done, 1)
                act.activation(s[:], s[:], ACT.Exp).then_inc(exp_done, 1)
                for i in order[2:]:
                    w.scalar_hi(act, i)
                act.wait_ge(small, 80)
                for n in range(E * M):
                    e, m = n // M, n % M
                    act.wait_ge(pre_done, n + 1)
                    if n >= 2:
                        act.wait_ge(a_lo, n - 1)
                    act.activation(af[n % 2][:], c.bank(m), (ACT.Tanh, ACT.Gelu, ACT.Silu)[e],
                                   bias=b1[:, e, m:m + 1]).then_inc(act_done, 1)
                    act.wait_ge(act_done, n + 1)
                    if e == 2:
                        act.wait_ge(out_done, NT)
                    act.activation(aT[e % 2][0][:, m, :], af[n % 2][:], ACT.Copy).then_inc(a_hi, 1)

            @block.vector
            def _(dve):
                link = Chain(dve, chain_sem)
                each = lambda v: v[:].unsqueeze(2).to_broadcast([P, NT, E])
                places = place[:].unsqueeze(1).to_broadcast([P, NT, E])

                def pick(src, value, i):
                    link(dve.reduce_max(value[:], src[:], AX.X))
                    link(dve.tensor_tensor(key[:], src[:], each(value), ALU.is_equal))
                    link(dve.tensor_tensor(key[:], key[:], places, ALU.mult))
                    link(dve.reduce_max(t4[:], key[:], AX.X))
                    link(dve.tensor_tensor(picks[:, i], key[:], each(t4), ALU.is_equal))

                ln.vector_norm(dve)
                ln.vector_lo(dve)
                raw, hi, lo, loaded = w.items[0]
                dve.wait_ge(loaded, 16)
                dve.tensor_copy(hi[:], raw[:]).then_inc(by_vector, 1)
                dve.wait_ge(by_vector, 1)
                dve.tensor_tensor(lo[:], raw[:], hi[:], ALU.subtract).then_inc(by_vector, 1)
                dve.wait_ge(tot_done, 1)
                dve.wait_ge(small, 80)
                link(dve.reduce_sum(tot[:], c.bank(4, DC * 4).rearrange("p (d n) -> p n d", d=DC), AX.X))
                link(dve.tensor_scalar(ratio[:], tot[:, 0:4:2], 1.0 / (VIS * D), 1e-8, ALU.mult, ALU.add))
                link(dve.reciprocal(ratio[:], ratio[:]))
                link(dve.tensor_scalar(tot[:, 1:4:2], tot[:, 1:4:2], 1.0 / ((SQ - VIS) * D), None, ALU.mult))
                link(dve.tensor_tensor(ratio[:], ratio[:], tot[:, 1:4:2], ALU.mult))
                for b in range(NB):
                    link(dve.scalar_tensor_tensor(gb2[:, b, :], gw_last[:], ratio[:, b:b + 1], gb[:],
                                                  ALU.mult, ALU.add))
                dve.wait_ge(gate_made, 1)
                for b in range(NB):
                    link(dve.tensor_tensor(s[:, 2 * b:2 * b + 2, :],
                                           c.bank(5, 2 * E, at=2 * E * b).rearrange("p (t e) -> p t e", e=E),
                                           gb2[:, b, :].unsqueeze(1).to_broadcast([P, 2, E]), ALU.add))
                link(dve.reduce_max(t4[:], s[:], AX.X))
                dve.tensor_tensor(s[:], s[:], each(t4), ALU.subtract).then_inc(sub_done, 1)
                dve.wait_ge(exp_done, 1)
                link(dve.reduce_sum(t4[:], s[:], AX.X))
                link(dve.reciprocal(t4[:], t4[:]))
                link(dve.tensor_tensor(s[:], s[:], each(t4), ALU.mult))
                pick(s, v1, 0)
                link(dve.scalar_tensor_tensor(s2[:], picks[:, 0], -4.0, s[:], ALU.mult, ALU.add))
                pick(s2, v2, 1)
                link(dve.tensor_tensor(u4[:], v1[:], v2[:], ALU.add))
                link(dve.tensor_scalar(u4[:], u4[:], 1e-8, None, ALU.add))
                link(dve.reciprocal(u4[:], u4[:]))
                link(dve.tensor_scalar(u4[:], u4[:], c.gates[:, 7:8], None, ALU.mult))
                link(dve.tensor_tensor(v1[:], v1[:], u4[:], ALU.mult))
                dve.tensor_tensor(v2[:], v2[:], u4[:], ALU.mult).then_inc(pick_done, 1)
                dve.wait_ge(pick_rep, 1)
                link(dve.tensor_copy(pick0[:], c.bank(6, 2 * NT * E).rearrange(
                    "p (i b t e) -> p i b t e", i=2, b=NB, t=2)[:, :, :, 0, :]))
                for b in range(NB):
                    rows = slice(2 * b, 2 * b + 2)
                    of0 = lambda i: pick0[:, i, b, :].unsqueeze(1).to_broadcast([P, 2, E])
                    w_of = lambda v: v[:, rows].unsqueeze(2).to_broadcast([P, 2, E])
                    link(dve.tensor_tensor(coef[:, rows, :], of0(0), w_of(v1), ALU.mult))
                    link(dve.tensor_tensor(coef2[:, rows, :], of0(1), w_of(v2), ALU.mult))
                dve.tensor_tensor(coef[:], coef[:], coef2[:], ALU.add).then_inc(coef_done, 1)
                dve.wait_ge(coef_done, 1)
                for n in range(E * NT):
                    e, t = n // NT, n % NT
                    dve.wait_ge(out_done, n + 1)
                    link(dve.tensor_tensor(tmp[n % 2][:], c.bank(4 + t), b2[:, e, :], ALU.add))
                    dve.scalar_tensor_tensor(c.x[:, t, :], tmp[n % 2][:], coef[:, t, e:e + 1], c.x[:, t, :],
                                             ALU.mult, ALU.add).then_inc(x_done, 1)

            @block.tensor
            def _(pe):
                def ready(n):
                    pe.wait_ge(w.hi_done, n)
                    pe.wait_ge(w.lo_done, n)

                def up(e):
                    if e:
                        ready(1 + order.index(2 * e))
                    else:
                        pe.wait_ge(by_vector, 2)
                    for m in range(M):
                        n = e * M + m
                        if n >= M:
                            pe.wait_ge(act_done, n - M + 1)
                        for d in range(DC):
                            last = three(pe, c.bank(m), [v[:, d, m * P:(m + 1) * P] for v in w1[e]],
                                         [v[:, d, :] for v in c.xT], d == 0, d == DC - 1)
                        last.then_inc(pre_done, 1)

                def down(e):
                    ready(1 + order.index(2 * e + 1))
                    pe.wait_ge(a_lo, (e + 1) * M)
                    for t in range(NT):
                        if e:
                            pe.wait_ge(x_done, (e - 1) * NT + t + 1)
                        for m in range(M):
                            last = three(pe, c.bank(4 + t), [v[:, m, t * P:(t + 1) * P] for v in aT[e % 2]],
                                         [v[:, m, :] for v in w2[e]], m == 0, m == M - 1)
                        last.then_inc(out_done, 1)

                ln.tensor_turn(pe)
                ln.wait_parts(pe)
                ready(1)
                for t in range(NT):
                    for d in range(DC):
                        last = three(pe, c.bank(5, E, at=t * E), [v[:, d, t * P:(t + 1) * P] for v in c.xT],
                                     [v[:, d, :] for v in gw], d == 0, d == DC - 1)
                last.then_inc(gate_made, 1)
                pe.wait_ge(abs_done, 4 * DC)
                pe.matmul(c.bank(4, DC * 4), c.ones[:], absum[:].rearrange("p d n -> p (d n)"),
                          start=True, stop=True).then_inc(tot_done, 1)
                up(0)
                pe.wait_ge(pick_done, 1)
                pe.wait_ge(sel_done, 2)
                pe.matmul(c.bank(6, 2 * NT * E), row0[:], picks[:].rearrange("p i t e -> p (i t e)"),
                          start=True, stop=True).then_inc(pick_rep, 1)
                up(1)
                pe.wait_ge(coef_done, 1)
                down(0)
                up(2)
                down(1)
                down(2)


def store(nc, core, out):
    stored = core.sem("stored")
    with nc.Block() as block:

        @block.sync
        def _(sp):
            sp.dma_start(out, core.x[:]).then_inc(stored, 16)
            sp.wait_ge(stored, 16)


def build(nc, a, out):
    with ExitStack() as ctx:
        core = Core(nc, ctx)
        setup_and_quant_product(nc, core, a)
        l1x = Attention(core, "l1x", 2, 8, 128, True, a["l1_qkv"], norm=True)
        lora_experts(nc, core, a, l1x)
        l1x.run(a["l1_wo"], {"qw": a["l1_qw"], "kw": a["l1_kw"]})
        l2x = Attention(core, "l2x", 4, 8, 128, False, a["l2_qkv"], rope=True, mask=True)
        sparse_rows(nc, core, a, l2x)
        l2x.run(a["l2_wo"], {n: a[n] for n in ("k_cos", "k_sin", "q_cos", "q_sin", "mask")})
        l3x = Attention(core, "l3x", 6, 4, 96, True, a["l3_qkv"])
        gated_lora(nc, core, a, l3x)
        l3x.run(a["l3_wo"], {})
        routed_experts(nc, core, a)
        store(nc, core, out)


def columns(w):
    k, n = w.shape
    return w.reshape(k // P, P, n).transpose(1, 0, 2)


def heads_together(wk, wv, wq, hd):
    rounds = wk.shape[1] // hd
    parts = [w.reshape(DC, P, rounds, -1) for w in (wk, wv, wq)]
    return np.concatenate(parts, 3).transpose(1, 2, 0, 3).reshape(P, -1)


def heads_out(wo, hd):
    return wo.reshape(-1, hd, D).transpose(1, 0, 2).reshape(hd, -1)


def rotation_tables(hd):
    inv = (1.0 / 10000.0 ** (np.arange(0, hd, 2, dtype=np.float32) / np.float32(hd))).astype(np.float32)
    ang = (np.arange(SC, dtype=np.float32)[None, :] * inv[:, None]).astype(np.float32)
    cos, sin = np.cos(ang).astype(np.float32), np.sin(ang).astype(np.float32)
    k_cos, k_sin = np.concatenate([cos, cos]), np.concatenate([sin, -sin])
    scale = np.float32(hd) ** np.float32(-0.5)
    q_cos, q_sin = (np.tile(w[:, :SQ] * scale, (1, 2)).astype(np.float32) for w in (k_cos, k_sin))
    return {"k_cos": k_cos, "k_sin": k_sin, "q_cos": q_cos, "q_sin": q_sin}


def lay_out(v):
    rows = lambda w: np.broadcast_to(w, (P, *w.shape))
    d = {
        "x": v["x"].reshape(NT, P, D).transpose(1, 0, 2),
        "context": v["ctx_4096"].reshape(-1, P, D).transpose(1, 0, 2),
        "context_T": columns(v["ctx_4096"].reshape(-1, D).T),
        "gates": rows(np.stack([v["g_xattn"], v["g_ffn"]], 1).reshape(8)),
        "quant": rows(np.concatenate([v["L0_xattn_x1_scale"], v["L0_xattn_x1_zp"],
                                      v["L0_xattn_x2_scale"], v["L0_xattn_x2_zp"]])),
    }
    d["l1_qkv"] = heads_together(v["L1_xattn_Wk"], v["L1_xattn_Wv"], v["L1_xattn_Wq"], 128)
    d["l1_wo"] = heads_out(v["L1_xattn_Wo"], 128)
    d["l1_qw"], d["l1_kw"] = v["L1_xattn_q_norm_w"][:, None], v["L1_xattn_k_norm_w"][:, None]
    d["l2_qkv"] = heads_together(v["L2_xattn_wk"], v["L2_xattn_wv"], v["L2_xattn_wq"], 128)
    d["l2_wo"] = heads_out(v["L2_xattn_wo"], 128)
    d.update(rotation_tables(128))
    d["mask"] = v["mask_BxSxS2_ff0"].reshape(NT, P, SC).transpose(1, 0, 2)
    d["l3_qkv"] = heads_together(v["L3_xattn_Wk"].T, v["L3_xattn_Wv"].T, v["L3_xattn_Wq"].T, 96)
    d["l3_wo"] = heads_out(v["L3_xattn_Wo"].T, 96)
    d["l0_down"] = columns(v["L0_ffn_lora_down"].transpose(1, 0, 2).reshape(D, -1))
    d["l0_up"] = columns(v["L0_ffn_lora_up"].reshape(-1, D))
    d["l0_worg"], d["l0_wq"] = columns(v["L0_ffn_W_org"].T), columns(v["L0_ffn_Wq"].T)
    d["l0_keys"] = v["L0_ffn_lora_keys"].T
    d["l1_c1"], d["l1_c2"] = columns(v["L1_ffn_c1_w"].T), v["L1_ffn_c2_w"].T
    d["l1_w1"], d["l1_w2"] = columns(v["L1_ffn_w1"].T), columns(v["L1_ffn_w2t"])
    d["place_value"] = rows(np.arange(32, 0, -1, dtype=np.float32))
    d["l2_awr"] = np.concatenate([columns(v["L2_ffn_A"].reshape(-1, D).T), columns(v["L2_ffn_Wr"].T)], 2)
    d["l2_w"], d["l2_b"] = columns(v["L2_ffn_W"].T), rows(v["L2_ffn_b"])
    d["l2_bm"] = v["L2_ffn_Bm"].transpose(0, 2, 1).reshape(-1, D)
    per_expert = lambda w: w.reshape(3, DC, P, D).transpose(2, 0, 1, 3)
    d["l3_w1"], d["l3_w2"] = per_expert(v["L3_ffn_w1"]), per_expert(v["L3_ffn_w2"])
    d["l3_b1"] = v["L3_ffn_b1"].reshape(3, DC, P).transpose(2, 0, 1)
    d["l3_b2"] = rows(v["L3_ffn_b2"])
    d["l3_gate_w"], d["l3_gate_w_last"] = columns(v["L3_ffn_gate_w"][:D]), rows(v["L3_ffn_gate_w"][D])
    d["l3_gate_b"] = rows(v["L3_ffn_gate_b"])
    d["place3"] = rows(np.arange(3, 0, -1, dtype=np.float32))
    return {k: np.ascontiguousarray(w) for k, w in d.items()}


def kernel(**inputs):
    import concourse.bacc as bacc
    from concourse.bass_utils import run_bass_kernel_spmd as run

    nc = bacc.Bacc("TRN2", target_bir_lowering=False, num_devices=1)
    arrays = lay_out({k: np.asarray(w) for k, w in inputs.items()})
    a = {k: nc.dram_tensor(k + "_dram", w.shape, mybir.dt.from_np(w.dtype), kind="ExternalInput").ap()
         for k, w in arrays.items()}
    out = nc.dram_tensor("out_dram", (P, NT, D), F32, kind="ExternalOutput").ap()
    build(nc, a, out)
    r = run(nc, [{k + "_dram": w for k, w in arrays.items()}], core_ids=[0])
    return r.results[0]["out_dram"].transpose(1, 0, 2).reshape(NB, SQ, D)
```
